# Optimizing a Trainium2 kernel written in Bass

```python
import numpy as np
import jax
import jax.numpy as jnp

def _softmax(x, axis=-1):
    return jax.nn.softmax(x, axis=axis)

def _gelu(x):
    return jax.nn.gelu(x, approximate=True)

def _silu(x):
    return jax.nn.silu(x)

def _sigmoid(x):
    return jax.nn.sigmoid(x)

def _layernorm(x, axis=-1, eps=1e-05):
    m = jnp.mean(x, axis=axis, keepdims=True)
    v = jnp.var(x, axis=axis, keepdims=True)
    return (x - m) / jnp.sqrt(v + eps)

def _scatter_add(tgt, idx, src, axis=0):
    return tgt.at[idx].add(src)

def _segment_sum(src, seg, n):
    return jax.ops.segment_sum(src, seg, n)
kernel_name = 'mk_decoder_preln_d1_seqx_r4_2dd530'

def setup_inputs(seed: int=0):
    np.random.seed(seed)
    _w = jnp.asarray

    def _rec_inputs():
        import jax
        import jax.numpy as jnp
        _rk = jax.random.key(seed)
        x = 7.22e-05 + 1 * jax.random.normal(jax.random.fold_in(_rk, 1), (16, 128, 512), jnp.float32)
        _lenS = 128 - jax.random.randint(jax.random.fold_in(_rk, 7), (16,), 0, max(1, 128 // 4) + 1, jnp.int32)
        _lenS2 = 128 - jax.random.randint(jax.random.fold_in(_rk, 8), (16,), 0, max(1, 128 // 4) + 1, jnp.int32)
        _ctx_1024P = jax.random.normal(jax.random.fold_in(_rk, 11), (16, 16, 256), jnp.float32)
        _ctx_1024c = jax.random.dirichlet(jax.random.fold_in(_rk, 511), 0.3 * jnp.ones((16,), jnp.float32), (16, 128))
        _ctx_1024t = jnp.einsum('bsk,bkd->bsd', _ctx_1024c, _ctx_1024P)
        _ctx_1024t = _ctx_1024t * jax.lax.rsqrt(jnp.mean(jnp.square(_ctx_1024t)) + 1e-12) * 0.953939
        ctx_1024 = -0.000673644 + 1.00013 * (_ctx_1024t + 0.3 * jax.random.normal(jax.random.fold_in(_rk, 611), (16, 128, 256), jnp.float32))
        return (x, ctx_1024)
    x, ctx_1024 = _rec_inputs()

    def _L0_attn_setup():
        import jax, jax.numpy as jnp
        import numpy as np
        H = 16
        NORM = 16.0
        SCALE = 128.0 ** (-0.5)
        EPS = 1e-05

        def _gla_core(x, Wq, Wk, Wkg1, Wkg2, bkg2, Wv, Wg, bg, Wo):
            B, L, D = x.shape
            q = x @ Wq.T
            k = x @ Wk.T * SCALE
            kg = x @ Wkg1.T @ Wkg2.T + bkg2
            v = x @ Wv.T
            gproj = x @ Wg.T + bg
            dk = q.shape[-1] // H
            dv = D // H
            heads = lambda t, dh: t.reshape(B, L, H, dh).transpose(0, 2, 1, 3)
            qh = heads(q, dk)
            kh = heads(k, dk)
            vh = heads(v, dv)
            gk = jax.nn.log_sigmoid(heads(kg, dk)) / NORM
            tfirst = lambda t: t.transpose(2, 0, 1, 3)

            def step(S, inp):
                qt, kt, vt, gt = inp
                S = S * jnp.exp(gt)[..., None] + kt[..., None] * vt[..., None, :]
                ot = jnp.einsum('bhk,bhkv->bhv', qt, S)
                return (S, ot)
            S0 = jnp.zeros((B, H, dk, dv), x.dtype)
            _, os = jax.lax.scan(step, S0, (tfirst(qh), tfirst(kh), tfirst(vh), tfirst(gk)))
            o = os.transpose(1, 2, 0, 3)
            mu = o.mean(-1, keepdims=True)
            var = ((o - mu) ** 2).mean(-1, keepdims=True)
            o = (o - mu) * jax.lax.rsqrt(var + EPS)
            o = o.transpose(0, 2, 1, 3).reshape(B, L, D)
            return jax.nn.silu(gproj) * o @ Wo.T
        key = jax.random.key(seed)
        ks = jax.random.split(key, 10)
        B, L, D = (2, 512, 512)
        g = lambda k, shape, s: jax.random.normal(k, shape, jnp.float32) * s
        return {'x': g(ks[0], (B, L, D), 1.0), 'Wq': g(ks[1], (256, D), 0.02), 'Wk': g(ks[2], (256, D), 0.02), 'Wkg1': g(ks[3], (16, D), 0.02), 'Wkg2': g(ks[4], (256, 16), 0.05), 'bkg2': jnp.zeros((256,), jnp.float32), 'Wv': g(ks[5], (D, D), 0.02), 'Wg': g(ks[6], (D, D), 0.02), 'bg': jnp.zeros((D,), jnp.float32), 'Wo': g(ks[7], (D, D), 0.02)}
    _L0_attn_all = _L0_attn_setup()
    _L0_attn_in = {k: v for k, v in _L0_attn_all.items() if k in ('Wq', 'Wk', 'Wkg1', 'Wkg2', 'bkg2', 'Wv', 'Wg', 'bg', 'Wo')}
    del _L0_attn_all

    def _L0_xattn_setup():
        import jax, jax.numpy as jnp
        import numpy as np
        B, S1, S2, DCA = (2, 512, 256, 16)
        QDIM, KDIM, H = (512, 256, 16)
        HD = QDIM // H
        SCALE = HD ** (-0.5)
        EPS = 1e-06
        DCA_WEIGHT = 1.0

        def _ln(t, w, b):
            m = jnp.mean(t, axis=-1, keepdims=True)
            v = jnp.var(t, axis=-1, keepdims=True)
            return (t - m) * jax.lax.rsqrt(v + EPS) * w + b

        def _attn(q, k, v):
            s = jnp.einsum('bhqd,bhkd->bhqk', q, k) * SCALE
            p = jax.nn.softmax(s, axis=-1)
            return jnp.einsum('bhqk,bhkd->bhqd', p, v)
        key = jax.random.key(seed)
        ks = jax.random.split(key, 8)
        w = lambda k, shape: jax.random.normal(k, shape, jnp.float32) * 0.02
        return {'x': jax.random.normal(ks[0], (B, S1, QDIM), jnp.float32), 'y': jax.random.normal(ks[1], (B, S2 + DCA, KDIM), jnp.float32), 'Wq': w(ks[2], (QDIM, QDIM)), 'bq': jnp.zeros((QDIM,), jnp.float32), 'Wk': w(ks[3], (KDIM, QDIM)), 'bk': jnp.zeros((QDIM,), jnp.float32), 'Wv': w(ks[4], (KDIM, QDIM)), 'bv': jnp.zeros((QDIM,), jnp.float32), 'Wkv_dca': w(ks[5], (KDIM, 2 * QDIM)), 'bkv_dca': jnp.zeros((2 * QDIM,), jnp.float32), 'qn_w': jnp.ones((HD,), jnp.float32), 'qn_b': jnp.zeros((HD,), jnp.float32), 'kn_w': jnp.ones((HD,), jnp.float32), 'kn_b': jnp.zeros((HD,), jnp.float32), 'kn_dca_w': jnp.ones((HD,), jnp.float32), 'kn_dca_b': jnp.zeros((HD,), jnp.float32), 'Wo': w(ks[6], (QDIM, QDIM)), 'bo': jnp.zeros((QDIM,), jnp.float32)}
    _L0_xattn_all = _L0_xattn_setup()
    _L0_xattn_in = {k: v for k, v in _L0_xattn_all.items() if k in ('Wq', 'bq', 'Wk', 'bk', 'Wv', 'bv', 'Wkv_dca', 'bkv_dca', 'qn_w', 'qn_b', 'kn_w', 'kn_b', 'kn_dca_w', 'kn_dca_b', 'Wo', 'bo')}
    del _L0_xattn_all

    def _L0_ffn_setup():
        import jax, jax.numpy as jnp
        import numpy as np
        B, T, D, E, H = (4, 512, 512, 4, 2048)
        TOPK = 2
        CAPACITY_FACTOR = 1
        key = jax.random.key(seed)
        k0, k1, k2, k3 = jax.random.split(key, 4)
        x = jax.random.normal(k0, (B, T, D), dtype=jnp.float32)
        Wg = jax.random.normal(k1, (D, E), dtype=jnp.float32) * 0.02
        bg = jnp.zeros((E,), dtype=jnp.float32)
        W1 = jax.random.normal(k2, (E, D, H), dtype=jnp.float32) * (1.0 / np.sqrt(D))
        W2 = jax.random.normal(k3, (E, H, D), dtype=jnp.float32) * (1.0 / np.sqrt(H))
        return {'x': x, 'Wg': Wg, 'bg': bg, 'W1': W1, 'W2': W2}
    _L0_ffn_all = _L0_ffn_setup()
    _L0_ffn_in = {k: v for k, v in _L0_ffn_all.items() if k in ('Wg', 'bg', 'W1', 'W2')}
    del _L0_ffn_all
    return {'x': x, 'ctx_1024': ctx_1024, 'L0_attn_Wq': _L0_attn_in['Wq'], 'L0_attn_Wk': _L0_attn_in['Wk'], 'L0_attn_Wkg1': _L0_attn_in['Wkg1'], 'L0_attn_Wkg2': _L0_attn_in['Wkg2'], 'L0_attn_bkg2': _L0_attn_in['bkg2'], 'L0_attn_Wv': _L0_attn_in['Wv'], 'L0_attn_Wg': _L0_attn_in['Wg'], 'L0_attn_bg': _L0_attn_in['bg'], 'L0_attn_Wo': _L0_attn_in['Wo'], 'L0_xattn_Wq': _L0_xattn_in['Wq'], 'L0_xattn_bq': _L0_xattn_in['bq'], 'L0_xattn_Wk': _L0_xattn_in['Wk'], 'L0_xattn_bk': _L0_xattn_in['bk'], 'L0_xattn_Wv': _L0_xattn_in['Wv'], 'L0_xattn_bv': _L0_xattn_in['bv'], 'L0_xattn_Wkv_dca': _L0_xattn_in['Wkv_dca'], 'L0_xattn_bkv_dca': _L0_xattn_in['bkv_dca'], 'L0_xattn_qn_w': _L0_xattn_in['qn_w'], 'L0_xattn_qn_b': _L0_xattn_in['qn_b'], 'L0_xattn_kn_w': _L0_xattn_in['kn_w'], 'L0_xattn_kn_b': _L0_xattn_in['kn_b'], 'L0_xattn_kn_dca_w': _L0_xattn_in['kn_dca_w'], 'L0_xattn_kn_dca_b': _L0_xattn_in['kn_dca_b'], 'L0_xattn_Wo': _L0_xattn_in['Wo'], 'L0_xattn_bo': _L0_xattn_in['bo'], 'L0_ffn_Wg': _L0_ffn_in['Wg'], 'L0_ffn_bg': _L0_ffn_in['bg'], 'L0_ffn_W1': _L0_ffn_in['W1'], 'L0_ffn_W2': _L0_ffn_in['W2']}

def reference(x, ctx_1024, L0_attn_Wq, L0_attn_Wk, L0_attn_Wkg1, L0_attn_Wkg2, L0_attn_bkg2, L0_attn_Wv, L0_attn_Wg, L0_attn_bg, L0_attn_Wo, L0_xattn_Wq, L0_xattn_bq, L0_xattn_Wk, L0_xattn_bk, L0_xattn_Wv, L0_xattn_bv, L0_xattn_Wkv_dca, L0_xattn_bkv_dca, L0_xattn_qn_w, L0_xattn_qn_b, L0_xattn_kn_w, L0_xattn_kn_b, L0_xattn_kn_dca_w, L0_xattn_kn_dca_b, L0_xattn_Wo, L0_xattn_bo, L0_ffn_Wg, L0_ffn_bg, L0_ffn_W1, L0_ffn_W2):
    import jax
    import jax.numpy as jnp

    def _L0_attn_ref(x, Wq, Wk, Wkg1, Wkg2, bkg2, Wv, Wg, bg, Wo):
        import jax, jax.numpy as jnp
        import numpy as np
        H = 16
        NORM = 16.0
        SCALE = 128.0 ** (-0.5)
        EPS = 1e-05

        def _gla_core(x, Wq, Wk, Wkg1, Wkg2, bkg2, Wv, Wg, bg, Wo):
            B, L, D = x.shape
            q = x @ Wq.T
            k = x @ Wk.T * SCALE
            kg = x @ Wkg1.T @ Wkg2.T + bkg2
            v = x @ Wv.T
            gproj = x @ Wg.T + bg
            dk = q.shape[-1] // H
            dv = D // H
            heads = lambda t, dh: t.reshape(B, L, H, dh).transpose(0, 2, 1, 3)
            qh = heads(q, dk)
            kh = heads(k, dk)
            vh = heads(v, dv)
            gk = jax.nn.log_sigmoid(heads(kg, dk)) / NORM
            tfirst = lambda t: t.transpose(2, 0, 1, 3)

            def step(S, inp):
                qt, kt, vt, gt = inp
                S = S * jnp.exp(gt)[..., None] + kt[..., None] * vt[..., None, :]
                ot = jnp.einsum('bhk,bhkv->bhv', qt, S)
                return (S, ot)
            S0 = jnp.zeros((B, H, dk, dv), x.dtype)
            _, os = jax.lax.scan(step, S0, (tfirst(qh), tfirst(kh), tfirst(vh), tfirst(gk)))
            o = os.transpose(1, 2, 0, 3)
            mu = o.mean(-1, keepdims=True)
            var = ((o - mu) ** 2).mean(-1, keepdims=True)
            o = (o - mu) * jax.lax.rsqrt(var + EPS)
            o = o.transpose(0, 2, 1, 3).reshape(B, L, D)
            return jax.nn.silu(gproj) * o @ Wo.T
        return _gla_core(x, Wq, Wk, Wkg1, Wkg2, bkg2, Wv, Wg, bg, Wo)

    def _L0_xattn_ref(x, y, Wq, bq, Wk, bk, Wv, bv, Wkv_dca, bkv_dca, qn_w, qn_b, kn_w, kn_b, kn_dca_w, kn_dca_b, Wo, bo):
        import jax, jax.numpy as jnp
        import numpy as np
        B, S1, S2, DCA = (2, 512, 256, 16)
        QDIM, KDIM, H = (512, 256, 16)
        HD = QDIM // H
        SCALE = HD ** (-0.5)
        EPS = 1e-06
        DCA_WEIGHT = 1.0

        def _ln(t, w, b):
            m = jnp.mean(t, axis=-1, keepdims=True)
            v = jnp.var(t, axis=-1, keepdims=True)
            return (t - m) * jax.lax.rsqrt(v + EPS) * w + b

        def _attn(q, k, v):
            s = jnp.einsum('bhqd,bhkd->bhqk', q, k) * SCALE
            p = jax.nn.softmax(s, axis=-1)
            return jnp.einsum('bhqk,bhkd->bhqd', p, v)
        b, s1, _ = x.shape
        y_dca = y[:, -DCA:, :]
        y_main = y[:, :-DCA, :]
        kv_dca = (y_dca @ Wkv_dca + bkv_dca).reshape(b, DCA, 2, H, HD)
        k_dca = _ln(kv_dca[:, :, 0], kn_dca_w, kn_dca_b)
        v_dca = kv_dca[:, :, 1]
        s2 = y_main.shape[1]
        q = _ln((x @ Wq + bq).reshape(b, s1, H, HD), qn_w, qn_b)
        kv = jnp.concatenate([y_main @ Wk + bk, y_main @ Wv + bv], axis=-1)
        kv = kv.reshape(b, s2, H, 2 * HD)
        k = _ln(kv[..., :HD], kn_w, kn_b)
        v = kv[..., HD:]
        qT = q.transpose(0, 2, 1, 3)
        ctx = _attn(qT, k.transpose(0, 2, 1, 3), v.transpose(0, 2, 1, 3))
        ctx = ctx.transpose(0, 2, 1, 3).reshape(b, s1, QDIM)
        ctx_dca = _attn(qT, k_dca.transpose(0, 2, 1, 3), v_dca.transpose(0, 2, 1, 3))
        ctx_dca = ctx_dca.transpose(0, 2, 1, 3).reshape(b, s1, QDIM)
        ctx = ctx + DCA_WEIGHT * ctx_dca
        return ctx @ Wo + bo

    def _L0_ffn_ref(x, Wg, bg, W1, W2):
        import jax, jax.numpy as jnp
        import numpy as np
        B, T, D, E, H = (4, 512, 512, 4, 2048)
        TOPK = 2
        CAPACITY_FACTOR = 1
        Bq, Tq, Dq = x.shape
        N = Bq * Tq
        capacity = int(N * CAPACITY_FACTOR / E)
        flat_x = x.reshape(N, Dq)
        logits = flat_x @ Wg + bg
        top_vals, top_idx = jax.lax.top_k(logits, TOPK)
        sparse = jnp.full_like(logits, -jnp.inf)
        sparse = sparse.at[jnp.arange(N)[:, None], top_idx].set(top_vals)
        probs = jax.nn.softmax(sparse, axis=-1)
        out = jnp.zeros_like(flat_x)
        for i in range(E):
            assigned = (top_idx == i).any(axis=-1)
            score = jnp.where(assigned, probs[:, i], -jnp.inf)
            sel_p, sel_idx = jax.lax.top_k(score, capacity)
            p = jnp.where(jnp.isfinite(sel_p), sel_p, 0.0)[:, None]
            tok = flat_x[sel_idx]
            h = jax.nn.gelu(tok @ W1[i], approximate=False)
            y = h @ W2[i] * p
            out = out.at[sel_idx].add(y)
        return out.reshape(Bq, Tq, Dq)
    x = x + _L0_attn_ref(_layernorm(x, axis=-1), L0_attn_Wq, L0_attn_Wk, L0_attn_Wkg1, L0_attn_Wkg2, L0_attn_bkg2, L0_attn_Wv, L0_attn_Wg, L0_attn_bg, L0_attn_Wo)
    x = x + _L0_xattn_ref(_layernorm(x, axis=-1), ctx_1024, L0_xattn_Wq, L0_xattn_bq, L0_xattn_Wk, L0_xattn_bk, L0_xattn_Wv, L0_xattn_bv, L0_xattn_Wkv_dca, L0_xattn_bkv_dca, L0_xattn_qn_w, L0_xattn_qn_b, L0_xattn_kn_w, L0_xattn_kn_b, L0_xattn_kn_dca_w, L0_xattn_kn_dca_b, L0_xattn_Wo, L0_xattn_bo)
    x = x + _L0_ffn_ref(_layernorm(x, axis=-1), L0_ffn_Wg, L0_ffn_bg, L0_ffn_W1, L0_ffn_W2)
    return x

_drawn_inputs = setup_inputs


def setup_inputs(seed=0):
    import zlib

    import numpy as np

    out = dict(_drawn_inputs(seed))
    spreads = {'L0_attn_bkg2': (0.0, 0.387),
     'L0_attn_bg': (0.0, 0.1),
     'L0_xattn_bq': (0.0, 0.1),
     'L0_xattn_bk': (0.0, 0.1),
     'L0_xattn_bv': (0.0, 0.1),
     'L0_xattn_bkv_dca': (0.0, 0.1),
     'L0_xattn_qn_w': (1.0, 0.548),
     'L0_xattn_qn_b': (0.0, 0.39),
     'L0_xattn_kn_w': (1.0, 0.6),
     'L0_xattn_kn_b': (0.0, 0.8),
     'L0_xattn_kn_dca_w': (1.0, 0.2),
     'L0_xattn_kn_dca_b': (0.0, 0.8),
     'L0_xattn_bo': (0.0, 0.1),
     'L0_ffn_bg': (0.0, 0.1)}
    factors = {'L0_attn_Wkg1': 6.697, 'L0_attn_Wkg2': 4.566}
    for name, (base, spread) in spreads.items():
        noise = np.random.default_rng([zlib.crc32(name.encode()), seed]).standard_normal(out[name].shape)
        drawn = base * np.exp(spread * noise) if base else spread * noise
        out[name] = jnp.asarray(drawn.astype(out[name].dtype))
    for name, factor in factors.items():
        out[name] = (out[name] * factor).astype(out[name].dtype)
    return out
```

```python
from contextlib import ExitStack

import concourse.bass as bass
from concourse import mybir

ALU = mybir.AluOpType
ACT = mybir.ActivationFunctionType
AX = mybir.AxisListType
F32 = mybir.dt.float32
F16 = mybir.dt.float16
I32 = mybir.dt.int32


def decoder_layer(nc, stage_out, x, ctx_t, dca_t, w_attn, w_ctx, w_kg2, b_kg2, b_g, b_q, b_kv, b_dca,
                  w_qn, b_qn, w_kn, b_kn, w_kd, b_kd, b_o, w_gate, b_gate, w1, w2, out):
    B, L, D = x.shape
    P = 128
    KC = D // P
    HEADS = 16
    DV = D // HEADS
    DK = 16
    QK = HEADS * DK
    KEYS = ctx_t.shape[2]
    NDCA = L - KEYS
    CC = ctx_t.shape[1] // P
    BLK = 32
    NBLK = L // BLK
    KTW = [BLK * (i + 1) for i in range(NBLK)]
    KTO = [sum(KTW[:i]) for i in range(NBLK)]
    KTN = sum(KTW)
    E = w_gate.shape[1]
    HID = w1.shape[2]
    N = B * L
    CAP = N // E
    XS, WS = 16.0, 256.0
    UN = 1.0 / (XS * WS)
    PADS = 4
    EPS_ROW = 1e-5
    EPS_HEAD = (1e-5, 1e-6, 1e-6)
    GLA_SCALE = 128.0 ** -0.5
    NORM = 16.0
    XSCALE = DV ** -0.5
    RADIX = 5
    SHIFTS = list(range(30 - RADIX, -1, -RADIX))
    FAR = float(2 * N)

    C_QK, C_KG, C_V, C_G, C_O, C_XQ, C_XO = 0, 512, 528, 1040, 1552, 2064, 2576
    W_COLS = C_XO + D

    dca_dram = nc.dram_tensor("dca_scratch", (B * NDCA, 2 * D), F32).ap()
    xg_dram = nc.dram_tensor("xg_scratch", (E * CAP, D), F32).ap()
    y_dram = nc.dram_tensor("y_scratch", (E * CAP, D), F32).ap()
    out_rows = out.rearrange("b l d -> (b l) d")

    with ExitStack() as ctx:
        def sem(name):
            return ctx.enter_context(nc.semaphore(name))

        def sems(name, n):
            return [sem(f"{name}{i}") for i in range(n)]

        def keep(name, shape, dt=F32):
            return ctx.enter_context(nc.sbuf_tensor(name, shape, dt))

        x_all = keep("x_all", [P, B * D])
        ident = keep("ident", [P, P])
        logit_all = keep("logit_all", [P, B * E])
        mr_all = keep("mr_all", [P, 2 * B])
        neg_half = keep("neg_half", [P, HEADS])

        at = ExitStack()

        def sb(name, shape, dt=F32):
            return at.enter_context(nc.sbuf_tensor(name, shape, dt))

        wh = sb("wh", [P, KC, W_COLS], F16)
        wl = sb("wl", [P, KC, W_COLS], F16)
        wch = sb("wch", [P, CC, 2 * D], F16)
        wcl = sb("wcl", [P, CC, 2 * D], F16)
        wkg2_sb = sb("wkg2_sb", [DK, QK])
        bkg2_sb = sb("bkg2_sb", [P, QK // P])
        bg_sb = sb("bg_sb", [P, D])
        bq_sb = sb("bq_sb", [P, D])
        bo_sb = sb("bo_sb", [P, D])
        bkv_sb = sb("bkv_sb", [P, 2 * D])
        qw_sb = sb("qw_sb", [P, DV])
        qb_sb = sb("qb_sb", [P, DV])
        kw_sb = sb("kw_sb", [P, DV])
        kb_sb = sb("kb_sb", [P, DV])
        wgate_sb = sb("wgate_sb", [P, KC, E])
        bgate_sb = sb("bgate_sb", [P, E])
        row_id = sb("row_id", [P, 1], I32)
        half_id = sb("half_id", [P, 1], I32)
        pair_half = sb("pair_half", [P, 2])
        causal = sb("causal", [P, NBLK, 2 * BLK])
        carry = sb("carry", [P, QK])

        stats = [sb(f"stats{n}", [P, 6]) for n in range(3)]
        aggr = [sb(f"aggr{n}", [P, 2]) for n in range(3)]
        vare = [sb(f"vare{n}", [P, 1]) for n in range(3)]
        rstd = [sb(f"rstd{n}", [P, 1]) for n in range(3)]
        hsum = [sb(f"hsum{n}", [P, HEADS]) for n in range(3)]
        hvar = [sb(f"hvar{n}", [P, HEADS]) for n in range(3)]
        hve = [sb(f"hve{n}", [P, HEADS]) for n in range(3)]
        hrs = [sb(f"hrs{n}", [P, HEADS]) for n in range(3)]

        wait_pad = sb("wait_pad", [P, PADS])
        eps_row = sb("eps_row", [P, 3])
        eps_head = sb("eps_head", [P, 3, HEADS])
        one_col = sb("one_col", [P, 1])

        xn = sb("xn", [P, D])
        xth = sb("xth", [P, KC, L], F16)
        xtl = sb("xtl", [P, KC, L], F16)
        kg1 = sb("kg1", [DK, L])
        z = sb("z", [P, QK])
        zabs = sb("zabs", [P, QK])
        zexp = sb("zexp", [P, QK])
        zln = sb("zln", [P, QK])
        lsg = sb("lsg", [P, QK])
        G = sb("G", [P, QK])
        dq = sb("dq", [P, QK])
        eq = sb("eq", [P, QK])
        dk = sb("dk", [P, 2, KTN])
        qeo = [sb(f"qeo{i}", [P, 2 * NBLK, 2, BLK]) for i in range(2)]
        kt = [sb(f"kt{i}", [P, 2, KTN]) for i in range(2)]
        v = [sb(f"v{i}", [P, D]) for i in range(2)]
        gf = sb("gf", [P, D])
        ge = sb("ge", [P, D])
        gate = [sb(f"gate{i}", [P, D]) for i in range(2)]

        scm = sb("scm", [P, 4 * 2 * NBLK * 2 * BLK])
        od = sb("od", [P, D])
        osq = sb("osq", [P, D])
        oth = sb("oth", [P, KC, L], F16)
        otl = sb("otl", [P, KC, L], F16)

        ctx32 = [sb(f"ctx32_{i}", [P, CC, KEYS]) for i in range(2)]
        cth = sb("cth", [P, CC, KEYS], F16)
        ctl = sb("ctl", [P, CC, KEYS], F16)
        kraw = sb("kraw", [P, D])
        vx = [sb(f"vx{i}", [P, D]) for i in range(2)]
        kd = sb("kd", [P, D])
        ksq = sb("ksq", [P, D])
        kT = sb("kT", [P, KC, L])
        xn2 = sb("xn2", [P, D])
        x2h = sb("x2h", [P, KC, L], F16)
        x2l = sb("x2l", [P, KC, L], F16)
        qraw = sb("qraw", [P, D])
        qd = sb("qd", [P, D])
        qsq = sb("qsq", [P, D])
        qT = sb("qT", [P, KC, L])
        mx = sb("mx", [P, 2, HEADS])
        sm = sb("sm", [P, 2, HEADS])
        rc = sb("rc", [P, 2, HEADS])
        pr = [sb(f"pr{i}", [P, HEADS * L]) for i in range(2)]
        pT = sb("pT", [P, KC, L])
        ch = sb("ch", [P, KC, L], F16)
        cl = sb("cl", [P, KC, L], F16)
        xn3 = sb("xn3", [P, D])
        x3T = sb("x3T", [P, KC, L])

        stage = [pr[i][:, :].rearrange("p (k n) -> p k n", k=KC) for i in range(2)]
        dca_w = scm[:, :].bitcast(F16).rearrange("p (h k n) -> p h k n", h=2, k=CC)
        dca32 = od[:, :].rearrange("p (k n) -> p k n", k=CC)
        dca_h = oth[:, :, :].rearrange("p k n -> p (k n)").rearrange("p (k n) -> p k n", k=CC)
        dca_l = otl[:, :, :].rearrange("p k n -> p (k n)").rearrange("p (k n) -> p k n", k=CC)
        dca_o = [xn2, qraw, kd, qd]
        at.close()

        ff = ExitStack()

        def fb(name, shape, dt=F32):
            return ff.enter_context(nc.sbuf_tensor(name, shape, dt))

        tri4 = fb("tri4", [P, E, E])
        cmp_gt = fb("cmp_gt", [P, B, E, E])
        cmp_eq = fb("cmp_eq", [P, B, E, E])
        rank = fb("rank", [P, B, E])
        oh = [fb(f"oh{k}", [P, B, E]) for k in range(2)]
        ohl = fb("ohl", [P, B, E])
        l1 = fb("l1", [P, B])
        l2 = fb("l2", [P, B])
        ldiff = fb("ldiff", [P, B])
        ed = fb("ed", [P, B])
        den = fb("den", [P, B])
        p12 = fb("p12", [P, 2, B])
        score = fb("score", [P, B, E])
        sc2 = fb("sc2", [P, B, E])
        big = [fb(f"big{i}", [P, N]) for i in range(4)]
        digit = fb("digit", [P, 1], I32)
        pid = fb("pid", [P, 1], I32)
        eid = fb("eid", [P, 1], I32)
        cands = fb("cands", [P, len(SHIFTS)], I32)
        cand = fb("cand", [P, 1], I32)
        thr = fb("thr", [P, 1], I32)
        count = fb("count", [P, 1])
        enough = fb("enough", [P, 1])
        same_e = fb("same_e", [P, E, P // E])
        ones = fb("ones", [P, 1])
        ties = fb("ties", [P, 1])
        slot0 = fb("slot0", [P, 1])
        posT = fb("posT", [P, B, E])
        sel_k = fb("sel_k", [P, B, E])
        idx = fb("idx", [P, 2, B])
        idx_put = fb("idx_put", [P, 2, B], I32)
        idx_get = fb("idx_get", [P, 2, B], I32)
        wk = fb("wk", [P, 2, B])
        xn_all = fb("xn_all", [P, B * D])
        zero = fb("zero", [P, D])
        NST = 2
        wst = [fb(f"wst{i}", [P, 2048]) for i in range(NST)]
        HALF = HID // 2
        w1h = [fb(f"w1h{i}", [P, KC, HALF], F16) for i in range(2)]
        w1l = [fb(f"w1l{i}", [P, KC, HALF], F16) for i in range(2)]
        FH = HALF // P
        w2h = [fb(f"w2h{i}", [P, FH, D], F16) for i in range(2)]
        w2l = [fb(f"w2l{i}", [P, FH, D], F16) for i in range(2)]
        xg32 = big[0][:, :].rearrange("p (t n) -> p t n", t=4)
        y_sb = big[1][:, :].rearrange("p (t n) -> p t n", t=4)
        xgh = big[2][:, :].bitcast(F16)[:, 0:2048].rearrange("p (k n) -> p k n", k=KC)
        xgl = big[2][:, :].bitcast(F16)[:, 2048:4096].rearrange("p (k n) -> p k n", k=KC)
        hg = [big[3][:, i * D:(i + 1) * D] for i in range(2)]
        h16 = big[3][:, 2 * D:4 * D].bitcast(F16)
        hh = [h16[:, i * D:(i + 1) * D] for i in range(2)]
        hl = [h16[:, (2 + i) * D:(3 + i) * D] for i in range(2)]
        NG = 8
        yg = [xn_all[:, i * D:(i + 1) * D] for i in range(NG)]
        ff.close()

        psum = [ctx.enter_context(nc.psum_tensor(f"ps{i}", [P, 1024], F32)) for i in range(4)]
        a0, a1 = psum[0][:, 0:512], psum[0][:, 512:1024]
        b0, b1 = psum[1][:, 0:512], psum[1][:, 512:1024]
        c0, c1 = psum[2][:, 0:512], psum[2][:, 512:1024]
        d0, d1 = psum[3][:, 0:512], psum[3][:, 512:1024]

        x_in = sems("x_in", 4)
        consts_in = sem("consts_in")
        stage_in = sems("stage_in", 2)
        stage_hi = sem("stage_hi")
        stage_lo = sem("stage_lo")
        kg1w_in = sem("kg1w_in")
        dca_in, dca_split, dca_ps, dca_out, dca_stored = map(sem, (
            "dca_in", "dca_split", "dca_ps", "dca_out", "dca_stored"))
        scm_zero = sem("scm_zero")
        pool_const, dve_const = sem("pool_const"), sem("dve_const")
        ctx_in = sems("ctx_in", 2)
        kdca_in, vdca_in = sem("kdca_in"), sems("vdca_in", 2)

        stat, dev = sems("stat", 3), sems("dev", 3)
        cent, hq, hv, hdev = (sems(n, 3) for n in ("cent", "hq", "hv", "hdev"))

        xn_r, xt_ps, xth_r, xtl_r = map(sem, ("xn_r", "xt_ps", "xth_r", "xtl_r"))
        a1_ps = sem("a1_ps")
        kg1_r, z_r, lsig, sums, dk_r, decay, qk_r = map(sem, ("kg1_r", "z_r", "lsig", "sums", "dk_r", "decay", "qk_r"))
        v_r, gate_v, ge_r, gate_p = map(sem, ("v_r", "gate_v", "ge_r", "gate_p"))
        sc_ps, scm_r = sem("sc_ps"), sem("scm_r")
        o_ps, on_r, og_r, ot_ps, oth_r, otl_r, wo_ps, x1_r = map(sem, (
            "o_ps", "on_r", "og_r", "ot_ps", "oth_r", "otl_r", "wo_ps", "x1_r"))
        cth_r, ctl_r, kv_ps, kv_ev, kv_bias = map(sem, ("cth_r", "ctl_r", "kv_ps", "kv_ev", "kv_bias"))
        kn_r, k_aff, kT_ps, kT_r = map(sem, ("kn_r", "k_aff", "kT_ps", "kT_r"))
        xn2_r, x2_ps, x2h_r, x2l_r, q_ps, q_r = map(sem, ("xn2_r", "x2_ps", "x2h_r", "x2l_r", "q_ps", "q_r"))
        qn_r, q_aff, qT_ps, qT_r = map(sem, ("qn_r", "q_aff", "qT_ps", "qT_r"))
        xs_ps, shift, exp_r, norm, pr_r = map(sem, ("xs_ps", "shift", "exp_r", "norm", "pr_r"))
        pT_ps, pT_r, pv_ps = map(sem, ("pT_ps", "pT_r", "pv_ps"))
        xbo_r, ch_r, cl_r, xo_ps, x2_r = map(sem, ("xbo_r", "ch_r", "cl_r", "xo_ps", "x2_r"))
        xn3_r, x3_ps, x3T_r, lg_ps, lg_r, mean3_r = map(sem, (
            "xn3_r", "x3_ps", "x3T_r", "lg_ps", "lg_r", "mean3_r"))

        route, route_const, ed_r, rep_r, scT_ps, scT_r, cnt_r, dig_ps, pos_r, posT_ps, posT_r = map(sem, (
            "route", "route_const", "ed_r", "rep_r", "scT_ps", "scT_r", "cnt_r", "dig_ps", "pos_r",
            "posT_ps", "posT_r"))
        idx_r, xnall_r, zero_r, zero_st, put_done = map(sem, ("idx_r", "xnall_r", "zero_r", "zero_st", "put_done"))
        w_in = sems("w_in", NST)
        w_hi, w_lo, xg_in = sem("w_hi"), sem("w_lo"), sem("xg_in")
        half_used = sems("half_used", 2)
        xgT_ps, xgh_r, xgl_r = sem("xgT_ps"), sem("xgh_r"), sem("xgl_r")
        h_ps, hg_r, hh_r, hl_r, h_used = map(sem, ("h_ps", "hg_r", "hh_r", "hl_r", "h_used"))
        yps_r, y_ev, y_st = sem("yps_r"), sem("y_ev"), sem("y_st")
        yg_in, comb, comb_r, out_st = sems("yg_in", NG), sem("comb"), sem("comb_r"), sem("out_st")

        def heads(ap):
            return ap.rearrange("p (h c) -> p h c", c=DV)

        def per_head(ap):
            return ap.unsqueeze(2).to_broadcast([P, HEADS, DV])

        def over_heads(ap):
            return ap.unsqueeze(1).to_broadcast([P, HEADS, DV])

        LAGS = 4

        def pipeline(eng, body):
            def fixed(t):
                return [(t - k, (t - k) % 2, (t - k) // 2) if 0 <= t - k < B else None for k in range(LAGS)]
            for t in range(LAGS):
                body(fixed(t))
            with eng.Fori(LAGS // 2, B // 2) as j:
                for u in range(2):
                    body([(2 * j + (u - k), (u - k) % 2, j + (u - k) // 2) for k in range(LAGS)])
            for t in range(B, B + LAGS - 1):
                body(fixed(t))

        def seq(b):
            return bass.ds(b * D, D)

        block = ctx.enter_context(nc.Block())

        pieces = []
        for c in (C_QK, C_V, C_G, C_O, C_XQ, C_XO):
            pieces.append((w_attn[:, c:c + D].rearrange("(k p) n -> p k n", p=P), wh[:, :, c:c + D], wl[:, :, c:c + D], KC))
        pieces.append((w_ctx[:, 0:2 * D].rearrange("(k p) n -> p k n", p=P), wch[:, :, :], wcl[:, :, :], CC))
        pieces.insert(1, (w_ctx[:, 2 * D:4 * D].rearrange("(k p) n -> p k n", p=P), dca_w[:, 0], dca_w[:, 1], CC))
        KG_STAGE = xn3[:, 0:KC * DK].rearrange("p (k n) -> p k n", k=KC)

        def staged(n):
            return pr[n % 2][:, :].rearrange("p (k n) -> p k n", k=pieces[n][3])

        consts = [(wkg2_sb[:, :], w_kg2), (bkg2_sb[:, :], b_kg2), (bg_sb[:, :], b_g.partition_broadcast(P)),
                  (bq_sb[:, :], b_q.partition_broadcast(P)), (bo_sb[:, :], b_o.partition_broadcast(P)),
                  (bkv_sb[0:KEYS, :], b_kv.partition_broadcast(KEYS)), (bkv_sb[KEYS:P, :], b_dca.partition_broadcast(NDCA)),
                  (qw_sb[:, :], w_qn.partition_broadcast(P)), (qb_sb[:, :], b_qn.partition_broadcast(P)),
                  (kw_sb[0:KEYS, :], w_kn.partition_broadcast(KEYS)), (kw_sb[KEYS:P, :], w_kd.partition_broadcast(NDCA)),
                  (kb_sb[0:KEYS, :], b_kn.partition_broadcast(KEYS)), (kb_sb[KEYS:P, :], b_kd.partition_broadcast(NDCA)),
                  (wgate_sb[:, :, :], w_gate.rearrange("(k p) e -> p k e", p=P)), (bgate_sb[:, :], b_gate.partition_broadcast(P))]
        XPARTS = [(0, 1), (1, 2), (2, 4), (4, B)]

        def x_loaded(b):
            return [n for n, (lo, hi) in enumerate(XPARTS) if lo == b]

        def w_piece(e, n):
            hf, k = n // 4, n % 4
            if k < 2:
                src = w1[bass.ds(e, 1), k * 256:(k + 1) * 256, hf * HALF:(hf + 1) * HALF].rearrange("o (k p) n -> p (o k) n", p=P)
                return src, w1h[hf][:, 2 * k:2 * k + 2, :], w1l[hf][:, 2 * k:2 * k + 2, :], 2
            k -= 2
            lo = hf * HALF + k * 512
            src = w2[bass.ds(e, 1), lo:lo + 512, :].rearrange("o (f p) d -> p (o f) d", p=P)
            return src, w2h[hf][:, 4 * k:4 * k + 4, :], w2l[hf][:, 4 * k:4 * k + 4, :], 4
        W_PIECES = 8

        @block.sync
        def _(sp):
            sp.dma_start(x_all[:, 0:D], x[0]).then_inc(x_in[0], 16)
            for n in range(2):
                sp.dma_start(staged(n), pieces[n][0]).then_inc(stage_in[n], 16)
            sp.dma_start(KG_STAGE, w_attn[:, C_KG:C_KG + DK].rearrange("(k p) n -> p k n", p=P)).then_inc(kg1w_in, 16)
            sp.dma_start(dca32, dca_t.rearrange("(k p) n -> p k n", p=P)).then_inc(dca_in, 16)
            for dst, src in consts:
                sp.dma_start(dst, src).then_inc(consts_in, 16)
            for n in range(2, len(pieces)):
                if n - 2 < 3:
                    lo, hi = XPARTS[n - 1]
                    sp.dma_start(x_all[:, lo * D:hi * D].rearrange("p (b d) -> p b d", d=D),
                                 x[lo:hi].rearrange("b p d -> p b d")).then_inc(x_in[n - 1], 16)
                sp.wait_ge(stage_lo, n)
                sp.dma_start(staged(n), pieces[n][0]).then_inc(stage_in[n % 2], 16)
            for t in range(4):
                sp.wait_ge(dca_out, t + 1)
                sp.dma_start(dca_dram[(t // 2) * P:(t // 2 + 1) * P, (t % 2) * D:(t % 2 + 1) * D],
                             dca_o[t][:, :]).then_inc(dca_stored, 16)
            sp.wait_ge(dca_stored, 64)

            def body(s):
                a, _, q, _ = s
                nxt = s[1]
                if nxt:
                    b, par, half = nxt
                    sp.wait_ge(ctl_r, b - 1) if not isinstance(b, int) or b >= 2 else None
                    sp.dma_start(ctx32[par][:, :, :], ctx_t[bass.ds(b, 1)].rearrange("o (k p) n -> p (o k) n", p=P))\
                      .then_inc(ctx_in[par], 16)
                if q:
                    b, par, half = q
                    if not isinstance(b, int) or b >= 1:
                        sp.wait_ge(cent[1], 2 * b)
                    sp.dma_start(kraw[KEYS:P, :], dca_dram[bass.ds(b * NDCA, NDCA), 0:D]).then_inc(kdca_in, 16)
                    if not isinstance(b, int) or b >= 2:
                        sp.wait_ge(pv_ps, 4 * (b - 1))
                    sp.dma_start(vx[par][KEYS:P, :], dca_dram[bass.ds(b * NDCA, NDCA), D:2 * D]).then_inc(vdca_in[par], 16)

            pipeline(sp, body)

            sp.wait_ge(lg_r, B)
            def load_piece(e, n):
                src, _, _, k = w_piece(e, n)
                sp.dma_start(wst[n % NST][:, :].rearrange("p (k n) -> p k n", k=k), src).then_inc(w_in[n % NST], 16)
            def load_expert(e, first):
                for n in range(W_PIECES):
                    if first and n < NST:
                        load_piece(e, n)
                    else:
                        sp.wait_ge(w_lo, e * W_PIECES + (n + 1 - NST))
                        load_piece(e, n)
            sp.wait_ge(zero_r, 1)
            for t in range(N // P):
                sp.dma_start(xg_dram[t * P:(t + 1) * P, :], zero[:, :]).then_inc(zero_st, 16)
            load_expert(0, True)
            sp.wait_ge(put_done, 16 * 2 * B)
            sp.dma_start(xg32, xg_dram[0:CAP, :].rearrange("(t p) d -> p t d", p=P)).then_inc(xg_in, 16)

            def after(e):
                load_expert(e + 1, False)
                sp.wait_ge(xgT_ps, 4 * (e + 1))
                sp.dma_start(xg32, xg_dram[bass.ds((e + 1) * CAP, CAP), :].rearrange("(t p) d -> p t d", p=P)).then_inc(xg_in, 16)
                sp.wait_ge(y_ev, 4 * (e + 1))
                sp.dma_start(y_dram[bass.ds(e * CAP, CAP), :].rearrange("(t p) d -> p t d", p=P), y_sb).then_inc(y_st, 16)
            with sp.Fori(0, E - 1) as e:
                after(e)
            sp.wait_ge(y_ev, 4 * E)
            sp.dma_start(y_dram[(E - 1) * CAP:, :].rearrange("(t p) d -> p t d", p=P), y_sb).then_inc(y_st, 16)
            for b in range(B):
                sp.wait_ge(comb_r, b + 1)
                sp.dma_start(out_rows[b * L:(b + 1) * L, :], x_all[:, b * D:(b + 1) * D]).then_inc(out_st, 16)
            sp.wait_ge(out_st, 16 * B)

        @block.gpsimd
        def _(pool):
            pool.memset(ident[:, :], 0.0).then_inc(pool_const, 1)
            pool.memset(causal[:, :, :], 1.0).then_inc(pool_const, 1)
            pool.memset(neg_half[:, :], -0.5).then_inc(pool_const, 1)
            for n in range(3):
                pool.memset(eps_row[:, n:n + 1], EPS_ROW)
                pool.memset(eps_head[:, n, :], DV * EPS_HEAD[n])
            pool.memset(one_col[:, :], 1.0)
            pool.iota(row_id[:, :], [[0, 1]], base=0, channel_multiplier=1).then_inc(pool_const, 1)
            pool.wait_ge(pool_const, 4)
            pool.affine_select(out=ident[:, :], in_=ident[:, :], compare_op=ALU.not_equal, fill=1.0, base=0,
                               pattern=[[-1, P]], channel_multiplier=1).then_inc(pool_const, 1)
            cz = causal[:, :, :].rearrange("p i (e t) -> p i e t", e=2)
            pool.affine_select(out=cz, in_=cz, compare_op=ALU.is_ge, fill=0.0, base=0,
                               pattern=[[BLK, NBLK], [0, 2], [1, BLK]], channel_multiplier=-1).then_inc(pool_const, 1)

            pool.wait_ge(consts_in, 16 * len(consts))

            def deviation(n, b):
                pool.wait_ge(stat[n], 2 * b + 2)
                pool.tensor_tensor(vare[n][:, :], aggr[n][:, 1:2], eps_row[:, n:n + 1], ALU.add).then_inc(dev[n], 1)
                pool.wait_ge(dev[n], 2 * b + 1)
                pool.tensor_tensor(rstd[n][:, :], vare[n][:, :], neg_half[:, 0:1], ALU.pow).then_inc(dev[n], 1)

            def head_deviation(n, b):
                pool.wait_ge(hv[n], b + 1)
                pool.tensor_tensor(hve[n][:, :], hvar[n][:, :], eps_head[:, n, :], ALU.add).then_inc(hdev[n], 1)
                pool.wait_ge(hdev[n], 2 * b + 1)
                pool.tensor_tensor(hrs[n][:, :], hve[n][:, :], neg_half[:, :], ALU.pow).then_inc(hdev[n], 1)

            def norm_affine(src, w, bias, ready, done, b):
                pool.wait_ge(ready, b + 1)
                pool.tensor_tensor(heads(src[:, :]), heads(src[:, :]), over_heads(w[:, :]), ALU.mult).then_inc(done, 1)
                pool.wait_ge(done, 2 * b + 1)
                pool.tensor_tensor(heads(src[:, :]), heads(src[:, :]), over_heads(bias[:, :]), ALU.add).then_inc(done, 1)

            def body(s):
                A1, A2, B1, B2 = s
                if A1:
                    deviation(0, A1[0])
                if B2:
                    b, par, half = B2
                    pool.wait_ge(xn2_r, b + 1)
                    pool.tensor_tensor(x_all[:, seq(b)], x_all[:, seq(b)], bo_sb[:, :], ALU.add).then_inc(xbo_r, 1)
                if B1:
                    b, par, half = B1
                    pool.wait_ge(kv_ev, 2 * b + 1)
                    pool.wait_ge(kdca_in, 16 * (b + 1))
                    pool.tensor_tensor(kraw[:, :], kraw[:, :], bkv_sb[:, 0:D], ALU.add).then_inc(kv_bias, 1)
                    pool.wait_ge(kv_ev, 2 * b + 2)
                    pool.wait_ge(vdca_in[par], 16 * (half + 1))
                    pool.tensor_tensor(vx[par][:, :], vx[par][:, :], bkv_sb[:, D:2 * D], ALU.add).then_inc(kv_bias, 1)
                    head_deviation(1, b)
                    deviation(1, b)
                    norm_affine(kd, kw_sb, kb_sb, kn_r, k_aff, b)
                if A1:
                    b, par, half = A1
                    pool.wait_ge(sums, 3 * b + 2)
                    G3 = G[:, :].rearrange("p (c t) -> p c t", c=2)
                    for i in range(NBLK):
                        m = BLK * i + BLK // 2 - 1
                        last = pool.tensor_tensor(dk[:, :, KTO[i]:KTO[i] + KTW[i]],
                                                  G3[:, :, m:m + 1].to_broadcast([P, 2, KTW[i]]),
                                                  G3[:, :, 0:KTW[i]], ALU.subtract)
                    last.then_inc(dk_r, 1)
                if A2:
                    b, par, half = A2
                    head_deviation(0, b)
                    pool.wait_ge(on_r, b + 1)
                    pool.tensor_tensor(od[:, :], od[:, :], gate[par][:, :], ALU.mult).then_inc(og_r, 1)
                if B1:
                    b, par, half = B1
                    head_deviation(2, b)
                    norm_affine(qd, qw_sb, qb_sb, qn_r, q_aff, b)
                if A1:
                    b, par, half = A1
                    pool.wait_ge(ge_r, b + 1)
                    pool.tensor_tensor(ge[:, :], ge[:, :], one_col[:, :].to_broadcast([P, D]), ALU.add).then_inc(gate_p, 1)
                    pool.wait_ge(gate_v, 2 * b + 2)
                    pool.tensor_tensor(gate[par][:, :], gf[:, :], ge[:, :], ALU.mult).then_inc(gate_p, 1)
                for rnd in range(2):
                    if B2 and rnd:
                        b, par, half = B2
                        deviation(2, b)
                        pool.tensor_copy(mr_all[:, bass.ds(2 * b, 1)], aggr[2][:, 0:1])
                        pool.wait_ge(dev[2], 2 * b + 2)
                        pool.tensor_copy(mr_all[:, bass.ds(2 * b + 1, 1)], rstd[2][:, :]).then_inc(mean3_r, 1)
                    if B1:
                        b, par, half = B1
                        pool.wait_ge(norm, 4 * b + (2 * rnd + 2))
                        p3 = pr[par][:, rnd * 1024:(rnd + 1) * 1024].rearrange("p (h k) -> p h k", k=L)
                        rr = rc[:, :, rnd * 8:(rnd + 1) * 8]
                        pool.tensor_tensor(p3[:, :, 0:KEYS], p3[:, :, 0:KEYS],
                                           rr[:, 0].unsqueeze(2).to_broadcast([P, 8, KEYS]), ALU.mult)
                        pool.tensor_tensor(p3[:, :, KEYS:L], p3[:, :, KEYS:L],
                                           rr[:, 1].unsqueeze(2).to_broadcast([P, 8, NDCA]), ALU.mult).then_inc(pr_r, 1)

            pipeline(pool, body)

            pool.wait_ge(lg_r, B)
            pool.wait_ge(mean3_r, B)
            pool.memset(zero[:, :], 0.0).then_inc(zero_r, 1)
            pool.memset(tri4[:, :, :], 1.0).then_inc(route_const, 1)
            pool.memset(same_e[:, :, :], 1.0).then_inc(route_const, 1)
            pool.memset(ones[:, :], 1.0).then_inc(route_const, 1)
            pool.iota(pid[:, :], [[0, 1]], base=0, channel_multiplier=1).then_inc(route_const, 1)
            pool.wait_ge(route_const, 4)
            pool.affine_select(out=tri4[:, :, :], in_=tri4[:, :, :], compare_op=ALU.is_gt, fill=0.0, base=0,
                               pattern=[[1, E], [-1, E]], channel_multiplier=0).then_inc(route_const, 1)
            pool.affine_select(out=same_e[:, :, :], in_=same_e[:, :, :], compare_op=ALU.is_ge, fill=0.0, base=0,
                               pattern=[[-(P // E), E], [0, P // E]], channel_multiplier=1).then_inc(route_const, 1)
            pool.wait_ge(route_const, 6)
            pool.affine_select(out=same_e[:, :, :], in_=same_e[:, :, :], compare_op=ALU.is_gt, fill=0.0, base=P // E,
                               pattern=[[P // E, E], [0, P // E]], channel_multiplier=-1).then_inc(route_const, 1)
            for b in range(B):
                last = pool.tensor_scalar(xn_all[:, b * D:(b + 1) * D], x_all[:, b * D:(b + 1) * D],
                                          mr_all[:, 2 * b:2 * b + 1], mr_all[:, 2 * b + 1:2 * b + 2],
                                          ALU.subtract, ALU.mult)
            last.then_inc(xnall_r, 1)
            pool.wait_ge(xnall_r, 1)
            pool.wait_ge(zero_st, 16 * (N // P))
            pool.wait_ge(idx_r, 1)
            for b in range(B):
                for k in range(2):
                    pool.indirect_dma_start(out=xg_dram, out_offset=bass.IndirectOffsetOnAxis(ap=idx_put[:, k, b:b + 1], axis=0),
                                            in_=xn_all[:, b * D:(b + 1) * D], in_offset=None,
                                            bounds_check=N - 1, oob_is_err=False).then_inc(put_done, 16)
            pool.wait_ge(put_done, 16 * 2 * B)
            pool.wait_ge(y_st, 16 * E)
            for b in range(B):
                for k in range(2):
                    n = 2 * b + k
                    if n >= NG:
                        pool.wait_ge(comb, n - NG + 1)
                    pool.indirect_dma_start(out=yg[n % NG], out_offset=None, in_=y_dram,
                                            in_offset=bass.IndirectOffsetOnAxis(ap=idx_get[:, k, b:b + 1], axis=0),
                                            bounds_check=N - 1, oob_is_err=False).then_inc(yg_in[n % NG], 16)

        @block.scalar
        def _(act):
            def split_hi(n, dst):
                act.wait_ge(stage_in[n % 2], 16 * (n // 2 + 1))
                act.activation(dst, staged(n), ACT.Copy, scale=WS).then_inc(stage_hi, 1)
            act.wait_ge(kg1w_in, 16)
            act.activation(wh[:, :, C_KG:C_KG + DK], KG_STAGE, ACT.Copy, scale=WS).then_inc(stage_hi, 1)
            act.wait_ge(dca_in, 16)
            act.activation(dca_h, dca32, ACT.Copy, scale=XS).then_inc(dca_split, 1)
            for n in range(len(pieces)):
                split_hi(n, pieces[n][1])

            for t in range(4):
                act.wait_ge(dca_ps, t + 1)
                act.activation(dca_o[t][:, :], psum[t // 2][:, (t % 2) * 512:(t % 2 + 1) * 512], ACT.Copy, scale=UN).then_inc(dca_out, 1)

            def square(dst, src, ready, done, b):
                act.wait_ge(ready, 2 * b + 2)
                act.activation(dst[:, :], src[:, :], ACT.Square).then_inc(done, 1)

            def take(dst, ps, scale, ready, count, done):
                act.wait_ge(ready, count)
                act.activation(dst, ps, ACT.Copy, scale=scale).then_inc(done, 1)

            def cols(ps):
                return ps.rearrange("p (k n) -> p k n", k=KC)

            def body(s):
                A1, A2, B1, B2 = s
                if B1:
                    b, par, half = B1
                    act.wait_ge(ctx_in[par], 16 * (half + 1))
                    if not isinstance(b, int) or b >= 1:
                        act.wait_ge(kv_ps, 2 * b)
                    act.activation(cth[:, :, :], ctx32[par][:, :, :], ACT.Copy, scale=XS).then_inc(cth_r, 1)
                if A1:
                    take(xth[:, :, :], cols(a0), XS, xt_ps, A1[0] + 1, xth_r)
                if B2:
                    take(pT[:, :, :], cols(d0), 1.0, pT_ps, 4 * B2[0] + 1, pT_r)
                if B1:
                    b, par, half = B1
                    take(kraw[0:KEYS, :], c0[0:KEYS], UN, kv_ps, 2 * b + 1, kv_ev)
                    take(vx[par][0:KEYS, :], c1[0:KEYS], UN, kv_ps, 2 * b + 2, kv_ev)
                if A1:
                    take(kg1[:, :], a1[0:DK, 0:L], UN, a1_ps, 5 * A1[0] + 1, kg1_r)
                if B1:
                    square(ksq, kd, cent[1], hq[1], B1[0])
                    take(x2h[:, :, :], cols(c0), XS, x2_ps, B1[0] + 1, x2h_r)
                if B2:
                    take(pT[:, :, :], cols(d0), 1.0, pT_ps, 4 * B2[0] + 2, pT_r)
                if A1:
                    b, par, half = A1
                    act.wait_ge(z_r, b + 1)
                    act.activation(zabs[:, :], z[:, :], ACT.Abs).then_inc(lsig, 1)
                    act.wait_ge(lsig, 3 * b + 1)
                    act.activation(zexp[:, :], zabs[:, :], ACT.Exp, scale=-1.0).then_inc(lsig, 1)
                    act.wait_ge(lsig, 3 * b + 2)
                    act.activation(zln[:, :], zexp[:, :], ACT.Ln, bias=1.0).then_inc(lsig, 1)
                if A2:
                    square(osq, od, cent[0], hq[0], A2[0])
                if B1:
                    take(kT[:, :, :], cols(c0), 1.0, kT_ps, B1[0] + 1, kT_r)
                if B2:
                    take(pT[:, :, :], cols(d0), 1.0, pT_ps, 4 * B2[0] + 3, pT_r)
                if B1:
                    square(qsq, qd, cent[2], hq[2], B1[0])
                if A1:
                    b, par, half = A1
                    take(v[par][:, :], a1, UN, a1_ps, 5 * b + 4, v_r)
                    act.wait_ge(sums, 3 * b + 3)
                    act.activation(eq[:, :], dq[:, :], ACT.Exp, scale=1.0 / NORM).then_inc(decay, 1)
                    act.wait_ge(dk_r, b + 1)
                    act.activation(dk[:, :, :], dk[:, :, :], ACT.Exp, scale=1.0 / NORM).then_inc(decay, 1)
                if B2:
                    take(pT[:, :, :], cols(d0), 1.0, pT_ps, 4 * B2[0] + 4, pT_r)
                if A2:
                    take(oth[:, :, :], cols(b1), XS, ot_ps, A2[0] + 1, oth_r)
                if B1:
                    take(qT[:, :, :], cols(c0), 1.0, qT_ps, B1[0] + 1, qT_r)
                if A1:
                    b, par, half = A1
                    act.wait_ge(gate_v, 2 * b + 1)
                    act.activation(ge[:, :], gf[:, :], ACT.Exp, scale=-1.0).then_inc(ge_r, 1)
                if B2:
                    take(ch[:, :, :], cols(d1), XS, pv_ps, 4 * B2[0] + 4, ch_r)
                if B1:
                    b, par, half = B1
                    for rnd in range(2):
                        act.wait_ge(shift, 4 * b + (2 * rnd + 2))
                        half_p = pr[par][:, rnd * 1024:(rnd + 1) * 1024]
                        act.activation(half_p, half_p, ACT.Exp, scale=XSCALE).then_inc(exp_r, 1)
                if B2:
                    take(x3T[:, :, :], cols(d1), 1.0, x3_ps, B2[0] + 1, x3T_r)

            pipeline(act, body)

            act.wait_ge(route, ROUTE_DIFF)
            act.activation(ed[:, :], ldiff[:, :], ACT.Exp).then_inc(ed_r, 1)
            for i in range(4):
                act.wait_ge(scT_ps, i + 1)
                act.activation(big[0][:, i * 512:(i + 1) * 512], psum[i // 2][:, (i % 2) * 512:(i % 2 + 1) * 512],
                               ACT.Copy).then_inc(scT_r, 1)

            def split_piece(e, n):
                _, dst, _, k = w_piece(e, n)
                act.wait_ge(w_in[n % NST], 16 * (e * (W_PIECES // NST) + n // NST + 1))
                act.activation(dst, wst[n % NST][:, :].rearrange("p (k n) -> p k n", k=k), ACT.Copy, scale=WS).then_inc(w_hi, 1)

            def tokens_hi(e):
                for t in range(4):
                    act.wait_ge(xgT_ps, 4 * e + (t + 1))
                    act.activation(xgh[:, :, t * P:(t + 1) * P], cols(psum[t % 2][:, 0:512]),
                                   ACT.Copy, scale=XS).then_inc(xgh_r, 1)

            def gelu(e, f):
                n = e * (2 * FH) + f
                act.wait_ge(h_ps, n + 1)
                if not (isinstance(e, int) and e == 0 and f < 2):
                    act.wait_ge(hl_r, n - 1)
                act.activation(hg[f % 2], psum[f % 2][:, 512:1024], ACT.Gelu, scale=UN).then_inc(hg_r, 1)

            for n in range(W_PIECES):
                split_piece(0, n)

            def expert(e, more):
                tokens_hi(e)
                for f in range(2 * FH):
                    gelu(e, f)
                    if more and f >= FH and f % 2 == 0:
                        split_first(e + 1, (f - FH) // 2)
                if more:
                    for n in range(W_PIECES // 2, W_PIECES):
                        act.wait_ge(half_used[1], e + 1)
                        split_piece(e + 1, n)

            def split_first(e, n):
                act.wait_ge(half_used[0], e)
                split_piece(e, n)

            expert(0, True)
            with act.Fori(1, E - 1) as e:
                expert(e, True)
            expert(E - 1, False)

        @block.tensor
        def _(pe):
            def mm3(o, lh, ll, rh, rl, first, last):
                nc.tensor.matmul(o, lh, rh, start=first, stop=False)
                nc.tensor.matmul(o, lh, rl, start=False, stop=False)
                return nc.tensor.matmul(o, ll, rh, start=False, stop=last)

            def turn(ps, src, done):
                for c in range(KC):
                    last = nc.tensor.transpose(ps[:, c * P:(c + 1) * P], src[:, c * P:(c + 1) * P], ident[:, :])
                last.then_inc(done, 1)

            def rows(ps, xh, xl, col, done):
                for k in range(KC):
                    last = mm3(ps, xh[:, k, :], xl[:, k, :], wh[:, k, col:col + D], wl[:, k, col:col + D], k == 0, k == KC - 1)
                last.then_inc(done, 1)

            pe.wait_ge(pool_const, 5)
            pe.wait_ge(stage_lo, 1 + 2)
            pe.wait_ge(dca_split, 2)
            for t in range(4):
                ps = psum[t // 2][:, (t % 2) * 512:(t % 2 + 1) * 512]
                tok = slice((t // 2) * P, (t // 2 + 1) * P)
                col = slice((t % 2) * D, (t % 2 + 1) * D)
                for k in range(CC):
                    last = mm3(ps, dca_h[:, k, tok], dca_l[:, k, tok], dca_w[:, 0, k, col], dca_w[:, 1, k, col], k == 0, k == CC - 1)
                last.then_inc(dca_ps, 1)
            pe.wait_ge(dca_out, 4)
            pe.wait_ge(consts_in, 16 * len(consts))
            pe.wait_ge(stage_lo, 1 + len(pieces))

            def a1_turn(b):
                pe.wait_ge(xn_r, b + 1)
                turn(a0, xn[:, :], xt_ps)

            def a1_qk(b):
                pe.wait_ge(xtl_r, b + 1)
                for k in range(KC):
                    last = mm3(a1[0:DK, 0:L], wh[:, k, C_KG:C_KG + DK], wl[:, k, C_KG:C_KG + DK],
                               xth[:, k, :], xtl[:, k, :], k == 0, k == KC - 1)
                last.then_inc(a1_ps, 1)
                for g in range(4):
                    for k in range(KC):
                        c = C_QK + g * P
                        last = mm3(a0[:, g * L:(g + 1) * L], wh[:, k, c:c + P], wl[:, k, c:c + P],
                                   xth[:, k, :], xtl[:, k, :], k == 0, k == KC - 1)
                last.then_inc(a1_ps, 1)

            def a1_kg2(b):
                pe.wait_ge(kg1_r, b + 1)
                for c in range(2):
                    last = nc.tensor.matmul(a1[:, c * L:(c + 1) * L], wkg2_sb[:, c * P:(c + 1) * P], kg1[:, :], start=True, stop=True)
                last.then_inc(a1_ps, 1)

            def a1_v(b):
                pe.wait_ge(z_r, b + 1)
                rows(a1, xth, xtl, C_V, a1_ps)

            def a1_g(b):
                pe.wait_ge(v_r, b + 1)
                rows(a1, xth, xtl, C_G, a1_ps)

            def a2_scores(b, par, rnd):
                pe.wait_ge(qk_r, b + 1)
                if rnd:
                    pe.wait_ge(scm_r, 2 * b + 1)
                for c in range(2):
                    for i in reversed(range(NBLK)):
                        for r in (2 * rnd, 2 * rnd + 1):
                            rw = slice(32 * r, 32 * r + 32)
                            col = (r % 2) * 512 + c * 256 + i * 2 * BLK
                            last = nc.tensor.matmul(psum[1][0:KTW[i], col:col + 2 * BLK], kt[par][rw, c, KTO[i]:KTO[i] + KTW[i]],
                                                    qeo[par][rw, c * NBLK + i, :, :].rearrange("p e t -> p (e t)"), start=True, stop=True)
                last.then_inc(sc_ps, 1)

            def a2_o(b, par):
                pe.wait_ge(scm_r, 2 * b + 2)
                pe.wait_ge(v_r, b + 1)
                sc = scm[:, :].rearrange("p (r c e t) -> p r c e t", r=4, c=2, e=2)
                for h in range(HEADS):
                    j, e = h // 2, h % 2
                    last = nc.tensor.matmul(b0[:, h * DV:(h + 1) * DV], sc[:, j % 4, j // 4, e, :],
                                            v[par][:, h * DV:(h + 1) * DV], start=True, stop=True)
                last.then_inc(o_ps, 1)

            def a2_turn(b):
                pe.wait_ge(og_r, b + 1)
                turn(b1, od[:, :], ot_ps)

            def a2_wo(b):
                pe.wait_ge(otl_r, b + 1)
                rows(b0, oth, otl, C_O, wo_ps)

            def b1_kv(b):
                pe.wait_ge(ctl_r, b + 1)
                if not isinstance(b, int) or b >= 1:
                    pe.wait_ge(shift, 4 * b)
                for n, ps in enumerate((c0, c1)):
                    col = slice(n * D, (n + 1) * D)
                    for k in range(CC):
                        last = mm3(ps[0:KEYS, :], cth[:, k, :], ctl[:, k, :], wch[:, k, col], wcl[:, k, col], k == 0, k == CC - 1)
                    last.then_inc(kv_ps, 1)

            def b1_x(b):
                pe.wait_ge(xn2_r, b + 1)
                pe.wait_ge(kv_ev, 2 * b + 1)
                turn(c0, xn2[:, :], x2_ps)

            def b1_q(b):
                pe.wait_ge(x2l_r, b + 1)
                pe.wait_ge(kv_ev, 2 * b + 2)
                rows(c1, x2h, x2l, C_XQ, q_ps)

            def b1_kT(b):
                pe.wait_ge(k_aff, 2 * b + 2)
                turn(c0, kd[:, :], kT_ps)

            def b1_qT(b):
                pe.wait_ge(q_aff, 2 * b + 2)
                pe.wait_ge(kT_r, b + 1)
                turn(c0, qd[:, :], qT_ps)

            def b1_scores(b, rnd):
                if rnd:
                    pe.wait_ge(shift, 4 * b + 2)
                else:
                    pe.wait_ge(qT_r, b + 1)
                for c in range(KC):
                    for r in (2 * rnd, 2 * rnd + 1):
                        rw = slice(32 * r, 32 * r + 32)
                        col = (r % 2) * 512 + c * P
                        last = nc.tensor.matmul(psum[2][:, col:col + L], qT[rw, c, :], kT[rw, c, :], start=True, stop=True)
                last.then_inc(xs_ps, 1)

            def b2_turn(b, par, r):
                pe.wait_ge(pr_r, 2 * b + (r // 2 + 1))
                if r:
                    pe.wait_ge(pT_r, 4 * b + r)
                elif not isinstance(b, int) or b >= 1:
                    pe.wait_ge(lg_r, b)
                turn(d0, pr[par][:, r * 512:(r + 1) * 512], pT_ps)

            def b2_pv(b, par, r):
                pe.wait_ge(pT_r, 4 * b + (r + 1))
                pe.wait_ge(kv_bias, 2 * b + 2)
                for c in range(KC):
                    h = 4 * c + r
                    last = nc.tensor.matmul(d1[32 * r:32 * r + 32, c * L:(c + 1) * L], vx[par][:, h * DV:(h + 1) * DV],
                                            pT[:, c, :], start=True, stop=True)
                last.then_inc(pv_ps, 1)

            def b2_wo(b):
                pe.wait_ge(cl_r, b + 1)
                rows(d0, ch, cl, C_XO, xo_ps)

            def b2_logits(b):
                pe.wait_ge(x3T_r, b + 1)
                pe.wait_ge(x2_r, b + 1)
                for k in range(KC):
                    last = nc.tensor.matmul(d0[:, 0:E], x3T[:, k, :], wgate_sb[:, k, :], start=(k == 0), stop=(k == KC - 1))
                last.then_inc(lg_ps, 1)

            def b2_x3(b):
                pe.wait_ge(xn3_r, b + 1)
                turn(d1, xn3[:, :], x3_ps)

            def body(s):
                A1, A2, B1, B2 = s
                if B1:
                    b1_kv(B1[0])
                if A1:
                    a1_turn(A1[0])
                if A2:
                    a2_scores(A2[0], A2[1], 0)
                if B2:
                    b2_turn(B2[0], B2[1], 0)
                if A1:
                    a1_qk(A1[0])
                if A2:
                    a2_scores(A2[0], A2[1], 1)
                if B1:
                    b1_x(B1[0])
                if B2:
                    b2_pv(B2[0], B2[1], 0)
                    b2_turn(B2[0], B2[1], 1)
                if A1:
                    a1_kg2(A1[0])
                if A2:
                    a2_o(*A2[0:2])
                if B1:
                    b1_q(B1[0])
                    b1_kT(B1[0])
                if B2:
                    b2_pv(B2[0], B2[1], 1)
                    b2_turn(B2[0], B2[1], 2)
                if A1:
                    a1_v(A1[0])
                if B2:
                    b2_pv(B2[0], B2[1], 2)
                    b2_turn(B2[0], B2[1], 3)
                if A2:
                    a2_turn(A2[0])
                if A1:
                    a1_g(A1[0])
                if B1:
                    b1_qT(B1[0])
                if B2:
                    b2_pv(B2[0], B2[1], 3)
                if A2:
                    a2_wo(A2[0])
                if B1:
                    b1_scores(B1[0], 0)
                if B2:
                    b2_wo(B2[0])
                if B1:
                    b1_scores(B1[0], 1)
                if B2:
                    b2_x3(B2[0])
                    b2_logits(B2[0])

            pipeline(pe, body)

            pe.wait_ge(rep_r, 1)
            for b in range(B):
                ps = psum[b // 8][:, (b % 8) * P:(b % 8 + 1) * P]
                last = nc.tensor.transpose(ps, big[0][:, b * P:(b + 1) * P], ident[:, :])
                if b % 4 == 3:
                    last.then_inc(scT_ps, 1)
            pe.wait_ge(route_const, 7)
            for n in range(len(SHIFTS)):
                pe.wait_ge(cnt_r, n + 1)
                nc.tensor.matmul(psum[2][:, 0:1], same_e[:, :, :].rearrange("p e r -> p (e r)"), enough[:, :],
                                 start=True, stop=True).then_inc(dig_ps, 1)
            pe.wait_ge(pos_r, 1)
            for b in range(B):
                ps = psum[b // 8][:, (b % 8) * P:(b % 8 + 1) * P]
                last = nc.tensor.transpose(ps, big[3][:, b * P:(b + 1) * P], ident[:, :])
            last.then_inc(posT_ps, 1)

            def tokens(e):
                pe.wait_ge(xg_in, 16 * (e + 1))
                for t in range(4):
                    if not (isinstance(e, int) and e == 0 and t < 2):
                        pe.wait_ge(xgl_r, 4 * e + (t - 1))
                    turn(psum[t % 2][:, 0:512], xg32[:, t, :], xgT_ps)

            def up(e, f):
                n = e * (2 * FH) + f
                if not (isinstance(e, int) and e == 0 and f < 2):
                    pe.wait_ge(hg_r, n - 1)
                hf, fc = f // FH, f % FH
                pe.wait_ge(w_lo, W_PIECES * e + (4 * hf + 2))
                for k in range(KC):
                    c = slice(fc * P, (fc + 1) * P)
                    last = mm3(psum[f % 2][:, 512:1024], w1h[hf][:, k, c], w1l[hf][:, k, c], xgh[:, k, :], xgl[:, k, :],
                               k == 0, k == KC - 1)
                last.then_inc(h_ps, 1)

            def down(e, f):
                n = e * (2 * FH) + f
                hf, fc = f // FH, f % FH
                pe.wait_ge(w_lo, W_PIECES * e + (4 * hf + 4))
                pe.wait_ge(hl_r, n + 1)
                if f == 0 and not (isinstance(e, int) and e == 0):
                    pe.wait_ge(y_ev, 4 * e)
                for t in range(4):
                    tk = slice(t * P, (t + 1) * P)
                    last = mm3(psum[2 + t // 2][:, (t % 2) * 512:(t % 2 + 1) * 512], hh[f % 2][:, tk], hl[f % 2][:, tk],
                               w2h[hf][:, fc, :], w2l[hf][:, fc, :], f == 0, f == 2 * FH - 1)
                if fc == FH - 1:
                    last.then_inc(half_used[hf], 1)
                else:
                    last.then_inc(h_used, 1)

            def expert(e):
                tokens(e)
                pe.wait_ge(xgl_r, 4 * (e + 1))
                up(e, 0)
                for f in range(2 * FH):
                    if f + 1 < 2 * FH:
                        up(e, f + 1)
                    down(e, f)

            expert(0)
            with pe.Fori(1, E) as e:
                expert(e)

        @block.vector
        def _(dve):
            dve.memset(carry[:, :], 1.0).then_inc(dve_const, 1)
            dve.wait_ge(dve_const, 1)
            dve.memset(carry[:, L:L + 1], 0.0).then_inc(dve_const, 1)
            dve.wait_ge(pool_const, 6)
            dve.tensor_scalar(half_id[:, :], row_id[:, :], DK, None, ALU.bitwise_and).then_inc(dve_const, 1)
            dve.wait_ge(dve_const, 3)
            dve.tensor_scalar(pair_half[:, 1:2], half_id[:, :], UN / DK, None, ALU.mult).then_inc(dve_const, 1)
            dve.tensor_scalar(pair_half[:, 0:1], half_id[:, :], -UN / DK, UN, ALU.mult, ALU.add).then_inc(dve_const, 1)

            def low(dst, src, scale, hi):
                return dve.scalar_tensor_tensor(dst, src, scale, hi, ALU.mult, ALU.subtract)

            dve.wait_ge(stage_hi, 1)
            low(wl[:, :, C_KG:C_KG + DK], KG_STAGE, WS, wh[:, :, C_KG:C_KG + DK]).then_inc(stage_lo, 1)
            dve.wait_ge(dca_split, 1)
            low(dca_l, dca32, XS, dca_h).then_inc(dca_split, 1)
            for n in range(len(pieces)):
                dve.wait_ge(stage_hi, n + 2)
                low(pieces[n][2], staged(n), WS, pieces[n][1]).then_inc(stage_lo, 1)
            dve.wait_ge(dca_ps, 4)
            dve.memset(scm[:, :], 0.0).then_inc(scm_zero, 1)
            dve.wait_ge(scm_zero, 1)
            dve.wait_ge(dve_const, 5)
            dve.wait_ge(consts_in, 16 * len(consts))
            dve.wait_ge(dca_stored, 64)

            def cols(ps):
                return ps.rearrange("p (k n) -> p k n", k=KC)

            apart = [0]

            def wait_apart(signal, value):
                dve.wait_ge(signal, value)
                apart[0] = (apart[0] + 1) % PADS
                dve.memset(wait_pad[:, apart[0]:apart[0] + 1], 0.0)

            def row_stats(n, src, b):
                dve.bn_stats(stats[n][:, :], src).then_inc(stat[n], 1)
                wait_apart(stat[n], 2 * b + 1)
                dve.bn_aggr(aggr[n][:, :], stats[n][:, :]).then_inc(stat[n], 1)

            def row_norm(n, dst, src, done, b):
                dve.wait_ge(dev[n], 2 * b + 2)
                dve.tensor_scalar(dst[:, :], src, aggr[n][:, 0:1], rstd[n][:, :], ALU.subtract, ALU.mult).then_inc(done, 1)

            def head_centre(n, dst, src, b):
                dve.tensor_reduce(hsum[n][:, :], heads(src), AX.X, ALU.add).then_inc(cent[n], 1)
                dve.wait_ge(cent[n], 2 * b + 1)
                dve.scalar_tensor_tensor(heads(dst[:, :]), per_head(hsum[n][:, :]), -1.0 / DV, heads(src),
                                         ALU.mult, ALU.add).then_inc(cent[n], 1)

            def head_var(n, sq, b):
                dve.wait_ge(hq[n], b + 1)
                dve.tensor_reduce(hvar[n][:, :], heads(sq[:, :]), AX.X, ALU.add).then_inc(hv[n], 1)

            def head_norm(n, dst, done, b):
                dve.wait_ge(hdev[n], 2 * b + 2)
                dve.scalar_tensor_tensor(heads(dst[:, :]), heads(dst[:, :]), DV ** 0.5, per_head(hrs[n][:, :]), ALU.mult, ALU.mult).then_inc(done, 1)

            def a1_norm(b):
                if isinstance(b, int):
                    for n in x_loaded(b):
                        dve.wait_ge(x_in[n], 16)
                row_stats(0, x_all[:, seq(b)], b)
                row_norm(0, xn, x_all[:, seq(b)], xn_r, b)

            def a1_low(b):
                dve.wait_ge(xth_r, b + 1)
                low(xtl[:, :, :], cols(a0), XS, xth[:, :, :]).then_inc(xtl_r, 1)

            def a1_decay(b):
                dve.wait_ge(a1_ps, 5 * b + 3)
                z3 = z[:, :].rearrange("p (c t) -> p c t", c=2)
                dve.tensor_tensor(z3, a1[:, 0:QK].rearrange("p (c t) -> p c t", c=2),
                                  bkg2_sb[:, :].unsqueeze(2).to_broadcast([P, 2, L]), ALU.add).then_inc(z_r, 1)

            def a1_sums(b):
                dve.wait_ge(lsig, 3 * b + 3)
                dve.scalar_tensor_tensor(lsg[:, :], z[:, :], 0.0, zln[:, :], ALU.min, ALU.subtract).then_inc(sums, 1)
                dve.wait_ge(sums, 3 * b + 1)
                dve.tensor_tensor_scan(G[:, :], carry[:, :], lsg[:, :], 0.0, ALU.mult, ALU.add).then_inc(sums, 1)
                dve.wait_ge(sums, 3 * b + 2)
                G3 = G[:, :].rearrange("p (n t) -> p n t", t=BLK)
                m = BLK // 2 - 1
                dve.tensor_tensor(dq[:, :].rearrange("p (n t) -> p n t", t=BLK), G3,
                                  G3[:, :, m:m + 1].to_broadcast([P, 2 * NBLK, BLK]), ALU.subtract).then_inc(sums, 1)

            def a1_decayed(b, par):
                dve.wait_ge(a1_ps, 5 * b + 2)
                dve.wait_ge(decay, 2 * b + 1)
                blocks = lambda ap: ap.rearrange("p (n t) -> p n t", t=BLK)
                for e in range(2):
                    dve.scalar_tensor_tensor(qeo[par][:, :, e, :], blocks(a0[:, 0:QK]), pair_half[:, e:e + 1], blocks(eq[:, :]),
                                             ALU.mult, ALU.mult)
                dve.wait_ge(decay, 2 * b + 2)
                k3 = a0[:, QK:2 * QK].rearrange("p (c t) -> p c t", c=2)
                for i in range(NBLK):
                    w = slice(KTO[i], KTO[i] + KTW[i])
                    last = dve.scalar_tensor_tensor(kt[par][:, :, w], k3[:, :, 0:KTW[i]], GLA_SCALE * UN, dk[:, :, w],
                                                    ALU.mult, ALU.mult)
                last.then_inc(qk_r, 1)

            def a1_gate(b):
                dve.wait_ge(a1_ps, 5 * b + 5)
                dve.scalar_tensor_tensor(gf[:, :], a1, UN, bg_sb[:, :], ALU.mult, ALU.add).then_inc(gate_v, 1)

            def a1_recip(b):
                dve.wait_ge(gate_p, 2 * b + 1)
                dve.reciprocal(ge[:, :], ge[:, :]).then_inc(gate_v, 1)

            def a2_mask(b, rnd):
                wait_apart(sc_ps, 2 * b + (rnd + 1))
                for i in range(NBLK):
                    w = KTW[i]
                    dst = scm[0:w, rnd * 1024:(rnd + 1) * 1024].rearrange("p (g t) -> p g t", t=L)[:, :, i * BLK:(i + 1) * BLK]
                    dst = dst.rearrange("p (g e) t -> p g e t", e=2)
                    src = psum[1][0:w, :].rearrange("p (g i e t) -> p g i e t", i=NBLK, e=2, t=BLK)[:, :, i]
                    mask = causal[0:w, i:i + 1, :].bitcast(I32).rearrange("p i (e t) -> p i e t", e=2).to_broadcast([w, 4, 2, BLK])
                    last = dve.copy_predicated(dst, mask, src)
                last.then_inc(scm_r, 1)

            def a2_centre(b):
                dve.wait_ge(o_ps, b + 1)
                head_centre(0, od, b0, b)

            def a2_low(b):
                dve.wait_ge(oth_r, b + 1)
                low(otl[:, :, :], cols(b1), XS, oth[:, :, :]).then_inc(otl_r, 1)

            def a2_residual(b):
                dve.wait_ge(wo_ps, b + 1)
                dve.scalar_tensor_tensor(x_all[:, seq(b)], b0, UN, x_all[:, seq(b)], ALU.mult, ALU.add).then_inc(x1_r, 1)

            def b1_ctx(b, par):
                dve.wait_ge(cth_r, b + 1)
                low(ctl[:, :, :], ctx32[par][:, :, :], XS, cth[:, :, :]).then_inc(ctl_r, 1)

            def b1_norm(b):
                wait_apart(x1_r, b + 1)
                row_stats(1, x_all[:, seq(b)], b)

            def b1_low(b):
                dve.wait_ge(x2h_r, b + 1)
                low(x2l[:, :, :], cols(c0), XS, x2h[:, :, :]).then_inc(x2l_r, 1)

            def b1_q(b):
                dve.wait_ge(q_ps, b + 1)
                dve.scalar_tensor_tensor(qraw[:, :], c1, UN, bq_sb[:, :], ALU.mult, ALU.add).then_inc(q_r, 1)
                dve.wait_ge(q_r, b + 1)
                head_centre(2, qd, qraw[:, :], b)

            def b1_softmax(b, par, rnd):
                dve.wait_ge(xs_ps, 2 * b + (rnd + 1))
                s3 = psum[2][:, :].rearrange("p (h k) -> p h k", k=L)
                p3 = pr[par][:, rnd * 1024:(rnd + 1) * 1024].rearrange("p (h k) -> p h k", k=L)
                hh8 = slice(rnd * 8, rnd * 8 + 8)
                parts = ((0, slice(0, KEYS), KEYS), (1, slice(KEYS, L), NDCA))
                for n, ks, w in parts:
                    last = dve.tensor_reduce(mx[:, n, hh8], s3[:, :, ks], AX.X, ALU.max)
                last.then_inc(shift, 1)
                dve.wait_ge(shift, 4 * b + (2 * rnd + 1))
                for n, ks, w in parts:
                    last = dve.tensor_tensor(p3[:, :, ks], s3[:, :, ks], mx[:, n, hh8].unsqueeze(2).to_broadcast([P, 8, w]), ALU.subtract)
                last.then_inc(shift, 1)

            def b1_sums(b, par, rnd):
                p3 = pr[par][:, rnd * 1024:(rnd + 1) * 1024].rearrange("p (h k) -> p h k", k=L)
                hh8 = slice(rnd * 8, rnd * 8 + 8)
                dve.wait_ge(exp_r, 2 * b + (rnd + 1))
                for n, ks in ((0, slice(0, KEYS)), (1, slice(KEYS, L))):
                    last = dve.tensor_reduce(sm[:, n, hh8], p3[:, :, ks], AX.X, ALU.add)
                last.then_inc(norm, 1)
                dve.wait_ge(norm, 4 * b + (2 * rnd + 1))
                dve.reciprocal(rc[:, :, hh8], sm[:, :, hh8]).then_inc(norm, 1)

            def b2_low(b):
                dve.wait_ge(ch_r, b + 1)
                low(cl[:, :, :], cols(d1), XS, ch[:, :, :]).then_inc(cl_r, 1)

            def b2_residual(b):
                dve.wait_ge(xo_ps, b + 1)
                dve.wait_ge(xbo_r, b + 1)
                dve.scalar_tensor_tensor(x_all[:, seq(b)], d0, UN, x_all[:, seq(b)], ALU.mult, ALU.add).then_inc(x2_r, 1)
                wait_apart(x2_r, b + 1)
                row_stats(2, x_all[:, seq(b)], b)

            def b2_logits(b):
                dve.wait_ge(lg_ps, b + 1)
                dve.tensor_tensor(logit_all[:, bass.ds(b * E, E)], d0[:, 0:E], bgate_sb[:, :], ALU.add).then_inc(lg_r, 1)

            def body(s):
                A1, A2, B1, B2 = s
                if B1:
                    b1_ctx(B1[0], B1[1])
                    b1_norm(B1[0])
                if A1:
                    a1_norm(A1[0])
                if A2:
                    a2_mask(A2[0], 0)
                if A1:
                    a1_low(A1[0])
                if B1:
                    dve.wait_ge(kv_bias, 2 * B1[0] + 1)
                    head_centre(1, kd, kraw[:, :], B1[0])
                    head_var(1, ksq, B1[0])
                    row_norm(1, xn2, x_all[:, seq(B1[0])], xn2_r, B1[0])
                if A2:
                    a2_mask(A2[0], 1)
                if B1:
                    head_norm(1, kd, kn_r, B1[0])
                    b1_low(B1[0])
                if A1:
                    a1_decay(A1[0])
                if A2:
                    a2_centre(A2[0])
                if A1:
                    a1_sums(A1[0])
                if A2:
                    head_var(0, osq, A2[0])
                if B1:
                    b1_q(B1[0])
                if A2:
                    head_norm(0, od, on_r, A2[0])
                if B1:
                    head_var(2, qsq, B1[0])
                if A1:
                    a1_decayed(A1[0], A1[1])
                if B1:
                    head_norm(2, qd, qn_r, B1[0])
                if A2:
                    a2_low(A2[0])
                if A1:
                    a1_gate(A1[0])
                if B2:
                    b2_low(B2[0])
                if A1:
                    a1_recip(A1[0])
                if B1:
                    b1_softmax(B1[0], B1[1], 0)
                if A2:
                    a2_residual(A2[0])
                if B2:
                    b2_residual(B2[0])
                if B1:
                    b1_softmax(B1[0], B1[1], 1)
                    b1_sums(B1[0], B1[1], 0)
                if B2:
                    row_norm(2, xn3, x_all[:, seq(B2[0])], xn3_r, B2[0])
                if B1:
                    b1_sums(B1[0], B1[1], 1)
                if B2:
                    b2_logits(B2[0])

            pipeline(dve, body)

            step = [0]

            def link(ins):
                step[0] += 1
                ins.then_inc(route, 1)
                dve.wait_ge(route, step[0])

            dve.wait_ge(lg_r, B)
            dve.wait_ge(route_const, 7)
            lg = logit_all[:, :].rearrange("p (b e) -> p b e", e=E)
            mine = lg.unsqueeze(3).to_broadcast([P, B, E, E])
            other = lg.unsqueeze(2).to_broadcast([P, B, E, E])
            tri_b = tri4[:, :, :].rearrange("p a c -> p (a c)").unsqueeze(1).to_broadcast([P, B, E * E])
            flat = lambda t: t[:, :, :, :].rearrange("p b a c -> p b (a c)")
            dve.tensor_tensor(cmp_gt[:, :, :, :], other, mine, ALU.is_gt)
            link(dve.tensor_tensor(cmp_eq[:, :, :, :], other, mine, ALU.is_equal))
            link(dve.tensor_tensor(flat(cmp_eq), flat(cmp_eq), tri_b, ALU.mult))
            link(dve.tensor_tensor(flat(cmp_gt), flat(cmp_gt), flat(cmp_eq), ALU.add))
            link(dve.tensor_reduce(rank[:, :, :], cmp_gt[:, :, :, :], AX.X, ALU.add))
            dve.tensor_scalar(oh[0][:, :, :], rank[:, :, :], 0.0, None, ALU.is_equal)
            dve.tensor_reduce(l1[:, :], lg, AX.X, ALU.max)
            link(dve.tensor_scalar(oh[1][:, :, :], rank[:, :, :], 1.0, None, ALU.is_equal))
            link(dve.tensor_tensor(ohl[:, :, :], oh[1][:, :, :], lg, ALU.mult))
            link(dve.tensor_reduce(l2[:, :], ohl[:, :, :], AX.X, ALU.add))
            link(dve.tensor_tensor(ldiff[:, :], l2[:, :], l1[:, :], ALU.subtract))
            assert step[0] == ROUTE_DIFF
            dve.wait_ge(ed_r, 1)
            link(dve.tensor_scalar(den[:, :], ed[:, :], 1.0, None, ALU.add))
            link(dve.reciprocal(p12[:, 0, :], den[:, :]))
            link(dve.tensor_tensor(p12[:, 1, :], p12[:, 0, :], ed[:, :], ALU.mult))
            pk = lambda k: p12[:, k, :].unsqueeze(2).to_broadcast([P, B, E])
            dve.tensor_tensor(score[:, :, :], oh[0][:, :, :], pk(0), ALU.mult)
            link(dve.tensor_tensor(sc2[:, :, :], oh[1][:, :, :], pk(1), ALU.mult))
            link(dve.tensor_tensor(score[:, :, :], score[:, :, :], sc2[:, :, :], ALU.add))
            rep = score[:, :, :].rearrange("p b e -> p (b e)").unsqueeze(2).to_broadcast([P, B * E, P // E])
            dve.tensor_copy(big[0][:, :].rearrange("p (n r) -> p n r", r=P // E), rep).then_inc(rep_r, 1)
            link(dve.tensor_scalar(digit[:, :], pid[:, :], P // E - 1, None, ALU.bitwise_and))
            link(dve.tensor_scalar(eid[:, :], pid[:, :], RADIX, None, ALU.logical_shift_right))
            for n, s in enumerate(SHIFTS):
                dve.tensor_scalar(cands[:, n:n + 1], digit[:, :], s, None, ALU.logical_shift_left)
            dve.tensor_scalar(slot0[:, :], eid[:, :], float(CAP), -1.0 - FAR, ALU.mult, ALU.add)
            link(dve.memset(thr[:, :], 0))
            dve.wait_ge(scT_r, 4)
            for n, s in enumerate(SHIFTS):
                link(dve.tensor_tensor(cand[:, :], thr[:, :], cands[:, n:n + 1], ALU.bitwise_or))
                link(dve.tensor_scalar(big[1][:, :], big[0][:, :], cand[:, :].bitcast(F32), 0.0, ALU.is_ge, ALU.add, accum_out=count[:, :]))
                dve.tensor_scalar(enough[:, :], count[:, :], float(CAP), None, ALU.is_ge).then_inc(cnt_r, 1)
                dve.wait_ge(dig_ps, n + 1)
                link(dve.tensor_scalar(digit[:, :], psum[2][:, 0:1], -1.0, None, ALU.add))
                link(dve.tensor_scalar(digit[:, :], digit[:, :], s, None, ALU.logical_shift_left))
                link(dve.tensor_tensor(thr[:, :], thr[:, :], digit[:, :], ALU.bitwise_or))
            thr_f = thr[:, :].bitcast(F32)
            link(dve.tensor_scalar(big[1][:, :], big[0][:, :], thr_f, 0.0, ALU.is_gt, ALU.add, accum_out=count[:, :]))
            dve.tensor_scalar(ties[:, :], count[:, :], -1.0, float(CAP), ALU.mult, ALU.add)
            link(dve.tensor_scalar(big[2][:, :], big[0][:, :], thr_f, None, ALU.is_equal))
            one = ones[:, :].to_broadcast([P, N])
            link(dve.tensor_tensor_scan(big[3][:, :], one, big[2][:, :], 0.0, ALU.mult, ALU.add))
            link(dve.scalar_tensor_tensor(big[2][:, :], big[3][:, :], ties[:, :], big[2][:, :], ALU.is_le, ALU.mult))
            link(dve.tensor_tensor(big[1][:, :], big[1][:, :], big[2][:, :], ALU.add))
            link(dve.tensor_tensor_scan(big[2][:, :], one, big[1][:, :], 0.0, ALU.mult, ALU.add))
            dve.scalar_tensor_tensor(big[3][:, :], big[2][:, :], slot0[:, :], big[1][:, :], ALU.add, ALU.mult).then_inc(pos_r, 1)
            dve.wait_ge(posT_ps, 1)
            for g in range(2):
                src = psum[g][:, :].rearrange("p (b e r) -> p b e r", b=8, r=P // E)[:, :, :, 0]
                last = dve.tensor_scalar(posT[:, 8 * g:8 * g + 8, :], src, FAR, None, ALU.add)
            link(last)
            for k in range(2):
                link(dve.tensor_tensor(sel_k[:, :, :], oh[k][:, :, :], posT[:, :, :], ALU.mult))
                link(dve.tensor_reduce(idx[:, k, :], sel_k[:, :, :], AX.X, ALU.add))
            dve.scalar_tensor_tensor(wk[:, :, :], idx[:, :, :], float(N), p12[:, :, :], ALU.is_lt, ALU.mult)
            dve.tensor_scalar(idx_get[:, :, :], idx[:, :, :], float(N - 1), None, ALU.min)
            link(dve.tensor_copy(idx_put[:, :, :], idx[:, :, :]))
            dve.tensor_copy(ldiff[:, :], ldiff[:, :]).then_inc(idx_r, 1)

            def low_piece(e, n):
                _, hi, lo, k = w_piece(e, n)
                dve.wait_ge(w_hi, e * W_PIECES + (n + 1))
                low(lo, wst[n % NST][:, :].rearrange("p (k n) -> p k n", k=k), WS, hi).then_inc(w_lo, 1)

            def tokens_low(e):
                for t in range(4):
                    dve.wait_ge(xgh_r, 4 * e + (t + 1))
                    tk = slice(t * P, (t + 1) * P)
                    low(xgl[:, :, tk], cols(psum[t % 2][:, 0:512]), XS, xgh[:, :, tk]).then_inc(xgl_r, 1)

            def split_h(e, f):
                n = e * (2 * FH) + f
                dve.wait_ge(hg_r, n + 1)
                dve.tensor_scalar(hh[f % 2], hg[f % 2], XS, None, ALU.mult).then_inc(hh_r, 1)
                dve.wait_ge(hh_r, n + 1)
                low(hl[f % 2], hg[f % 2], XS, hh[f % 2]).then_inc(hl_r, 1)

            def results(e):
                dve.wait_ge(half_used[1], e + 1)
                if not isinstance(e, int) or e >= 1:
                    dve.wait_ge(y_st, 16 * e)
                for t in range(4):
                    dve.tensor_scalar(y_sb[:, t, :], psum[2 + t // 2][:, (t % 2) * 512:(t % 2 + 1) * 512], UN, None,
                                      ALU.mult).then_inc(y_ev, 1)

            def expert(e, more):
                tokens_low(e)
                for f in range(2 * FH):
                    if f >= 2 and f != FH + 1:
                        dve.wait_ge(h_used, e * (2 * FH - 2) + (f - 1 if f <= FH else f - 2))
                    split_h(e, f)
                    if more and f >= FH and f % 2 == 0:
                        low_piece(e + 1, (f - FH) // 2)
                results(e)
                if more:
                    for n in range(W_PIECES // 2, W_PIECES):
                        low_piece(e + 1, n)

            for n in range(W_PIECES):
                low_piece(0, n)
            expert(0, True)
            with dve.Fori(1, E - 1) as e:
                expert(e, True)
            expert(E - 1, False)

            for b in range(B):
                for k in range(2):
                    n = 2 * b + k
                    dve.wait_ge(yg_in[n % NG], 16 * (n // NG + 1))
                    if k:
                        dve.wait_ge(comb, n)
                    ins = dve.scalar_tensor_tensor(x_all[:, b * D:(b + 1) * D], yg[n % NG], wk[:, k, b:b + 1],
                                                   x_all[:, b * D:(b + 1) * D], ALU.mult, ALU.add)
                    ins.then_inc(comb, 1)
                dve.wait_ge(comb, 2 * b + 2)
                dve.tensor_copy(ldiff[:, :], l1[:, :]).then_inc(comb_r, 1)


ROUTE_DIFF = 8


def kernel(**inputs):
    import numpy as np
    import concourse.bacc as bacc
    from concourse import mybir as my
    from concourse.bass_utils import run_bass_kernel_spmd

    g = {k: np.asarray(a) for k, a in inputs.items()}
    cat = np.concatenate
    main = g["ctx_1024"].shape[1] - 16
    kv = cat([g["L0_xattn_Wk"], g["L0_xattn_Wv"]], axis=1).reshape(256, 16, 2, 32)
    kvb = cat([g["L0_xattn_bk"], g["L0_xattn_bv"]]).reshape(16, 2, 32)
    arrays = {
        "x": g["x"],
        "ctx_t": g["ctx_1024"][:, :main].transpose(0, 2, 1),
        "dca_t": g["ctx_1024"][:, main:].reshape(-1, 256).T,
        "w_attn": cat([g["L0_attn_Wq"].T, g["L0_attn_Wk"].T, g["L0_attn_Wkg1"].T, g["L0_attn_Wv"].T, g["L0_attn_Wg"].T,
                       g["L0_attn_Wo"].T, g["L0_xattn_Wq"], g["L0_xattn_Wo"]], axis=1),
        "w_ctx": cat([kv[:, :, 0].reshape(256, 512), kv[:, :, 1].reshape(256, 512), g["L0_xattn_Wkv_dca"]], axis=1),
        "w_kg2": g["L0_attn_Wkg2"].T,
        "b_kg2": g["L0_attn_bkg2"].reshape(2, 128).T,
        "b_g": g["L0_attn_bg"], "b_q": g["L0_xattn_bq"],
        "b_kv": cat([kvb[:, 0].reshape(512), kvb[:, 1].reshape(512)]),
        "b_dca": g["L0_xattn_bkv_dca"],
        "w_qn": g["L0_xattn_qn_w"], "b_qn": g["L0_xattn_qn_b"], "w_kn": g["L0_xattn_kn_w"], "b_kn": g["L0_xattn_kn_b"],
        "w_kd": g["L0_xattn_kn_dca_w"], "b_kd": g["L0_xattn_kn_dca_b"],
        "b_o": g["L0_xattn_bo"], "w_gate": g["L0_ffn_Wg"], "b_gate": g["L0_ffn_bg"],
        "w1": g["L0_ffn_W1"], "w2": g["L0_ffn_W2"],
    }
    nc = bacc.Bacc("TRN2", target_bir_lowering=False, num_devices=1)
    feed, args = {}, []
    for name, a in arrays.items():
        a = np.ascontiguousarray(a)
        feed[f"in_{name}"] = a
        args.append(nc.dram_tensor(f"in_{name}", a.shape, my.dt.from_np(a.dtype), kind="ExternalInput").ap())
    out = nc.dram_tensor("out", g["x"].shape, my.dt.float32, kind="ExternalOutput").ap()
    decoder_layer(nc, None, *args, out)
    r = run_bass_kernel_spmd(nc, [feed], core_ids=[0])
    return r.results[0]["out"]
```

```python
from contextlib import ExitStack

import concourse.bass as bass
from concourse import mybir

ALU = mybir.AluOpType
ACT = mybir.ActivationFunctionType
AX = mybir.AxisListType
F32 = mybir.dt.float32
F16 = mybir.dt.float16
I32 = mybir.dt.int32


def decoder_layer(nc, stage_out, x, ctx_t, dca_t, w_attn, w_ctx, w_kg2, b_kg2, b_g, b_q, b_kv, b_dca,
                  cols_n, b_o, w_gate, b_gate, w1, w2, out):
    B, L, D = x.shape
    P = 128
    KC = D // P
    HEADS = 16
    DV = D // HEADS
    DK = 16
    QK = HEADS * DK
    KEYS = ctx_t.shape[2]
    NDCA = L - KEYS
    CC = ctx_t.shape[1] // P
    BLK = 32
    NBLK = L // BLK
    KTW = [BLK * (i + 1) for i in range(NBLK)]
    KTO = [sum(KTW[:i]) for i in range(NBLK)]
    KTN = sum(KTW)
    E = w_gate.shape[1]
    HID = w1.shape[2]
    N = B * L
    CAP = N // E
    XS, WS = 16.0, 256.0
    UN = 1.0 / (XS * WS)
    PADS = 4
    EPS_ROW = 1e-5
    EPS_HEAD = (1e-5, 1e-6, 1e-6)
    GLA_SCALE = 128.0 ** -0.5
    NORM = 16.0
    XSCALE = DV ** -0.5
    RADIX = 5
    SHIFTS = list(range(30 - RADIX, -1, -RADIX))
    FAR = float(2 * N)

    C_QK, C_KG, C_V, C_G, C_O, C_XQ, C_XO = 0, 512, 528, 1040, 1552, 2064, 2576
    W_COLS = C_XO + D

    dca_dram = nc.dram_tensor("dca_scratch", (B * NDCA, 2 * D), F32).ap()
    xg_dram = nc.dram_tensor("xg_scratch", (E * CAP, D), F32).ap()
    y_dram = nc.dram_tensor("y_scratch", (E * CAP, D), F32).ap()
    out_rows = out.rearrange("b l d -> (b l) d")

    with ExitStack() as ctx:
        def sem(name):
            return ctx.enter_context(nc.semaphore(name))

        def sems(name, n):
            return [sem(f"{name}{i}") for i in range(n)]

        def keep(name, shape, dt=F32):
            return ctx.enter_context(nc.sbuf_tensor(name, shape, dt))

        x_all = keep("x_all", [P, B * D])
        ident = keep("ident", [P, P])
        logit_all = keep("logit_all", [P, B * E])
        mr_all = keep("mr_all", [P, 2 * B])
        neg_half = keep("neg_half", [P, HEADS])

        at = ExitStack()

        def sb(name, shape, dt=F32):
            return at.enter_context(nc.sbuf_tensor(name, shape, dt))

        wh = sb("wh", [P, KC, W_COLS], F16)
        wl = sb("wl", [P, KC, W_COLS], F16)
        wch = sb("wch", [P, CC, 2 * D], F16)
        wcl = sb("wcl", [P, CC, 2 * D], F16)
        wkg2_sb = sb("wkg2_sb", [DK, QK])
        bkg2_sb = sb("bkg2_sb", [P, QK // P])
        bg_sb = sb("bg_sb", [P, D])
        bq_sb = sb("bq_sb", [P, D])
        bo_sb = sb("bo_sb", [P, D])
        bkv_sb = sb("bkv_sb", [P, 2 * D])
        head_cols = sb("head_cols", [P, 6])
        cent_sums = sb("cent_sums", [P, KC, HEADS])
        wgate_sb = sb("wgate_sb", [P, KC, E])
        bgate_sb = sb("bgate_sb", [P, E])
        row_id = sb("row_id", [P, 1], I32)
        half_id = sb("half_id", [P, 1], I32)
        pair_half = sb("pair_half", [P, 2])
        causal = sb("causal", [P, NBLK, 2 * BLK])
        carry = sb("carry", [P, QK])

        stats = [sb(f"stats{n}", [P, 6]) for n in range(3)]
        aggr = [sb(f"aggr{n}", [P, 2]) for n in range(3)]
        vare = [sb(f"vare{n}", [P, 1]) for n in range(3)]
        rstd = [sb(f"rstd{n}", [P, 1]) for n in range(3)]
        hvar = [sb(f"hvar{n}", [P, HEADS]) for n in range(3)]
        hve = [sb(f"hve{n}", [P, HEADS]) for n in range(3)]
        hrs = [sb(f"hrs{n}", [P, HEADS]) for n in range(3)]

        wait_pad = sb("wait_pad", [P, PADS])
        eps_row = sb("eps_row", [P, 3])
        eps_head = sb("eps_head", [P, 3, HEADS])
        one_col = sb("one_col", [P, 1])

        xn = sb("xn", [P, D])
        xth = sb("xth", [P, KC, L], F16)
        xtl = sb("xtl", [P, KC, L], F16)
        kg1 = sb("kg1", [DK, L])
        z = sb("z", [P, QK])
        zl = sb("zl", [P, QK])
        lsg = sb("lsg", [P, QK])
        G = sb("G", [P, QK])
        dq = sb("dq", [P, QK])
        eq = sb("eq", [P, QK])
        dk = sb("dk", [P, 2, KTN])
        qeo = [sb(f"qeo{i}", [P, 2 * NBLK, 2, BLK]) for i in range(2)]
        kt = [sb(f"kt{i}", [P, 2, KTN]) for i in range(2)]
        v = [sb(f"v{i}", [P, D]) for i in range(2)]
        gf = sb("gf", [P, D])
        ge = sb("ge", [P, D])
        gate = [sb(f"gate{i}", [P, D]) for i in range(2)]

        scm = sb("scm", [P, 4 * 2 * NBLK * 2 * BLK])
        oT = sb("oT", [P, KC, L])
        od = sb("od", [P, D])
        osq = sb("osq", [P, D])
        oth = sb("oth", [P, KC, L], F16)
        otl = sb("otl", [P, KC, L], F16)

        ctx32 = [sb(f"ctx32_{i}", [P, CC, KEYS]) for i in range(2)]
        cth = sb("cth", [P, CC, KEYS], F16)
        ctl = sb("ctl", [P, CC, KEYS], F16)
        kraw = sb("kraw", [P, D])
        vx = [sb(f"vx{i}", [P, D]) for i in range(2)]
        ksq = sb("ksq", [P, D])
        kT = sb("kT", [P, KC, L])
        xn2 = sb("xn2", [P, D])
        x2h = sb("x2h", [P, KC, L], F16)
        x2l = sb("x2l", [P, KC, L], F16)
        qraw = sb("qraw", [P, D])
        qsq = sb("qsq", [P, D])
        qT = sb("qT", [P, KC, L])
        mx = sb("mx", [P, 2, HEADS])
        sm = sb("sm", [P, 2, HEADS])
        rc = sb("rc", [P, 2, HEADS])
        pr = [sb(f"pr{i}", [P, HEADS * L]) for i in range(2)]
        pT = [sb(f"pT{i}", [P, KC, L]) for i in range(2)]
        ch = sb("ch", [P, KC, L], F16)
        cl = sb("cl", [P, KC, L], F16)
        xn3 = sb("xn3", [P, D])
        x3T = sb("x3T", [P, KC, L])
        lgT = sb("lgT", [P, L])

        NSTAGE = 5
        stage_buf = [pr[0][:, :], pr[1][:, :]] + [x_all[:, 4 * n * D:4 * (n + 1) * D] for n in range(1, 4)]

        def flat(t):
            return t[:, :, :].rearrange("p k n -> p (k n)")
        dca_w = [[flat(pT[0]).bitcast(F16), flat(pT[1]).bitcast(F16)], [xn3[:, :].bitcast(F16), flat(x3T).bitcast(F16)]]
        dca32 = flat(qT).rearrange("p (k n) -> p k n", k=CC)
        dca_h = flat(ch).rearrange("p (k n) -> p k n", k=CC)
        dca_l = flat(cl).rearrange("p (k n) -> p k n", k=CC)
        dca_o = [qraw[:, :], qsq[:, :], flat(kT), vx[1][:, :]]
        at.close()

        ff = ExitStack()

        def fb(name, shape, dt=F32):
            return ff.enter_context(nc.sbuf_tensor(name, shape, dt))

        tri4 = fb("tri4", [P, E, E])
        cmp_gt = fb("cmp_gt", [P, B, E, E])
        cmp_eq = fb("cmp_eq", [P, B, E, E])
        rank = fb("rank", [P, B, E])
        oh = [fb(f"oh{k}", [P, B, E]) for k in range(2)]
        taken = fb("taken", [P, B, E])
        upto = fb("upto", [P, B, E])
        by_id = [fb(f"by_id{k}", [P, B, E]) for k in range(2)]
        neg_one = fb("neg_one", [P, B])
        nmr = fb("nmr", [P, B])
        w_raw = fb("w_raw", [P, 2, B])
        ohl = fb("ohl", [P, B, E])
        l1 = fb("l1", [P, B])
        l2 = fb("l2", [P, B])
        ldiff = fb("ldiff", [P, B])
        ed = fb("ed", [P, B])
        den = fb("den", [P, B])
        p12 = fb("p12", [P, 2, B])
        score = fb("score", [P, B, E])
        sc2 = fb("sc2", [P, B, E])
        big = [fb(f"big{i}", [P, N]) for i in range(4)]
        digit = fb("digit", [P, 1], I32)
        pid = fb("pid", [P, 1], I32)
        eid = fb("eid", [P, 1], I32)
        cands = fb("cands", [P, len(SHIFTS)], I32)
        cand = fb("cand", [P, 1], I32)
        thr = fb("thr", [P, 1], I32)
        count = fb("count", [P, 1])
        enough = fb("enough", [P, 1])
        same_e = fb("same_e", [P, E, P // E])
        ones = fb("ones", [P, 1])
        ties = fb("ties", [P, 1])
        slot0 = fb("slot0", [P, 1])
        posT = fb("posT", [P, B, E])
        sel_k = fb("sel_k", [P, B, E])
        idx = fb("idx", [P, 2, B])
        idx_put = fb("idx_put", [P, 2, B], I32)
        idx_get = fb("idx_get", [P, 2, B], I32)
        wk = fb("wk", [P, 2, B])
        xn_all = fb("xn_all", [P, B * D])
        zero = fb("zero", [P, D])
        NST = 2
        wst = [fb(f"wst{i}", [P, 2048]) for i in range(NST)]
        HALF = HID // 2
        w1h = [fb(f"w1h{i}", [P, KC, HALF], F16) for i in range(2)]
        w1l = [fb(f"w1l{i}", [P, KC, HALF], F16) for i in range(2)]
        FH = HALF // P
        w2h = [fb(f"w2h{i}", [P, FH, D], F16) for i in range(2)]
        w2l = [fb(f"w2l{i}", [P, FH, D], F16) for i in range(2)]
        xg32 = big[0][:, :].rearrange("p (t n) -> p t n", t=4)
        y_sb = big[1][:, :].rearrange("p (t n) -> p t n", t=4)
        xgh = big[2][:, :].bitcast(F16)[:, 0:2048].rearrange("p (k n) -> p k n", k=KC)
        xgl = big[2][:, :].bitcast(F16)[:, 2048:4096].rearrange("p (k n) -> p k n", k=KC)
        hg = [big[3][:, i * D:(i + 1) * D] for i in range(2)]
        h16 = big[3][:, 2 * D:4 * D].bitcast(F16)
        hh = [h16[:, i * D:(i + 1) * D] for i in range(2)]
        hl = [h16[:, (2 + i) * D:(3 + i) * D] for i in range(2)]
        GET_ROWS = ((E - 1) * CAP, E * CAP)
        NG = 4
        yg = [xn_all[:, b * D:(b + 1) * D] for b in range(B)]
        ff.close()

        psum = [ctx.enter_context(nc.psum_tensor(f"ps{i}", [P, 1024], F32)) for i in range(4)]
        a0, a1 = psum[0][:, 0:512], psum[0][:, 512:1024]
        b0, b1 = psum[1][:, 0:512], psum[1][:, 512:1024]
        c0, c1 = psum[2][:, 0:512], psum[2][:, 512:1024]
        d0, d1 = psum[3][:, 0:512], psum[3][:, 512:1024]

        x_in = sems("x_in", 4)
        consts_a1_in, consts_b_in = sem("consts_a1_in"), sem("consts_b_in")
        stage_in = sems("stage_in", NSTAGE)
        cent, stage_hi, stage_lo = map(sem, ("cent", "stage_hi", "stage_lo"))
        dca_in, dca_split, dca_ps, dca_out, dca_stored = map(sem, (
            "dca_in", "dca_split", "dca_ps", "dca_out", "dca_stored"))
        pool_const, dve_const = sem("pool_const"), sem("dve_const")
        ctx_in = sems("ctx_in", 2)
        kdca_in, vdca_in = sem("kdca_in"), sems("vdca_in", 2)

        stat, dev = sems("stat", 3), sems("dev", 3)
        hq, hv, hdev = (sems(n, 3) for n in ("hq", "hv", "hdev"))

        xn_r, xt_ps, xth_r, xtl_r = map(sem, ("xn_r", "xt_ps", "xth_r", "xtl_r"))
        kg1_ps, qk_ps, kg2_ps, v_ps, g_ps = map(sem, ("kg1_ps", "qk_ps", "kg2_ps", "v_ps", "g_ps"))
        kg1_r, z_r, lsig, sums, dk_r, eq_r, dke_r, qk_r = map(sem, (
            "kg1_r", "z_r", "lsig", "sums", "dk_r", "eq_r", "dke_r", "qk_r"))
        v_r, gf_r, ge_r, gp_r, gr_r, gate_r = map(sem, ("v_r", "gf_r", "ge_r", "gp_r", "gr_r", "gate_r"))
        sc_ps, scm_r = sem("sc_ps"), sem("scm_r")
        oT_ps, oT_r, o_ps, on_r, og_r, ot_ps, oth_r, otl_r, wo_ps, x1_r = map(sem, (
            "oT_ps", "oT_r", "o_ps", "on_r", "og_r", "ot_ps", "oth_r", "otl_r", "wo_ps", "x1_r"))
        cth_r, ctl_r, kv_ps, kv_ev, kb_r, vb_r = map(sem, ("cth_r", "ctl_r", "kv_ps", "kv_ev", "kb_r", "vb_r"))
        kn_r, kT_ps, kT_r = map(sem, ("kn_r", "kT_ps", "kT_r"))
        xn2_r, x2_ps, x2h_r, x2l_r, q_ps, q_r = map(sem, ("xn2_r", "x2_ps", "x2h_r", "x2l_r", "q_ps", "q_r"))
        qn_r, qT_ps, qT_r = map(sem, ("qn_r", "qT_ps", "qT_r"))
        xs_ps, shift = sem("xs_ps"), sem("shift")
        exp_r, norm, pr_r = (sems(n, 2) for n in ("exp_r", "norm", "pr_r"))
        pT_ps, pT_r, pv_ps = map(sem, ("pT_ps", "pT_r", "pv_ps"))
        xbo_r, ch_r, cl_r, xo_ps, x2_r = map(sem, ("xbo_r", "ch_r", "cl_r", "xo_ps", "x2_r"))
        xn3_r, x3_ps, x3T_r, lg_ps, lgT_r, lgt_ps, lg_r, mean3_r = map(sem, (
            "xn3_r", "x3_ps", "x3T_r", "lg_ps", "lgT_r", "lgt_ps", "lg_r", "mean3_r"))

        route, route_const, rep_r, scT_ps, route_act, cnt_r, dig_ps, pos_r, posT_ps = map(sem, (
            "route", "route_const", "rep_r", "scT_ps", "route_act", "cnt_r", "dig_ps", "pos_r",
            "posT_ps"))
        idx_r, xnall_r, zero_r, zero_st = map(sem, ("idx_r", "xnall_r", "zero_r", "zero_st"))
        put_done = sems("put_done", 2)
        w_in = sems("w_in", NST)
        w_hi, w_lo, xg_in = sem("w_hi"), sem("w_lo"), sem("xg_in")
        half_used = sems("half_used", 2)
        xgT_ps, xgh_r, xgl_r = sem("xgT_ps"), sem("xgh_r"), sem("xgl_r")
        h_ps, hg_r, hh_r, hl_r, h_used = map(sem, ("h_ps", "hg_r", "hh_r", "hl_r", "h_used"))
        y_ev, y_st = sem("y_ev"), sem("y_st")
        lo_in, hi_in, comb, out_st = sem("lo_in"), sems("hi_in", NG), sem("comb"), sem("out_st")

        def heads(ap):
            return ap.rearrange("p (h c) -> p h c", c=DV)

        def per_head(ap):
            return ap.unsqueeze(2).to_broadcast([P, HEADS, DV])

        def over_heads(ap):
            return ap.unsqueeze(1).to_broadcast([P, HEADS, DV])

        LAGS = 4

        def after(eng, signal, b, nth=1, per=1, ago=0):
            if not isinstance(b, int) or b >= ago:
                eng.wait_ge(signal, per * (b - ago) + nth)

        def first(b, n):
            return isinstance(b, int) and b == n

        def on(stage, step, *args):
            if stage:
                step(stage, *args)

        def pipeline(eng, body, first={}):
            def fixed(t):
                return [(t - k, (t - k) % 2, (t - k) // 2) if 0 <= t - k < B else None for k in range(LAGS)]
            for t in range(LAGS):
                if t in first:
                    first[t]()
                body(fixed(t))
            with eng.Fori(LAGS // 2, B // 2) as j:
                for u in range(2):
                    body([(2 * j + (u - k), (u - k) % 2, j + (u - k) // 2) for k in range(LAGS)])
            for t in range(B, B + LAGS - 1):
                body(fixed(t))

        def seq(b):
            return bass.ds(b * D, D)

        block = ctx.enter_context(nc.Block())

        def w_piece_of(c):
            return (w_attn[:, c:c + D].rearrange("(k p) n -> p k n", p=P), wh[:, :, c:c + D], wl[:, :, c:c + D], KC)
        pieces = [w_piece_of(c) for c in (C_QK, C_V, C_G, C_O)]
        pieces.append((w_ctx[:, 2 * D:4 * D].rearrange("(k p) n -> p k n", p=P), None, None, CC))
        pieces.append((w_ctx[:, 0:2 * D].rearrange("(k p) n -> p k n", p=P), wch[:, :, :], wcl[:, :, :], CC))
        pieces += [w_piece_of(c) for c in (C_XQ, C_XO)]
        CENTRED = (1, 4, 5, 6)
        CENT0 = [sum(pieces[n][3] for n in CENTRED[:m]) for m in range(len(CENTRED) + 1)]
        KG_STAGE = xn3[:, 0:KC * DK].rearrange("p (k n) -> p k n", k=KC)

        def staged(n):
            return stage_buf[n % NSTAGE].rearrange("p (k n) -> p k n", k=pieces[n][3])

        def split_parts(n):
            _, hi, lo, k = pieces[n]
            if hi is None:
                return [(staged(n)[:, i, :], dca_w[0][i], dca_w[1][i]) for i in range(k)]
            return [(staged(n), hi, lo)]

        consts_a1 = [(KG_STAGE, w_attn[:, C_KG:C_KG + DK].rearrange("(k p) n -> p k n", p=P)), (wkg2_sb[:, :], w_kg2), (bkg2_sb[:, :], b_kg2), (bg_sb[:, :], b_g.partition_broadcast(P))]
        consts_b = [(bq_sb[:, :], b_q.partition_broadcast(P)), (bo_sb[:, :], b_o.partition_broadcast(P)),
                    (bkv_sb[0:KEYS, :], b_kv.partition_broadcast(KEYS)), (bkv_sb[KEYS:P, :], b_dca.partition_broadcast(NDCA)),
                    (head_cols[:, :], cols_n), (wgate_sb[:, :, :], w_gate.rearrange("(k p) e -> p k e", p=P)),
                    (bgate_sb[:, :], b_gate.partition_broadcast(P))]
        XPARTS = [(0, 1), (1, 2), (2, 4), (4, B)]

        def x_loaded(b):
            return [n for n, (lo, hi) in enumerate(XPARTS) if lo == b]

        def w_piece(e, n):
            hf, k = n // 4, n % 4
            if k < 2:
                src = w1[bass.ds(e, 1), k * 256:(k + 1) * 256, hf * HALF:(hf + 1) * HALF].rearrange("o (k p) n -> p (o k) n", p=P)
                return src, w1h[hf][:, 2 * k:2 * k + 2, :], w1l[hf][:, 2 * k:2 * k + 2, :], 2
            k -= 2
            lo = hf * HALF + k * 512
            src = w2[bass.ds(e, 1), lo:lo + 512, :].rearrange("o (f p) d -> p (o f) d", p=P)
            return src, w2h[hf][:, 4 * k:4 * k + 4, :], w2l[hf][:, 4 * k:4 * k + 4, :], 4
        W_PIECES = 8

        @block.sync
        def _(sp):
            sp.dma_start(x_all[:, 0:D], x[0]).then_inc(x_in[0], 16)

            def weights(n):
                if n >= NSTAGE:
                    sp.wait_ge(stage_lo, n - NSTAGE + 2)
                sp.dma_start(staged(n), pieces[n][0]).then_inc(stage_in[n % NSTAGE], 16)

            def load_x(n):
                lo, hi = XPARTS[n]
                sp.dma_start(x_all[:, lo * D:hi * D].rearrange("p (b d) -> p b d", d=D),
                             x[lo:hi].rearrange("b p d -> p b d")).then_inc(x_in[n], 16)

            def load_ctx(b, par):
                sp.dma_start(ctx32[par][:, :, :], ctx_t[bass.ds(b, 1)].rearrange("o (k p) n -> p (o k) n", p=P))\
                  .then_inc(ctx_in[par], 16)

            for dst, src in consts_a1:
                sp.dma_start(dst, src).then_inc(consts_a1_in, 16)
            for n in range(3):
                weights(n)
            load_x(1)
            weights(3)
            load_ctx(0, 0)
            weights(4)
            sp.dma_start(dca32, dca_t.rearrange("(k p) n -> p k n", p=P)).then_inc(dca_in, 16)
            load_x(2)
            for dst, src in consts_b:
                sp.dma_start(dst, src).then_inc(consts_b_in, 16)
            for n in range(NSTAGE, len(pieces)):
                weights(n)
            for t in range(4):
                sp.wait_ge(dca_out, t + 1)
                sp.dma_start(dca_dram[(t // 2) * P:(t // 2 + 1) * P, (t % 2) * D:(t % 2 + 1) * D],
                             dca_o[t]).then_inc(dca_stored, 16)
            sp.wait_ge(dca_stored, 64)

            def k_dca(s):
                b, par, half = s
                after(sp, kT_ps, b, ago=1)
                sp.dma_start(kraw[KEYS:P, :], dca_dram[bass.ds(b * NDCA, NDCA), 0:D]).then_inc(kdca_in, 16)

            def v_dca(s):
                b, par, half = s
                after(sp, pv_ps, b, nth=4, per=4, ago=2)
                sp.dma_start(vx[par][KEYS:P, :], dca_dram[bass.ds(b * NDCA, NDCA), D:2 * D]).then_inc(vdca_in[par], 16)

            def context(s):
                b, par, half = s
                if not isinstance(b, int) or b >= 1:
                    after(sp, ctl_r, b, ago=2)
                    load_ctx(b, par)

            def body(s):
                on(s[2], v_dca)
                on(s[1], context)
                on(s[1], k_dca)
            def last_x():
                sp.wait_ge(stage_lo, len(pieces) + 1)
                load_x(3)

            pipeline(sp, body, {2: last_x})

            sp.wait_ge(lg_r, B)
            def load_piece(e, n):
                src, _, _, k = w_piece(e, n)
                sp.dma_start(wst[n % NST][:, :].rearrange("p (k n) -> p k n", k=k), src).then_inc(w_in[n % NST], 16)

            def load_pieces(e, ns):
                for n in ns:
                    if not (isinstance(e, int) and e == 0 and n < NST):
                        sp.wait_ge(w_lo, e * W_PIECES + (n + 1 - NST))
                    load_piece(e, n)

            def load_tokens(e):
                sp.dma_start(xg32, xg_dram[bass.ds(e * CAP, CAP), :].rearrange("(t p) d -> p t d", p=P)).then_inc(xg_in, 16)

            def store_results(e):
                sp.wait_ge(y_ev, 4 * (e + 1))
                sp.dma_start(y_dram[bass.ds(e * CAP, CAP), :].rearrange("(t p) d -> p t d", p=P), y_sb).then_inc(y_st, 16)
            FIRST_HALF, SECOND_HALF = range(W_PIECES // 2), range(W_PIECES // 2, W_PIECES)

            load_pieces(0, FIRST_HALF[:NST])
            sp.wait_ge(zero_r, 1)
            for t in range(N // P):
                sp.dma_start(xg_dram[t * P:(t + 1) * P, :], zero[:, :]).then_inc(zero_st, 16)
            load_pieces(0, FIRST_HALF[NST:])
            sp.wait_ge(put_done[0], 16 * B)
            load_tokens(0)

            def next_expert(e):
                sp.wait_ge(xgT_ps, 4 * (e + 1))
                load_tokens(e + 1)
                load_pieces(e, SECOND_HALF)
                load_pieces(e + 1, FIRST_HALF)
                store_results(e)
            load_pieces(0, SECOND_HALF[:1])
            sp.wait_ge(put_done[1], 16 * B)
            sp.wait_ge(xgT_ps, 4)
            load_tokens(1)
            load_pieces(0, SECOND_HALF[1:])
            load_pieces(1, FIRST_HALF)
            store_results(0)
            with sp.Fori(1, E - 1) as e:
                next_expert(e)
            load_pieces(E - 1, SECOND_HALF)
            store_results(E - 1)
            for g in range(NG):
                n = B // NG
                sp.wait_ge(comb, B + n * (g + 1))
                sp.dma_start(out_rows[g * n * L:(g + 1) * n * L, :].rearrange("(b p) d -> p b d", p=P),
                             x_all[:, g * n * D:(g + 1) * n * D].rearrange("p (b d) -> p b d", d=D)).then_inc(out_st, 16)
            sp.wait_ge(out_st, 16 * NG)

        @block.gpsimd
        def _(pool):
            pool.memset(ident[:, :], 0.0).then_inc(pool_const, 1)
            pool.memset(causal[:, :, :], 1.0).then_inc(pool_const, 1)
            pool.memset(neg_half[:, :], -0.5).then_inc(pool_const, 1)
            for n in range(3):
                pool.memset(eps_row[:, n:n + 1], EPS_ROW)
                pool.memset(eps_head[:, n, :], DV * EPS_HEAD[n])
            pool.memset(one_col[:, :], 1.0)
            pool.iota(row_id[:, :], [[0, 1]], base=0, channel_multiplier=1).then_inc(pool_const, 1)
            pool.wait_ge(pool_const, 4)
            pool.affine_select(out=ident[:, :], in_=ident[:, :], compare_op=ALU.not_equal, fill=1.0, base=0,
                               pattern=[[-1, P]], channel_multiplier=1).then_inc(pool_const, 1)
            cz = causal[:, :, :].rearrange("p i (e t) -> p i e t", e=2)
            pool.affine_select(out=cz, in_=cz, compare_op=ALU.is_ge, fill=0.0, base=0,
                               pattern=[[BLK, NBLK], [0, 2], [1, BLK]], channel_multiplier=-1).then_inc(pool_const, 1)

            def deviation(s, n):
                b, par, half = s
                after(pool, stat[n], b, nth=2, per=2)
                pool.tensor_tensor(vare[n][:, :], aggr[n][:, 1:2], eps_row[:, n:n + 1], ALU.add).then_inc(dev[n], 1)
                after(pool, dev[n], b, nth=1, per=2)
                pool.tensor_tensor(rstd[n][:, :], vare[n][:, :], neg_half[:, 0:1], ALU.pow).then_inc(dev[n], 1)

            def head_deviation(s, n):
                b, par, half = s
                after(pool, hv[n], b)
                pool.tensor_tensor(hve[n][:, :], hvar[n][:, :], eps_head[:, n, :], ALU.add).then_inc(hdev[n], 1)
                after(pool, hdev[n], b, nth=1, per=2)
                pool.tensor_tensor(hrs[n][:, :], hve[n][:, :], neg_half[:, :], ALU.pow).then_inc(hdev[n], 1)

            def k_decay(s):
                b, par, half = s
                after(pool, sums, b, nth=2, per=3)
                G3 = G[:, :].rearrange("p (c t) -> p c t", c=2)
                for i in range(NBLK):
                    m = BLK * i + BLK // 2 - 1
                    last = pool.tensor_tensor(dk[:, :, KTO[i]:KTO[i] + KTW[i]],
                                              G3[:, :, m:m + 1].to_broadcast([P, 2, KTW[i]]),
                                              G3[:, :, 0:KTW[i]], ALU.subtract)
                last.then_inc(dk_r, 1)

            def gate_one(s):
                after(pool, ge_r, s[0])
                pool.tensor_tensor(ge[:, :], ge[:, :], one_col[:, :].to_broadcast([P, D]), ALU.add).then_inc(gp_r, 1)

            def gate_silu(s):
                b, par, half = s
                after(pool, gr_r, b)
                pool.tensor_tensor(gate[par][:, :], gf[:, :], ge[:, :], ALU.mult).then_inc(gate_r, 1)

            def gated(s):
                b, par, half = s
                after(pool, on_r, b)
                after(pool, gate_r, b)
                pool.tensor_tensor(od[:, :], od[:, :], gate[par][:, :], ALU.mult).then_inc(og_r, 1)

            def k_bias(s):
                b, par, half = s
                after(pool, kv_ev, b, nth=1, per=2)
                after(pool, kdca_in, b, nth=16, per=16)
                pool.tensor_tensor(kraw[:, :], kraw[:, :], bkv_sb[:, 0:D], ALU.add).then_inc(kb_r, 1)

            def v_bias(s):
                b, par, half = s
                after(pool, kv_ev, b, nth=2, per=2)
                after(pool, vdca_in[par], half, nth=16, per=16)
                pool.tensor_tensor(vx[par][:, :], vx[par][:, :], bkv_sb[:, D:2 * D], ALU.add).then_inc(vb_r, 1)

            def out_bias(s):
                b, par, half = s
                after(pool, xn2_r, b)
                pool.tensor_tensor(x_all[:, seq(b)], x_all[:, seq(b)], bo_sb[:, :], ALU.add).then_inc(xbo_r, 1)

            def probs(s, rnd):
                b, par, half = s
                after(pool, norm[rnd], b, nth=2, per=2)
                p3 = pr[par][:, rnd * 1024:(rnd + 1) * 1024].rearrange("p (h k) -> p h k", k=L)
                rr = rc[:, :, rnd * 8:(rnd + 1) * 8]
                pool.tensor_tensor(p3[:, :, 0:KEYS], p3[:, :, 0:KEYS],
                                   rr[:, 0].unsqueeze(2).to_broadcast([P, 8, KEYS]), ALU.mult)
                pool.tensor_tensor(p3[:, :, KEYS:L], p3[:, :, KEYS:L],
                                   rr[:, 1].unsqueeze(2).to_broadcast([P, 8, NDCA]), ALU.mult).then_inc(pr_r[rnd], 1)

            def keep_norm(s):
                b, par, half = s
                deviation(s, 2)
                pool.tensor_copy(mr_all[:, bass.ds(2 * b, 1)], aggr[2][:, 0:1])
                after(pool, dev[2], b, nth=2, per=2)
                pool.tensor_copy(mr_all[:, bass.ds(2 * b + 1, 1)], rstd[2][:, :]).then_inc(mean3_r, 1)

            def body(s):
                on(s[3], v_bias)
                on(s[3], probs, 0)
                on(s[0], deviation, 0)
                on(s[2], k_bias)
                on(s[3], probs, 1)
                on(s[2], head_deviation, 1)
                on(s[1], gate_one)
                on(s[2], head_deviation, 2)
                on(s[1], head_deviation, 0)
                on(s[1], gate_silu)
                on(s[1], gated)
                on(s[3], keep_norm)
                on(s[2], out_bias)
                on(s[0], k_decay)
                on(s[1], deviation, 1)
            pipeline(pool, body, {2: lambda: pool.wait_ge(dve_const, 9)})

            pool.wait_ge(lg_r, B)
            pool.wait_ge(mean3_r, B)
            pool.memset(zero[:, :], 0.0).then_inc(zero_r, 1)
            pool.memset(tri4[:, :, :], 1.0).then_inc(route_const, 1)
            pool.memset(same_e[:, :, :], 1.0).then_inc(route_const, 1)
            pool.memset(ones[:, :], 1.0).then_inc(route_const, 1)
            pool.iota(pid[:, :], [[0, 1]], base=0, channel_multiplier=1).then_inc(route_const, 1)
            pool.memset(neg_one[:, :], -1.0)
            pool.wait_ge(route_const, 4)
            pool.affine_select(out=tri4[:, :, :], in_=tri4[:, :, :], compare_op=ALU.is_gt, fill=0.0, base=0,
                               pattern=[[1, E], [-1, E]], channel_multiplier=0).then_inc(route_const, 1)
            pool.affine_select(out=same_e[:, :, :], in_=same_e[:, :, :], compare_op=ALU.is_ge, fill=0.0, base=0,
                               pattern=[[-(P // E), E], [0, P // E]], channel_multiplier=1).then_inc(route_const, 1)
            pool.wait_ge(route_const, 6)
            pool.affine_select(out=same_e[:, :, :], in_=same_e[:, :, :], compare_op=ALU.is_gt, fill=0.0, base=P // E,
                               pattern=[[P // E, E], [0, P // E]], channel_multiplier=-1).then_inc(route_const, 1)
            mr = mr_all[:, :].rearrange("p (b n) -> p n b", n=2)
            pool.tensor_tensor(nmr[:, :], mr[:, 0, :], mr[:, 1, :], ALU.mult).then_inc(route_const, 1)
            pool.wait_ge(route_const, 8)
            pool.tensor_tensor(nmr[:, :], nmr[:, :], neg_one[:, :], ALU.mult).then_inc(route_const, 1)
            pool.wait_ge(xnall_r, 1)
            pool.wait_ge(zero_st, 16 * (N // P))
            pool.wait_ge(idx_r, 1)
            for k in range(2):
                for b in range(B):
                    pool.indirect_dma_start(out=xg_dram, out_offset=bass.IndirectOffsetOnAxis(ap=idx_put[:, k, b:b + 1], axis=0),
                                            in_=xn_all[:, b * D:(b + 1) * D], in_offset=None,
                                            bounds_check=N - 1, oob_is_err=False).then_inc(put_done[k], 16)

            def fetch(k, b, done):
                pool.indirect_dma_start(out=yg[b], out_offset=None, in_=y_dram[0:GET_ROWS[k], :],
                                        in_offset=bass.IndirectOffsetOnAxis(ap=idx_get[:, k, b:b + 1], axis=0),
                                        bounds_check=GET_ROWS[k] - 1, oob_is_err=False).then_inc(done, 16)
            for k in range(2):
                pool.wait_ge(put_done[k], 16 * B)
            pool.wait_ge(y_st, 16 * (E - 1))
            for b in range(B):
                fetch(0, b, lo_in)
            pool.wait_ge(y_st, 16 * E)
            pool.wait_ge(comb, B)
            for b in range(B):
                fetch(1, b, hi_in[b // (B // NG)])

        @block.scalar
        def _(act):
            def split_hi(n):
                act.wait_ge(stage_in[n % NSTAGE], 16 * (n // NSTAGE + 1))
                if n in CENTRED:
                    act.wait_ge(cent, 2 * CENT0[CENTRED.index(n) + 1])
                for src, hi, lo in split_parts(n):
                    last = act.activation(hi, src, ACT.Copy, scale=WS)
                last.then_inc(stage_hi, 1)

            def weights_attention():
                act.wait_ge(consts_a1_in, 16 * len(consts_a1))
                act.activation(wh[:, :, C_KG:C_KG + DK], KG_STAGE, ACT.Copy, scale=WS).then_inc(stage_hi, 1)
                split_hi(0)

            def second_hi():
                act.wait_ge(dca_in, 16)
                act.activation(dca_h, dca32, ACT.Copy, scale=XS).then_inc(dca_split, 1)
                split_hi(4)

            def second_out():
                for t in range(4):
                    act.wait_ge(dca_ps, t + 1)
                    act.activation(dca_o[t], psum[2 + t // 2][:, (t % 2) * 512:(t % 2 + 1) * 512], ACT.Copy, scale=UN).then_inc(dca_out, 1)

            def square(dst, src, ready, value_of, done):
                after(act, ready, value_of)
                act.activation(dst, src, ACT.Square).then_inc(done, 1)

            def take(dst, ps, scale, done):
                act.activation(dst, ps, ACT.Copy, scale=scale).then_inc(done, 1)

            def cols(ps):
                return ps.rearrange("p (k n) -> p k n", k=KC)

            def x_hi(s):
                after(act, xt_ps, s[0])
                take(xth[:, :, :], cols(a0), XS, xth_r)

            def kg1_out(s):
                after(act, kg1_ps, s[0])
                take(kg1[:, :], a1[0:DK, 0:L], UN, kg1_r)
                if first(s[0], 0):
                    split_hi(1)
                if first(s[0], 1):
                    second_hi()

            def log_sigmoid(s):
                b, par, half = s
                after(act, z_r, b)
                act.activation(zl[:, :], z[:, :], ACT.Abs).then_inc(lsig, 1)
                after(act, lsig, b, nth=1, per=3)
                act.activation(zl[:, :], zl[:, :], ACT.Exp, scale=-1.0).then_inc(lsig, 1)
                after(act, lsig, b, nth=2, per=3)
                act.activation(zl[:, :], zl[:, :], ACT.Ln, bias=1.0).then_inc(lsig, 1)
                if first(b, 0):
                    split_hi(2)
                if first(b, 1):
                    second_out()

            def q_decay(s):
                after(act, sums, s[0], nth=3, per=3)
                act.activation(eq[:, :], dq[:, :], ACT.Exp, scale=1.0 / NORM).then_inc(eq_r, 1)

            def k_decay(s):
                after(act, dk_r, s[0])
                act.activation(dk[:, :, :], dk[:, :, :], ACT.Exp, scale=1.0 / NORM).then_inc(dke_r, 1)
                if first(s[0], 0):
                    split_hi(3)
                if first(s[0], 1):
                    split_hi(6)
                    split_hi(7)

            def v_out(s):
                b, par, half = s
                after(act, v_ps, b)
                take(v[par][:, :], a1, UN, v_r)

            def gate_exp(s):
                after(act, gf_r, s[0])
                act.activation(ge[:, :], gf[:, :], ACT.Exp, scale=-1.0).then_inc(ge_r, 1)

            def o_out(s):
                after(act, oT_ps, s[0])
                take(oT[:, :, :], cols(b0), 1.0, oT_r)

            def o_square(s):
                square(osq[:, :], b1, o_ps, s[0], hq[0])

            def o_hi(s):
                after(act, ot_ps, s[0])
                take(oth[:, :, :], cols(b0), XS, oth_r)
                if first(s[0], 0):
                    split_hi(5)

            def ctx_hi(s):
                b, par, half = s
                after(act, ctx_in[par], half, nth=16, per=16)
                after(act, kv_ps, b, nth=2, per=2, ago=1)
                act.activation(cth[:, :, :], ctx32[par][:, :, :], ACT.Copy, scale=XS).then_inc(cth_r, 1)

            def kv_out(s):
                b, par, half = s
                after(act, kv_ps, b, nth=1, per=2)
                take(kraw[0:KEYS, :], c0[0:KEYS], UN, kv_ev)
                after(act, kv_ps, b, nth=2, per=2)
                take(vx[par][0:KEYS, :], c1[0:KEYS], UN, kv_ev)

            def k_square(s):
                square(ksq[:, :], kraw[:, :], kb_r, s[0], hq[1])

            def k_out(s):
                after(act, kT_ps, s[0])
                act.activation(kT[:, :, 0:KEYS], cols(c0)[:, :, 0:KEYS], ACT.Identity, scale=head_cols[:, 2:3], bias=head_cols[:, 3:4])
                act.activation(kT[:, :, KEYS:L], cols(c0)[:, :, KEYS:L], ACT.Identity, scale=head_cols[:, 4:5], bias=head_cols[:, 5:6]).then_inc(kT_r, 1)

            def x2_hi(s):
                after(act, x2_ps, s[0])
                take(x2h[:, :, :], cols(c0), XS, x2h_r)

            def q_square(s):
                square(qsq[:, :], qraw[:, :], q_r, s[0], hq[2])

            def q_out(s):
                after(act, qT_ps, s[0])
                act.activation(qT[:, :, :], cols(c0), ACT.Identity, scale=head_cols[:, 0:1], bias=head_cols[:, 1:2]).then_inc(qT_r, 1)

            def exponents(s, rnd):
                b, par, half = s
                after(act, shift, b, nth=2 * rnd + 2, per=4)
                half_p = pr[par][:, rnd * 1024:(rnd + 1) * 1024]
                act.activation(half_p, half_p, ACT.Exp, scale=XSCALE).then_inc(exp_r[rnd], 1)

            def p_out(s, r):
                after(act, pT_ps, s[0], nth=r + 1, per=4)
                take(pT[r % 2][:, :, :], cols(d0), 1.0, pT_r)

            def c_hi(s):
                after(act, pv_ps, s[0], nth=4, per=4)
                take(ch[:, :, :], cols(d1), XS, ch_r)

            def x3_out(s):
                after(act, x3_ps, s[0])
                take(x3T[:, :, :], cols(d1), 1.0, x3T_r)

            def logits_out(s):
                after(act, lg_ps, s[0])
                take(lgT[0:E, :], d0[0:E, 0:L], 1.0, lgT_r)

            def body(s):
                on(s[2], kv_out)
                on(s[3], p_out, 0)
                on(s[2], x2_hi)
                on(s[0], x_hi)
                on(s[2], k_square)
                on(s[3], p_out, 1)
                on(s[1], gate_exp)
                on(s[3], p_out, 2)
                on(s[2], q_square)
                on(s[1], o_out)
                on(s[3], p_out, 3)
                on(s[0], kg1_out)
                on(s[1], o_square)
                on(s[3], c_hi)
                on(s[1], ctx_hi)
                on(s[2], k_out)
                on(s[0], log_sigmoid)
                on(s[2], q_out)
                on(s[1], o_hi)
                on(s[3], x3_out)
                on(s[0], q_decay)
                on(s[0], v_out)
                on(s[0], k_decay)
                on(s[3], logits_out)
                on(s[2], exponents, 0)
                on(s[2], exponents, 1)
            nc.scalar.preload_act_table_set("natural_log_exp_and_others")
            pipeline(act, body, {0: weights_attention})

            act.wait_ge(route, ROUTE_DIFF)
            act.activation(ed[:, :], ldiff[:, :], ACT.Exp).then_inc(route_act, 1)
            for i in range(4):
                act.wait_ge(scT_ps, i + 1)
                act.activation(big[0][:, i * 512:(i + 1) * 512], psum[i // 2][:, (i % 2) * 512:(i % 2 + 1) * 512],
                               ACT.Copy).then_inc(route_act, 1)
            act.wait_ge(route_const, 9)
            for b in range(B):
                last = act.activation(xn_all[:, b * D:(b + 1) * D], x_all[:, b * D:(b + 1) * D], ACT.Identity,
                                      scale=mr_all[:, 2 * b + 1:2 * b + 2], bias=nmr[:, b:b + 1])
            last.then_inc(xnall_r, 1)

            def split_piece(e, n):
                _, dst, _, k = w_piece(e, n)
                act.wait_ge(w_in[n % NST], 16 * (e * (W_PIECES // NST) + n // NST + 1))
                act.activation(dst, wst[n % NST][:, :].rearrange("p (k n) -> p k n", k=k), ACT.Copy, scale=WS).then_inc(w_hi, 1)

            def tokens_hi(e):
                for t in range(4):
                    act.wait_ge(xgT_ps, 4 * e + (t + 1))
                    act.activation(xgh[:, :, t * P:(t + 1) * P], cols(psum[t % 2][:, 0:512]),
                                   ACT.Copy, scale=XS).then_inc(xgh_r, 1)

            def gelu(e, f):
                n = e * (2 * FH) + f
                act.wait_ge(h_ps, n + 1)
                if not (isinstance(e, int) and e == 0 and f < 2):
                    act.wait_ge(hl_r, n - 1)
                act.activation(hg[f % 2], psum[f % 2][:, 512:1024], ACT.Gelu, scale=UN).then_inc(hg_r, 1)

            def expert(e, more):
                for f in range(2 * FH):
                    gelu(e, f)
                    if f < FH and f % 2 == 0:
                        if not (isinstance(e, int) and e == 0):
                            act.wait_ge(half_used[1], e)
                        split_piece(e, W_PIECES // 2 + f // 2)
                    if more and f >= FH and f % 2 == 0:
                        act.wait_ge(half_used[0], e + 1)
                        split_piece(e + 1, (f - FH) // 2)
                if more:
                    tokens_hi(e + 1)

            for n in range(W_PIECES // 2):
                split_piece(0, n)
            tokens_hi(0)
            expert(0, True)
            with act.Fori(1, E - 1) as e:
                expert(e, True)
            expert(E - 1, False)

        @block.tensor
        def _(pe):
            def mm3(o, lh, ll, rh, rl, first, last):
                nc.tensor.matmul(o, lh, rh, start=first, stop=False)
                nc.tensor.matmul(o, lh, rl, start=False, stop=False)
                return nc.tensor.matmul(o, ll, rh, start=False, stop=last)

            def turn(ps, src, done):
                for c in range(KC):
                    last = nc.tensor.transpose(ps[:, c * P:(c + 1) * P], src[:, c * P:(c + 1) * P], ident[:, :])
                last.then_inc(done, 1)

            def rows(ps, xh, xl, col, done):
                for k in range(KC):
                    last = mm3(ps, xh[:, k, :], xl[:, k, :], wh[:, k, col:col + D], wl[:, k, col:col + D], k == 0, k == KC - 1)
                last.then_inc(done, 1)

            def second_kv():
                pe.wait_ge(stage_lo, 4 + 2)
                pe.wait_ge(dca_split, 2)
                for t in range(4):
                    ps = psum[2 + t // 2][:, (t % 2) * 512:(t % 2 + 1) * 512]
                    tok = slice((t // 2) * P, (t // 2 + 1) * P)
                    col = slice((t % 2) * D, (t % 2 + 1) * D)
                    for k in range(CC):
                        last = mm3(ps, dca_h[:, k, tok], dca_l[:, k, tok], dca_w[0][k][:, col], dca_w[1][k][:, col], k == 0, k == CC - 1)
                    last.then_inc(dca_ps, 1)

            def weights(b, n):
                if isinstance(b, int) and b == 0:
                    pe.wait_ge(stage_lo, n + 2)

            def a1_turn(s):
                b, par, half = s
                if isinstance(b, int) and b == 0:
                    pe.wait_ge(pool_const, 5)
                after(pe, xn_r, b)
                turn(a0, xn[:, :], xt_ps)

            def a1_kg1(s):
                b, par, half = s
                weights(b, -1)
                after(pe, xtl_r, b)
                for k in range(KC):
                    last = mm3(a1[0:DK, 0:L], wh[:, k, C_KG:C_KG + DK], wl[:, k, C_KG:C_KG + DK],
                               xth[:, k, :], xtl[:, k, :], k == 0, k == KC - 1)
                last.then_inc(kg1_ps, 1)

            def a1_qk(s):
                b, par, half = s
                weights(b, 0)
                after(pe, xtl_r, b)
                for g in range(4):
                    for k in range(KC):
                        c = C_QK + g * P
                        last = mm3(a0[:, g * L:(g + 1) * L], wh[:, k, c:c + P], wl[:, k, c:c + P],
                                   xth[:, k, :], xtl[:, k, :], k == 0, k == KC - 1)
                last.then_inc(qk_ps, 1)

            def a1_kg2(s):
                b, par, half = s
                if isinstance(b, int) and b == 0:
                    pe.wait_ge(consts_a1_in, 16 * len(consts_a1))
                after(pe, kg1_r, b)
                for c in range(2):
                    last = nc.tensor.matmul(a1[:, c * L:(c + 1) * L], wkg2_sb[:, c * P:(c + 1) * P], kg1[:, :], start=True, stop=True)
                last.then_inc(kg2_ps, 1)

            def a1_v(s):
                b, par, half = s
                weights(b, 1)
                after(pe, z_r, b)
                rows(a1, xth, xtl, C_V, v_ps)
                if first(b, 1):
                    second_kv()

            def a1_g(s):
                b, par, half = s
                weights(b, 2)
                after(pe, v_r, b)
                rows(a1, xth, xtl, C_G, g_ps)

            def a2_scores(s, rnd):
                b, par, half = s
                after(pe, qk_r, b)
                if rnd:
                    after(pe, scm_r, b, nth=1, per=2)
                for c in range(2):
                    for i in reversed(range(NBLK)):
                        for r in (2 * rnd, 2 * rnd + 1):
                            rw = slice(32 * r, 32 * r + 32)
                            col = (r % 2) * 512 + c * 256 + i * 2 * BLK
                            last = nc.tensor.matmul(psum[1][0:KTW[i], col:col + 2 * BLK], kt[par][rw, c, KTO[i]:KTO[i] + KTW[i]],
                                                    qeo[par][rw, c * NBLK + i, :, :].rearrange("p e t -> p (e t)"), start=True, stop=True)
                last.then_inc(sc_ps, 1)

            def a2_o(s):
                b, par, half = s
                after(pe, scm_r, b, nth=2, per=2)
                after(pe, v_r, b)
                sc = scm[:, :].rearrange("p (r c e t) -> p r c e t", r=4, c=2, e=2)
                for h in range(HEADS):
                    j, e = h // 2, h % 2
                    n, c = h % 4, h // 4
                    last = nc.tensor.matmul(b0[n * DV:(n + 1) * DV, c * L:(c + 1) * L], v[par][:, h * DV:(h + 1) * DV],
                                            sc[:, j % 4, j // 4, e, :], start=True, stop=True)
                last.then_inc(oT_ps, 1)

            def a2_o_turn(s):
                after(pe, oT_r, s[0])
                turn(b1, oT[:, :, :].rearrange("p k n -> p (k n)"), o_ps)

            def a2_turn(s):
                after(pe, og_r, s[0])
                turn(b0, od[:, :], ot_ps)

            def a2_wo(s):
                b, par, half = s
                weights(b, 3)
                after(pe, otl_r, b)
                rows(b1, oth, otl, C_O, wo_ps)

            def b1_kv(s):
                b, par, half = s
                weights(b, 5)
                if isinstance(b, int) and b == 0:
                    pe.wait_ge(dca_out, 4)
                after(pe, ctl_r, b)
                after(pe, shift, b, nth=4, per=4, ago=1)
                for n, ps in enumerate((c0, c1)):
                    col = slice(n * D, (n + 1) * D)
                    for k in range(CC):
                        last = mm3(ps[0:KEYS, :], cth[:, k, :], ctl[:, k, :], wch[:, k, col], wcl[:, k, col], k == 0, k == CC - 1)
                    last.then_inc(kv_ps, 1)

            def b1_x(s):
                b, par, half = s
                after(pe, xn2_r, b)
                after(pe, kv_ev, b, nth=1, per=2)
                turn(c0, xn2[:, :], x2_ps)

            def b1_q(s):
                b, par, half = s
                weights(b, 6)
                after(pe, x2l_r, b)
                after(pe, kv_ev, b, nth=2, per=2)
                rows(c1, x2h, x2l, C_XQ, q_ps)

            def b1_kT(s):
                after(pe, kn_r, s[0])
                turn(c0, kraw[:, :], kT_ps)

            def b1_qT(s):
                b, par, half = s
                after(pe, qn_r, b)
                after(pe, kT_r, b)
                turn(c0, qraw[:, :], qT_ps)

            def b1_scores(s, rnd):
                b, par, half = s
                if rnd:
                    after(pe, shift, b, nth=2, per=4)
                else:
                    after(pe, qT_r, b)
                for c in range(KC):
                    for r in (2 * rnd, 2 * rnd + 1):
                        rw = slice(32 * r, 32 * r + 32)
                        col = (r % 2) * 512 + c * P
                        last = nc.tensor.matmul(psum[2][:, col:col + L], qT[rw, c, :], kT[rw, c, :], start=True, stop=True)
                last.then_inc(xs_ps, 1)

            def b2_turn(s, r):
                b, par, half = s
                after(pe, pr_r[r // 2], b)
                if r:
                    after(pe, pT_r, b, nth=r, per=4)
                else:
                    after(pe, lg_r, b, ago=1)
                turn(d0, pr[par][:, r * 512:(r + 1) * 512], pT_ps)

            def b2_pv(s, r):
                b, par, half = s
                after(pe, pT_r, b, nth=r + 1, per=4)
                after(pe, vb_r, b)
                for c in range(KC):
                    h = 4 * c + r
                    last = nc.tensor.matmul(d1[32 * r:32 * r + 32, c * L:(c + 1) * L], vx[par][:, h * DV:(h + 1) * DV],
                                            pT[r % 2][:, c, :], start=True, stop=True)
                last.then_inc(pv_ps, 1)

            def b2_wo(s):
                b, par, half = s
                weights(b, 7)
                after(pe, cl_r, b)
                rows(d0, ch, cl, C_XO, xo_ps)

            def b2_x3(s):
                after(pe, xn3_r, s[0])
                turn(d1, xn3[:, :], x3_ps)

            def b2_logits(s):
                b, par, half = s
                after(pe, x3T_r, b)
                after(pe, x2_r, b)
                for k in range(KC):
                    last = nc.tensor.matmul(d0[0:E, 0:L], wgate_sb[:, k, :], x3T[:, k, :], start=(k == 0), stop=(k == KC - 1))
                last.then_inc(lg_ps, 1)

            def b2_logits_turn(s):
                after(pe, lgT_r, s[0])
                nc.tensor.transpose(d0[:, L:2 * L], lgT[:, :], ident[:, :]).then_inc(lgt_ps, 1)

            def body(s):
                on(s[2], b1_kv)
                on(s[1], a2_scores, 0)
                on(s[3], b2_turn, 0)
                on(s[0], a1_turn)
                on(s[2], b1_x)
                on(s[3], b2_turn, 1)
                on(s[3], b2_pv, 0)
                on(s[1], a2_scores, 1)
                on(s[2], b1_q)
                on(s[3], b2_turn, 2)
                on(s[3], b2_pv, 1)
                on(s[1], a2_o)
                on(s[3], b2_turn, 3)
                on(s[0], a1_kg1)
                on(s[3], b2_pv, 2)
                on(s[1], a2_o_turn)
                on(s[0], a1_kg2)
                on(s[3], b2_pv, 3)
                on(s[0], a1_qk)
                on(s[2], b1_kT)
                on(s[3], b2_wo)
                on(s[2], b1_qT)
                on(s[0], a1_v)
                on(s[1], a2_turn)
                on(s[2], b1_scores, 0)
                on(s[3], b2_x3)
                on(s[1], a2_wo)
                on(s[2], b1_scores, 1)
                on(s[3], b2_logits)
                on(s[0], a1_g)
                on(s[3], b2_logits_turn)
            pipeline(pe, body)

            pe.wait_ge(rep_r, 1)
            for b in range(B):
                ps = psum[b // 8][:, (b % 8) * P:(b % 8 + 1) * P]
                last = nc.tensor.transpose(ps, big[0][:, b * P:(b + 1) * P], ident[:, :])
                if b % 4 == 3:
                    last.then_inc(scT_ps, 1)
            pe.wait_ge(route_const, 7)
            for n in range(len(SHIFTS)):
                pe.wait_ge(cnt_r, n + 1)
                nc.tensor.matmul(psum[2][:, 0:1], same_e[:, :, :].rearrange("p e r -> p (e r)"), enough[:, :],
                                 start=True, stop=True).then_inc(dig_ps, 1)
            pe.wait_ge(pos_r, 1)
            for b in range(B):
                ps = psum[b // 8][:, (b % 8) * P:(b % 8 + 1) * P]
                last = nc.tensor.transpose(ps, big[3][:, b * P:(b + 1) * P], ident[:, :])
            last.then_inc(posT_ps, 1)

            def token_turn(e, t):
                if not (isinstance(e, int) and e == 0 and t < 2):
                    pe.wait_ge(xgl_r, 4 * e + (t - 1))
                turn(psum[t % 2][:, 0:512], xg32[:, t, :], xgT_ps)

            def up(e, f):
                n = e * (2 * FH) + f
                if not (isinstance(e, int) and e == 0 and f < 2):
                    pe.wait_ge(hg_r, n - 1)
                hf, fc = f // FH, f % FH
                pe.wait_ge(w_lo, W_PIECES * e + (4 * hf + 2))
                for k in range(KC):
                    c = slice(fc * P, (fc + 1) * P)
                    last = mm3(psum[f % 2][:, 512:1024], w1h[hf][:, k, c], w1l[hf][:, k, c], xgh[:, k, :], xgl[:, k, :],
                               k == 0, k == KC - 1)
                last.then_inc(h_ps, 1)

            def down(e, f):
                n = e * (2 * FH) + f
                hf, fc = f // FH, f % FH
                pe.wait_ge(w_lo, W_PIECES * e + (4 * hf + 4))
                pe.wait_ge(hl_r, n + 1)
                if f == 0 and not (isinstance(e, int) and e == 0):
                    pe.wait_ge(y_ev, 4 * e)
                for t in range(4):
                    tk = slice(t * P, (t + 1) * P)
                    last = mm3(psum[2 + t // 2][:, (t % 2) * 512:(t % 2 + 1) * 512], hh[f % 2][:, tk], hl[f % 2][:, tk],
                               w2h[hf][:, fc, :], w2l[hf][:, fc, :], f == 0, f == 2 * FH - 1)
                if fc == FH - 1:
                    last.then_inc(half_used[hf], 1)
                else:
                    last.then_inc(h_used, 1)

            def expert(e, more):
                pe.wait_ge(xgl_r, 4 * (e + 1))
                up(e, 0)
                for f in range(2 * FH):
                    if f + 1 < 2 * FH:
                        up(e, f + 1)
                    if more and f >= 2 * FH - 2:
                        if f == 2 * FH - 2:
                            pe.wait_ge(xg_in, 16 * (e + 2))
                        token_turn(e + 1, 2 * (f - 2 * FH + 2))
                        token_turn(e + 1, 2 * (f - 2 * FH + 2) + 1)
                    down(e, f)

            pe.wait_ge(xg_in, 16)
            for t in range(4):
                token_turn(0, t)
            expert(0, True)
            with pe.Fori(1, E - 1) as e:
                expert(e, True)
            expert(E - 1, False)

        @block.vector
        def _(dve):
            dve.memset(carry[:, :], 1.0).then_inc(dve_const, 1)
            dve.wait_ge(dve_const, 1)
            dve.memset(carry[:, L:L + 1], 0.0).then_inc(dve_const, 1)
            dve.wait_ge(pool_const, 6)
            dve.tensor_scalar(half_id[:, :], row_id[:, :], DK, None, ALU.bitwise_and).then_inc(dve_const, 1)
            dve.wait_ge(dve_const, 3)
            dve.tensor_scalar(pair_half[:, 1:2], half_id[:, :], UN / DK, None, ALU.mult).then_inc(dve_const, 1)
            dve.tensor_scalar(pair_half[:, 0:1], half_id[:, :], -UN / DK, UN, ALU.mult, ALU.add).then_inc(dve_const, 1)
            dve.memset(scm[:, :], 0.0).then_inc(dve_const, 1)
            dve.memset(lgT[:, :], 0.0).then_inc(dve_const, 1)

            def low(dst, src, scale, hi):
                return dve.scalar_tensor_tensor(dst, src, scale, hi, ALU.mult, ALU.subtract)

            def centre_heads(ap, sums_ap, n):
                dve.tensor_reduce(sums_ap, ap, AX.X, ALU.add).then_inc(cent, 1)
                dve.wait_ge(cent, 2 * n - 1)
                return dve.scalar_tensor_tensor(ap, sums_ap.unsqueeze(len(sums_ap.shape)).to_broadcast(list(sums_ap.shape) + [DV]),
                                                -1.0 / DV, ap, ALU.mult, ALU.add).then_inc(cent, 1)

            def centre(n):
                dve.wait_ge(stage_in[n % NSTAGE], 16 * (n // NSTAGE + 1))
                w = staged(n)[:, :, 0:D]
                for i in range(pieces[n][3]):
                    centre_heads(heads(w[:, i, :]), cent_sums[:, i, :], CENT0[CENTRED.index(n)] + i + 1)

            def split_low(n):
                dve.wait_ge(stage_hi, n + 2)
                for src, hi, lo in split_parts(n):
                    last = low(lo, src, WS, hi)
                last.then_inc(stage_lo, 1)

            def weights_attention():
                dve.wait_ge(stage_hi, 1)
                low(wl[:, :, C_KG:C_KG + DK], KG_STAGE, WS, wh[:, :, C_KG:C_KG + DK]).then_inc(stage_lo, 1)
                dve.wait_ge(dve_const, 7)
                dve.wait_ge(consts_a1_in, 16 * len(consts_a1))

            def second_low():
                dve.wait_ge(dca_split, 1)
                low(dca_l, dca32, XS, dca_h).then_inc(dca_split, 1)
                split_low(4)

            def weights_cross():
                split_low(6)
                split_low(7)
                dve.wait_ge(consts_b_in, 16 * len(consts_b))
                n = CENT0[-1]
                centre_heads(heads(bq_sb[:, :]), cent_sums[:, 0, :], n + 1)
                centre_heads(heads(bkv_sb[:, 0:D]), cent_sums[:, 1, :], n + 2)
                dve.wait_ge(cent, 2 * n + 4)
                dve.memset(wait_pad[:, 0:1], 0.0).then_inc(dve_const, 2)

            def cols(ps):
                return ps.rearrange("p (k n) -> p k n", k=KC)

            apart = [0]

            def wait_apart(signal, value):
                dve.wait_ge(signal, value)
                apart[0] = (apart[0] + 1) % PADS
                dve.memset(wait_pad[:, apart[0]:apart[0] + 1], 0.0)

            def row_stats(n, src, b):
                dve.bn_stats(stats[n][:, :], src).then_inc(stat[n], 1)
                wait_apart(stat[n], 2 * b + 1)
                dve.bn_aggr(aggr[n][:, :], stats[n][:, :]).then_inc(stat[n], 1)

            def row_norm(n, dst, b, done):
                after(dve, dev[n], b, nth=2, per=2)
                dve.tensor_scalar(dst[:, :], x_all[:, seq(b)], aggr[n][:, 0:1], rstd[n][:, :], ALU.subtract, ALU.mult).then_inc(done, 1)

            def head_var(s, n, sq):
                after(dve, hq[n], s[0])
                dve.tensor_reduce(hvar[n][:, :], heads(sq[:, :]), AX.X, ALU.add).then_inc(hv[n], 1)
                if n == 0 and first(s[0], 0):
                    centre(5)

            def head_norm(s, n, dst, src, done):
                after(dve, hdev[n], s[0], nth=2, per=2)
                dve.scalar_tensor_tensor(heads(dst[:, :]), heads(src), DV ** 0.5, per_head(hrs[n][:, :]), ALU.mult, ALU.mult).then_inc(done, 1)

            def a1_stats(s):
                b, par, half = s
                if isinstance(b, int):
                    for n in x_loaded(b):
                        dve.wait_ge(x_in[n], 16)
                row_stats(0, x_all[:, seq(b)], b)

            def a1_norm(s):
                row_norm(0, xn, s[0], xn_r)
                if first(s[0], 0):
                    split_low(0)

            def a1_low(s):
                after(dve, xth_r, s[0])
                low(xtl[:, :, :], cols(a0), XS, xth[:, :, :]).then_inc(xtl_r, 1)
                if first(s[0], 0):
                    centre(1)
                if first(s[0], 1):
                    centre(4)

            def a1_z(s):
                after(dve, kg2_ps, s[0])
                z3 = z[:, :].rearrange("p (c t) -> p c t", c=2)
                dve.tensor_tensor(z3, a1[:, 0:QK].rearrange("p (c t) -> p c t", c=2),
                                  bkg2_sb[:, :].unsqueeze(2).to_broadcast([P, 2, L]), ALU.add).then_inc(z_r, 1)
                if first(s[0], 0):
                    split_low(1)
                if first(s[0], 1):
                    second_low()

            def a1_sums(s):
                b, par, half = s
                after(dve, lsig, b, nth=3, per=3)
                dve.scalar_tensor_tensor(lsg[:, :], z[:, :], 0.0, zl[:, :], ALU.min, ALU.subtract).then_inc(sums, 1)
                after(dve, sums, b, nth=1, per=3)
                dve.tensor_tensor_scan(G[:, :], carry[:, :], lsg[:, :], 0.0, ALU.mult, ALU.add).then_inc(sums, 1)
                after(dve, sums, b, nth=2, per=3)
                G3 = G[:, :].rearrange("p (n t) -> p n t", t=BLK)
                m = BLK // 2 - 1
                dve.tensor_tensor(dq[:, :].rearrange("p (n t) -> p n t", t=BLK), G3,
                                  G3[:, :, m:m + 1].to_broadcast([P, 2 * NBLK, BLK]), ALU.subtract).then_inc(sums, 1)
                if first(b, 0):
                    split_low(2)

            def a1_decayed(s):
                b, par, half = s
                after(dve, qk_ps, b)
                after(dve, eq_r, b)
                blocks = lambda ap: ap.rearrange("p (n t) -> p n t", t=BLK)
                for e in range(2):
                    dve.scalar_tensor_tensor(qeo[par][:, :, e, :], blocks(a0[:, 0:QK]), pair_half[:, e:e + 1], blocks(eq[:, :]),
                                             ALU.mult, ALU.mult)
                after(dve, dke_r, b)
                k3 = a0[:, QK:2 * QK].rearrange("p (c t) -> p c t", c=2)
                for i in range(NBLK):
                    w = slice(KTO[i], KTO[i] + KTW[i])
                    last = dve.scalar_tensor_tensor(kt[par][:, :, w], k3[:, :, 0:KTW[i]], GLA_SCALE * UN, dk[:, :, w],
                                                    ALU.mult, ALU.mult)
                last.then_inc(qk_r, 1)
                if first(b, 0):
                    split_low(3)
                if first(b, 1):
                    weights_cross()

            def a1_gate(s):
                after(dve, g_ps, s[0])
                dve.scalar_tensor_tensor(gf[:, :], a1, UN, bg_sb[:, :], ALU.mult, ALU.add).then_inc(gf_r, 1)

            def a1_recip(s):
                after(dve, gp_r, s[0])
                dve.reciprocal(ge[:, :], ge[:, :]).then_inc(gr_r, 1)

            def a2_mask(s, rnd):
                wait_apart(sc_ps, 2 * s[0] + (rnd + 1))
                for i in range(NBLK):
                    w = KTW[i]
                    dst = scm[0:w, rnd * 1024:(rnd + 1) * 1024].rearrange("p (g t) -> p g t", t=L)[:, :, i * BLK:(i + 1) * BLK]
                    dst = dst.rearrange("p (g e) t -> p g e t", e=2)
                    src = psum[1][0:w, :].rearrange("p (g i e t) -> p g i e t", i=NBLK, e=2, t=BLK)[:, :, i]
                    mask = causal[0:w, i:i + 1, :].bitcast(I32).rearrange("p i (e t) -> p i e t", e=2).to_broadcast([w, 4, 2, BLK])
                    last = dve.copy_predicated(dst, mask, src)
                last.then_inc(scm_r, 1)

            def a2_norm(s):
                head_norm(s, 0, od, b1, on_r)

            def a2_low(s):
                after(dve, oth_r, s[0])
                low(otl[:, :, :], cols(b0), XS, oth[:, :, :]).then_inc(otl_r, 1)
                if first(s[0], 0):
                    split_low(5)
                    centre(6)

            def a2_residual(s):
                b, par, half = s
                after(dve, wo_ps, b)
                dve.scalar_tensor_tensor(x_all[:, seq(b)], b1, UN, x_all[:, seq(b)], ALU.mult, ALU.add).then_inc(x1_r, 1)

            def b1_stats(s):
                b, par, half = s
                wait_apart(x1_r, b + 1)
                row_stats(1, x_all[:, seq(b)], b)

            def b1_norm(s):
                row_norm(1, xn2, s[0], xn2_r)

            def b1_ctx(s):
                b, par, half = s
                after(dve, cth_r, b)
                low(ctl[:, :, :], ctx32[par][:, :, :], XS, cth[:, :, :]).then_inc(ctl_r, 1)

            def b1_k_norm(s):
                head_norm(s, 1, kraw, kraw[:, :], kn_r)

            def b1_low(s):
                after(dve, x2h_r, s[0])
                low(x2l[:, :, :], cols(c0), XS, x2h[:, :, :]).then_inc(x2l_r, 1)

            def b1_q(s):
                b, par, half = s
                if isinstance(b, int) and b == 0:
                    dve.wait_ge(dca_stored, 64)
                after(dve, q_ps, b)
                dve.scalar_tensor_tensor(qraw[:, :], c1, UN, bq_sb[:, :], ALU.mult, ALU.add).then_inc(q_r, 1)

            def b1_q_norm(s):
                head_norm(s, 2, qraw, qraw[:, :], qn_r)

            def b1_softmax(s, rnd):
                b, par, half = s
                after(dve, xs_ps, b, nth=rnd + 1, per=2)
                s3 = psum[2][:, :].rearrange("p (h k) -> p h k", k=L)
                p3 = pr[par][:, rnd * 1024:(rnd + 1) * 1024].rearrange("p (h k) -> p h k", k=L)
                hh8 = slice(rnd * 8, rnd * 8 + 8)
                parts = ((0, slice(0, KEYS), KEYS), (1, slice(KEYS, L), NDCA))
                for n, ks, w in parts:
                    last = dve.tensor_reduce(mx[:, n, hh8], s3[:, :, ks], AX.X, ALU.max)
                last.then_inc(shift, 1)
                after(dve, shift, b, nth=2 * rnd + 1, per=4)
                for n, ks, w in parts:
                    last = dve.tensor_tensor(p3[:, :, ks], s3[:, :, ks], mx[:, n, hh8].unsqueeze(2).to_broadcast([P, 8, w]), ALU.subtract)
                last.then_inc(shift, 1)

            def b1_sums(s, rnd):
                b, par, half = s
                p3 = pr[par][:, rnd * 1024:(rnd + 1) * 1024].rearrange("p (h k) -> p h k", k=L)
                hh8 = slice(rnd * 8, rnd * 8 + 8)
                after(dve, exp_r[rnd], b)
                for n, ks in ((0, slice(0, KEYS)), (1, slice(KEYS, L))):
                    last = dve.tensor_reduce(sm[:, n, hh8], p3[:, :, ks], AX.X, ALU.add)
                last.then_inc(norm[rnd], 1)
                after(dve, norm[rnd], b, nth=1, per=2)
                dve.reciprocal(rc[:, :, hh8], sm[:, :, hh8]).then_inc(norm[rnd], 1)

            def b2_low(s):
                after(dve, ch_r, s[0])
                low(cl[:, :, :], cols(d1), XS, ch[:, :, :]).then_inc(cl_r, 1)

            def b2_residual(s):
                b, par, half = s
                after(dve, xo_ps, b)
                after(dve, xbo_r, b)
                dve.scalar_tensor_tensor(x_all[:, seq(b)], d0, UN, x_all[:, seq(b)], ALU.mult, ALU.add).then_inc(x2_r, 1)

            def b2_stats(s):
                b, par, half = s
                wait_apart(x2_r, b + 1)
                row_stats(2, x_all[:, seq(b)], b)

            def b2_norm(s):
                row_norm(2, xn3, s[0], xn3_r)

            def b2_logits(s):
                b, par, half = s
                after(dve, lgt_ps, b)
                dve.tensor_tensor(logit_all[:, bass.ds(b * E, E)], d0[:, L:L + E], bgate_sb[:, :], ALU.add).then_inc(lg_r, 1)

            def body(s):
                on(s[0], a1_stats)
                on(s[2], b1_norm)
                on(s[1], a1_gate)
                on(s[0], a1_norm)
                on(s[1], a2_mask, 0)
                on(s[3], b1_sums, 1)
                on(s[2], b1_low)
                on(s[2], head_var, 1, ksq)
                on(s[0], a1_low)
                on(s[1], a2_mask, 1)
                on(s[2], b1_q)
                on(s[2], head_var, 2, qsq)
                on(s[2], b1_k_norm)
                on(s[0], a1_z)
                on(s[1], head_var, 0, osq)
                on(s[3], b2_low)
                on(s[1], a1_recip)
                on(s[2], b1_q_norm)
                on(s[1], a2_norm)
                on(s[3], b2_residual)
                on(s[3], b2_stats)
                on(s[0], a1_sums)
                on(s[3], b2_norm)
                on(s[1], a2_low)
                on(s[1], b1_ctx)
                on(s[2], b1_softmax, 0)
                on(s[1], a2_residual)
                on(s[1], b1_stats)
                on(s[2], b1_softmax, 1)
                on(s[2], b1_sums, 0)
                on(s[0], a1_decayed)
                on(s[3], b2_logits)
            pipeline(dve, body, {0: weights_attention})

            step = [0]

            def link(ins):
                step[0] += 1
                ins.then_inc(route, 1)
                dve.wait_ge(route, step[0])

            dve.wait_ge(lg_r, B)
            dve.wait_ge(route_const, 7)
            lg = logit_all[:, :].rearrange("p (b e) -> p b e", e=E)
            mine = lg.unsqueeze(3).to_broadcast([P, B, E, E])
            other = lg.unsqueeze(2).to_broadcast([P, B, E, E])
            tri_b = tri4[:, :, :].rearrange("p a c -> p (a c)").unsqueeze(1).to_broadcast([P, B, E * E])
            flat = lambda t: t[:, :, :, :].rearrange("p b a c -> p b (a c)")
            dve.tensor_tensor(cmp_gt[:, :, :, :], other, mine, ALU.is_gt)
            link(dve.tensor_tensor(cmp_eq[:, :, :, :], other, mine, ALU.is_equal))
            link(dve.tensor_tensor(flat(cmp_eq), flat(cmp_eq), tri_b, ALU.mult))
            link(dve.tensor_tensor(flat(cmp_gt), flat(cmp_gt), flat(cmp_eq), ALU.add))
            link(dve.tensor_reduce(rank[:, :, :], cmp_gt[:, :, :, :], AX.X, ALU.add))
            dve.tensor_scalar(oh[0][:, :, :], rank[:, :, :], 0.0, None, ALU.is_equal)
            dve.tensor_reduce(l1[:, :], lg, AX.X, ALU.max)
            link(dve.tensor_scalar(oh[1][:, :, :], rank[:, :, :], 1.0, None, ALU.is_equal))
            link(dve.tensor_tensor(ohl[:, :, :], oh[1][:, :, :], lg, ALU.mult))
            link(dve.tensor_reduce(l2[:, :], ohl[:, :, :], AX.X, ALU.add))
            link(dve.tensor_tensor(ldiff[:, :], l2[:, :], l1[:, :], ALU.subtract))
            assert step[0] == ROUTE_DIFF
            dve.wait_ge(route_act, 1)
            link(dve.tensor_scalar(den[:, :], ed[:, :], 1.0, None, ALU.add))
            link(dve.reciprocal(p12[:, 0, :], den[:, :]))
            link(dve.tensor_tensor(p12[:, 1, :], p12[:, 0, :], ed[:, :], ALU.mult))
            pk = lambda k: p12[:, k, :].unsqueeze(2).to_broadcast([P, B, E])
            dve.tensor_tensor(score[:, :, :], oh[0][:, :, :], pk(0), ALU.mult)
            link(dve.tensor_tensor(sc2[:, :, :], oh[1][:, :, :], pk(1), ALU.mult))
            link(dve.tensor_tensor(score[:, :, :], score[:, :, :], sc2[:, :, :], ALU.add))
            rep = score[:, :, :].rearrange("p b e -> p (b e)").unsqueeze(2).to_broadcast([P, B * E, P // E])
            dve.tensor_copy(big[0][:, :].rearrange("p (n r) -> p n r", r=P // E), rep).then_inc(rep_r, 1)
            link(dve.tensor_scalar(digit[:, :], pid[:, :], P // E - 1, None, ALU.bitwise_and))
            link(dve.tensor_scalar(eid[:, :], pid[:, :], RADIX, None, ALU.logical_shift_right))
            for n, s in enumerate(SHIFTS):
                dve.tensor_scalar(cands[:, n:n + 1], digit[:, :], s, None, ALU.logical_shift_left)
            dve.tensor_scalar(slot0[:, :], eid[:, :], float(CAP), -1.0 - FAR, ALU.mult, ALU.add)
            link(dve.memset(thr[:, :], 0))
            link(dve.tensor_scalar(taken[:, :, :], rank[:, :, :], 2.0, None, ALU.is_lt))
            link(dve.tensor_copy(upto[:, :, 0], taken[:, :, 0]))
            for e in range(1, E):
                link(dve.tensor_tensor(upto[:, :, e], upto[:, :, e - 1], taken[:, :, e], ALU.add))
            for k in range(2):
                link(dve.scalar_tensor_tensor(by_id[k][:, :, :], upto[:, :, :], float(k + 1), taken[:, :, :], ALU.is_equal, ALU.mult))
            dve.wait_ge(route_act, 5)
            for n, s in enumerate(SHIFTS):
                link(dve.tensor_tensor(cand[:, :], thr[:, :], cands[:, n:n + 1], ALU.bitwise_or))
                link(dve.tensor_scalar(big[1][:, :], big[0][:, :], cand[:, :].bitcast(F32), 0.0, ALU.is_ge, ALU.add, accum_out=count[:, :]))
                dve.tensor_scalar(enough[:, :], count[:, :], float(CAP), None, ALU.is_ge).then_inc(cnt_r, 1)
                dve.wait_ge(dig_ps, n + 1)
                link(dve.tensor_scalar(digit[:, :], psum[2][:, 0:1], -1.0, None, ALU.add))
                link(dve.tensor_scalar(digit[:, :], digit[:, :], s, None, ALU.logical_shift_left))
                link(dve.tensor_tensor(thr[:, :], thr[:, :], digit[:, :], ALU.bitwise_or))
            thr_f = thr[:, :].bitcast(F32)
            link(dve.tensor_scalar(big[1][:, :], big[0][:, :], thr_f, 0.0, ALU.is_gt, ALU.add, accum_out=count[:, :]))
            dve.tensor_scalar(ties[:, :], count[:, :], -1.0, float(CAP), ALU.mult, ALU.add)
            link(dve.tensor_scalar(big[2][:, :], big[0][:, :], thr_f, None, ALU.is_equal))
            one = ones[:, :].to_broadcast([P, N])
            link(dve.tensor_tensor_scan(big[3][:, :], one, big[2][:, :], 0.0, ALU.mult, ALU.add))
            link(dve.scalar_tensor_tensor(big[2][:, :], big[3][:, :], ties[:, :], big[2][:, :], ALU.is_le, ALU.mult))
            link(dve.tensor_tensor(big[1][:, :], big[1][:, :], big[2][:, :], ALU.add))
            link(dve.tensor_tensor_scan(big[2][:, :], one, big[1][:, :], 0.0, ALU.mult, ALU.add))
            dve.scalar_tensor_tensor(big[3][:, :], big[2][:, :], slot0[:, :], big[1][:, :], ALU.add, ALU.mult).then_inc(pos_r, 1)
            dve.wait_ge(posT_ps, 1)
            for g in range(2):
                src = psum[g][:, :].rearrange("p (b e r) -> p b e r", b=8, r=P // E)[:, :, :, 0]
                last = dve.tensor_scalar(posT[:, 8 * g:8 * g + 8, :], src, FAR, None, ALU.add)
            link(last)
            for k in range(2):
                link(dve.tensor_tensor(sel_k[:, :, :], by_id[k][:, :, :], posT[:, :, :], ALU.mult))
                link(dve.tensor_reduce(idx[:, k, :], sel_k[:, :, :], AX.X, ALU.add))
            link(dve.tensor_copy(idx_put[:, :, :], idx[:, :, :]))
            dve.tensor_scalar(idx_get[:, 0, :], idx[:, 0, :], float(GET_ROWS[0] - 1), None, ALU.min)
            dve.tensor_scalar(idx_get[:, 1, :], idx[:, 1, :], float(GET_ROWS[1] - 1), None, ALU.min).then_inc(idx_r, 1)

            def token_weights():
                for k in range(2):
                    link(dve.tensor_tensor(sel_k[:, :, :], by_id[k][:, :, :], score[:, :, :], ALU.mult))
                    link(dve.tensor_reduce(w_raw[:, k, :], sel_k[:, :, :], AX.X, ALU.add))
                dve.scalar_tensor_tensor(wk[:, :, :], idx[:, :, :], float(N), w_raw[:, :, :], ALU.is_lt, ALU.mult)

            def low_piece(e, n):
                _, hi, lo, k = w_piece(e, n)
                dve.wait_ge(w_hi, e * W_PIECES + (n + 1))
                low(lo, wst[n % NST][:, :].rearrange("p (k n) -> p k n", k=k), WS, hi).then_inc(w_lo, 1)

            def tokens_low(e):
                for t in range(4):
                    dve.wait_ge(xgh_r, 4 * e + (t + 1))
                    tk = slice(t * P, (t + 1) * P)
                    low(xgl[:, :, tk], cols(psum[t % 2][:, 0:512]), XS, xgh[:, :, tk]).then_inc(xgl_r, 1)

            def split_h(e, f):
                n = e * (2 * FH) + f
                dve.wait_ge(hg_r, n + 1)
                dve.tensor_scalar(hh[f % 2], hg[f % 2], XS, None, ALU.mult).then_inc(hh_r, 1)
                dve.wait_ge(hh_r, n + 1)
                low(hl[f % 2], hg[f % 2], XS, hh[f % 2]).then_inc(hl_r, 1)

            def results(e):
                dve.wait_ge(half_used[1], e + 1)
                if not isinstance(e, int) or e >= 1:
                    dve.wait_ge(y_st, 16 * e)
                for t in range(4):
                    dve.tensor_scalar(y_sb[:, t, :], psum[2 + t // 2][:, (t % 2) * 512:(t % 2 + 1) * 512], UN, None,
                                      ALU.mult).then_inc(y_ev, 1)

            def expert(e, more):
                for f in range(2 * FH):
                    if f >= 2 and f != FH + 1:
                        dve.wait_ge(h_used, e * (2 * FH - 2) + (f - 1 if f <= FH else f - 2))
                    split_h(e, f)
                    if f < FH and f % 2 == 0:
                        low_piece(e, W_PIECES // 2 + f // 2)
                    if more and f >= FH and f % 2 == 0:
                        low_piece(e + 1, (f - FH) // 2)
                    if not more and f >= 2 * FH - 4:
                        for b in range(4 * (f - 2 * FH + 4), 4 * (f - 2 * FH + 5)):
                            combine(0, b, lo_in, 16 * B)
                if more:
                    tokens_low(e + 1)
                results(e)

            def combine(k, b, fetched, count):
                dve.wait_ge(fetched, count)
                if k:
                    dve.wait_ge(comb, b + 1)
                dve.scalar_tensor_tensor(x_all[:, b * D:(b + 1) * D], yg[b], wk[:, k, b:b + 1],
                                         x_all[:, b * D:(b + 1) * D], ALU.mult, ALU.add).then_inc(comb, 1)

            for n in range(W_PIECES // 2):
                low_piece(0, n)
            token_weights()
            tokens_low(0)
            expert(0, True)
            with dve.Fori(1, E - 1) as e:
                expert(e, True)
            expert(E - 1, False)
            for b in range(B):
                combine(1, b, hi_in[b // (B // NG)], 16 * (B // NG))


ROUTE_DIFF = 8


def kernel(**inputs):
    import numpy as np
    import concourse.bacc as bacc
    from concourse import mybir as my
    from concourse.bass_utils import run_bass_kernel_spmd

    g = {k: np.asarray(a) for k, a in inputs.items()}
    cat = np.concatenate
    main = g["ctx_1024"].shape[1] - 16
    kv = cat([g["L0_xattn_Wk"], g["L0_xattn_Wv"]], axis=1).reshape(256, 16, 2, 32)
    kvb = cat([g["L0_xattn_bk"], g["L0_xattn_bv"]]).reshape(16, 2, 32)
    arrays = {
        "x": g["x"],
        "ctx_t": g["ctx_1024"][:, :main].transpose(0, 2, 1),
        "dca_t": g["ctx_1024"][:, main:].reshape(-1, 256).T,
        "w_attn": cat([g["L0_attn_Wq"].T, g["L0_attn_Wk"].T, g["L0_attn_Wkg1"].T, g["L0_attn_Wv"].T, g["L0_attn_Wg"].T,
                       g["L0_attn_Wo"].T, g["L0_xattn_Wq"], g["L0_xattn_Wo"]], axis=1),
        "w_ctx": cat([kv[:, :, 0].reshape(256, 512), kv[:, :, 1].reshape(256, 512), g["L0_xattn_Wkv_dca"]], axis=1),
        "w_kg2": g["L0_attn_Wkg2"].T,
        "b_kg2": g["L0_attn_bkg2"].reshape(2, 128).T,
        "b_g": g["L0_attn_bg"], "b_q": g["L0_xattn_bq"],
        "b_kv": cat([kvb[:, 0].reshape(512), kvb[:, 1].reshape(512)]),
        "b_dca": g["L0_xattn_bkv_dca"],
        "cols_n": np.stack([np.tile(g["L0_xattn_" + n], 4) for n in ("qn_w", "qn_b", "kn_w", "kn_b", "kn_dca_w", "kn_dca_b")], axis=1),
        "b_o": g["L0_xattn_bo"], "w_gate": g["L0_ffn_Wg"], "b_gate": g["L0_ffn_bg"],
        "w1": g["L0_ffn_W1"], "w2": g["L0_ffn_W2"],
    }
    nc = bacc.Bacc("TRN2", target_bir_lowering=False, num_devices=1)
    feed, args = {}, []
    for name, a in arrays.items():
        a = np.ascontiguousarray(a)
        feed[f"in_{name}"] = a
        args.append(nc.dram_tensor(f"in_{name}", a.shape, my.dt.from_np(a.dtype), kind="ExternalInput").ap())
    out = nc.dram_tensor("out", g["x"].shape, my.dt.float32, kind="ExternalOutput").ap()
    decoder_layer(nc, None, *args, out)
    r = run_bass_kernel_spmd(nc, [feed], core_ids=[0])
    return r.results[0]["out"]
```

```python
from contextlib import ExitStack

import concourse.bass as bass
from concourse import mybir

ALU = mybir.AluOpType
ACT = mybir.ActivationFunctionType
AX = mybir.AxisListType
F32 = mybir.dt.float32
F16 = mybir.dt.float16
I32 = mybir.dt.int32


def decoder_layer(nc, stage_out, x, ctx_t, dca_t, w_attn, w_ctx, w_kg2, b_kg2, b_g, b_q, b_kv, b_dca,
                  cols_n, b_o, w_gate, b_gate, w1, w2, out):
    B, L, D = x.shape
    P = 128
    KC = D // P
    HEADS = 16
    DV = D // HEADS
    DK = 16
    QK = HEADS * DK
    KEYS = ctx_t.shape[2]
    NDCA = L - KEYS
    CC = ctx_t.shape[1] // P
    BLK = 32
    NBLK = L // BLK
    KTW = [BLK * (i + 1) for i in range(NBLK)]
    KTO = [sum(KTW[:i]) for i in range(NBLK)]
    KTN = sum(KTW)
    E = w_gate.shape[0]
    HID = w1.shape[2]
    N = B * L
    CAP = N // E
    XS, WS = 16.0, 256.0
    UN = 1.0 / (XS * WS)
    PADS = 4
    EPS_ROW = 1e-5
    EPS_HEAD = (1e-5, 1e-6, 1e-6)
    GLA_SCALE = 128.0 ** -0.5
    NORM = 16.0
    XSCALE = DV ** -0.5
    RADIX = 5
    SHIFTS = list(range(30 - RADIX, -1, -RADIX))
    FAR = float(2 * N)

    C_QK, C_KG, C_V, C_G, C_O, C_XQ, C_XO = 0, 512, 528, 1040, 1552, 2064, 2576
    W_COLS = C_XO + D

    dca_dram = nc.dram_tensor("dca_scratch", (B * NDCA, 2 * D), F32).ap()
    xg_dram = nc.dram_tensor("xg_scratch", (E * CAP, D), F32).ap()
    y_dram = nc.dram_tensor("y_scratch", ((E - 1) * CAP, D), F32).ap()
    slot_dram = nc.dram_tensor("slot_scratch", (E * CAP, 2), F32).ap()
    out_rows = out.rearrange("b l d -> (b l) d")

    with ExitStack() as ctx:
        def sem(name):
            return ctx.enter_context(nc.semaphore(name))

        def sems(name, n):
            return [sem(f"{name}{i}") for i in range(n)]

        def keep(name, shape, dt=F32):
            return ctx.enter_context(nc.sbuf_tensor(name, shape, dt))

        x_all = keep("x_all", [P, B * D])
        ident = keep("ident", [P, P])
        logit_all = keep("logit_all", [P, B * E])
        mr_all = keep("mr_all", [P, 2 * B])
        bgate_sb = keep("bgate_sb", [P, E])
        neg_half = keep("neg_half", [P, HEADS])

        at = ExitStack()

        def sb(name, shape, dt=F32):
            return at.enter_context(nc.sbuf_tensor(name, shape, dt))

        wh = sb("wh", [P, KC, W_COLS], F16)
        wl = sb("wl", [P, KC, W_COLS], F16)
        wch = sb("wch", [P, CC, 2 * D], F16)
        wcl = sb("wcl", [P, CC, 2 * D], F16)
        wkg2_sb = sb("wkg2_sb", [DK, QK])
        bkg2_sb = sb("bkg2_sb", [P, QK // P])
        bg_sb = sb("bg_sb", [P, D])
        bq_sb = sb("bq_sb", [P, D])
        bo_sb = sb("bo_sb", [P, D])
        bkv_sb = sb("bkv_sb", [P, 2 * D])
        head_cols = sb("head_cols", [P, 6])
        cent_sums = sb("cent_sums", [P, KC, HEADS])
        wgate_sb = sb("wgate_sb", [P, E, D])
        row_id = sb("row_id", [P, 1], I32)
        half_id = sb("half_id", [P, 1], I32)
        pair_half = sb("pair_half", [P, 2])
        causal = sb("causal", [P, NBLK, 2 * BLK])
        carry = sb("carry", [P, QK])

        stats = [sb(f"stats{n}", [P, 6]) for n in range(3)]
        aggr = [sb(f"aggr{n}", [P, 2]) for n in range(3)]
        vare = [sb(f"vare{n}", [P, 1]) for n in range(3)]
        neg_mean = [sb(f"neg_mean{n}", [P, 1]) for n in range(3)]
        shift_row = [sb(f"shift_row{n}", [P, 1]) for n in range(3)]
        rstd = [sb(f"rstd{n}", [P, 1]) for n in range(3)]
        hvar = [sb(f"hvar{n}", [P, HEADS]) for n in range(3)]
        hve = [sb(f"hve{n}", [P, HEADS]) for n in range(3)]
        hrs = [sb(f"hrs{n}", [P, HEADS]) for n in range(3)]

        act_pad = sb("act_pad", [P, 3])
        wait_pad = sb("wait_pad", [P, PADS])
        eps_row = sb("eps_row", [P, 3])
        eps_head = sb("eps_head", [P, 3, HEADS])
        one_col = sb("one_col", [P, 1])

        xn = sb("xn", [P, D])
        xth = sb("xth", [P, KC, L], F16)
        xtl = sb("xtl", [P, KC, L], F16)
        kg1 = sb("kg1", [DK, L])
        z = sb("z", [P, QK])
        zl = sb("zl", [P, QK])
        lsg = sb("lsg", [P, QK])
        G = sb("G", [P, QK])
        dq = sb("dq", [P, QK])
        eq = sb("eq", [P, QK])
        dk = sb("dk", [P, 2, KTN])
        qeo = [sb(f"qeo{i}", [P, 2 * NBLK, 2, BLK]) for i in range(2)]
        kt = [sb(f"kt{i}", [P, 2, KTN]) for i in range(2)]
        v = [sb(f"v{i}", [P, D]) for i in range(2)]
        gf = sb("gf", [P, D])
        ge = sb("ge", [P, D])
        gate = [sb(f"gate{i}", [P, D]) for i in range(2)]

        scm = sb("scm", [P, 4 * 2 * NBLK * 2 * BLK])
        oT = sb("oT", [P, KC, L])
        od = sb("od", [P, D])
        oth = sb("oth", [P, KC, L], F16)
        otl = sb("otl", [P, KC, L], F16)

        ctx32 = [sb(f"ctx32_{i}", [P, CC, KEYS]) for i in range(2)]
        cth = sb("cth", [P, CC, KEYS], F16)
        ctl = sb("ctl", [P, CC, KEYS], F16)
        kraw = sb("kraw", [P, D])
        vx = [sb(f"vx{i}", [P, D]) for i in range(2)]
        ksq = sb("ksq", [P, D])
        kT = sb("kT", [P, KC, L])
        xn2 = sb("xn2", [P, D])
        x2h = sb("x2h", [P, KC, L], F16)
        x2l = sb("x2l", [P, KC, L], F16)
        qraw = sb("qraw", [P, D])
        qsq = sb("qsq", [P, D])
        qT = sb("qT", [P, KC, L])
        mx = sb("mx", [P, 2, HEADS])
        sm = sb("sm", [P, 2, HEADS])
        rc = sb("rc", [P, 2, HEADS])
        pr = [sb(f"pr{i}", [P, HEADS * L]) for i in range(2)]
        pT = [sb(f"pT{i}", [P, KC, L]) for i in range(2)]
        ch = sb("ch", [P, KC, L], F16)
        cl = sb("cl", [P, KC, L], F16)
        xn3 = sb("xn3", [P, D])

        NSTAGE = 5
        stage_buf = [pr[0][:, :], pr[1][:, :]] + [x_all[:, 4 * n * D:4 * (n + 1) * D] for n in range(1, 4)]

        def flat(t):
            return t[:, :, :].rearrange("p k n -> p (k n)")
        dca_w = [[flat(pT[0]).bitcast(F16), flat(pT[1]).bitcast(F16)], [xn3[:, :].bitcast(F16), xn2[:, :].bitcast(F16)]]
        dca32 = flat(qT).rearrange("p (k n) -> p k n", k=CC)
        dca_h = flat(ch).rearrange("p (k n) -> p k n", k=CC)
        dca_l = flat(cl).rearrange("p (k n) -> p k n", k=CC)
        dca_o = [qraw[:, :], qsq[:, :], flat(kT), vx[1][:, :]]
        at.close()

        ff = ExitStack()

        def fb(name, shape, dt=F32):
            return ff.enter_context(nc.sbuf_tensor(name, shape, dt))

        tri4 = fb("tri4", [P, E, E])
        cmp_gt = fb("cmp_gt", [P, B, E, E])
        cmp_eq = fb("cmp_eq", [P, B, E, E])
        rank = fb("rank", [P, B, E])
        oh = [fb(f"oh{k}", [P, B, E]) for k in range(2)]
        taken = fb("taken", [P, B, E])
        upto = fb("upto", [P, B, E])
        by_id = [fb(f"by_id{k}", [P, B, E]) for k in range(2)]
        w_raw = fb("w_raw", [P, 2, B])
        ohl = fb("ohl", [P, B, E])
        l1 = fb("l1", [P, B])
        l2 = fb("l2", [P, B])
        ldiff = fb("ldiff", [P, B])
        ed = fb("ed", [P, B])
        den = fb("den", [P, B])
        p12 = fb("p12", [P, 2, B])
        score = fb("score", [P, B, E])
        sc2 = fb("sc2", [P, B, E])
        big = [fb(f"big{i}", [P, N]) for i in range(4)]
        digit = fb("digit", [P, 1], I32)
        pid = fb("pid", [P, 1], I32)
        cands = fb("cands", [P, len(SHIFTS)], I32)
        cand = fb("cand", [P, 1], I32)
        thr = fb("thr", [P, 1], I32)
        count = fb("count", [P, 1])
        enough = fb("enough", [P, 1])
        same_e = fb("same_e", [P, E, P // E])
        base = fb("base", [P, 1], I32)
        thr_w = fb("thr_w", [P, P])
        tri_in = fb("tri_in", [P, P])
        ones_w = fb("ones_w", [P, P])
        picked = fb("picked", [P, 2, E, B])
        restart = fb("restart", [P, 2, E, B])
        running = fb("running", [P, 2, E, B])
        place = fb("place", [P, 2, E, B])
        ties = fb("ties", [P, E])
        slot0 = fb("slot0", [P, E])
        slot1 = fb("slot1", [P, E])
        take = fb("take", [P, E, B])
        pos_gt = fb("pos_gt", [P, E, B])
        pos_eq = fb("pos_eq", [P, E, B])
        posT = fb("posT", [P, E, B])
        sel_k = fb("sel_k", [P, B, E])
        idx = fb("idx", [P, 2, B])
        idx_put = fb("idx_put", [P, 2, B], I32)
        idx_get = fb("idx_get", [P, 2, B], I32)
        wk = fb("wk", [P, 2, B])
        ids = fb("ids", [P, B], I32)
        id_w = fb("id_w", [P, B, 2])
        no_token = fb("no_token", [P, CAP // P, 2])
        slot_id_w = fb("slot_id_w", [P, CAP // P, 2])
        slot_id = fb("slot_id", [P, CAP // P], I32)
        slot_w = fb("slot_w", [P, CAP // P])
        xn_all = fb("xn_all", [P, B * D])
        zero = fb("zero", [P, D])
        NST = 2
        wst = [fb(f"wst{i}", [P, 2048]) for i in range(NST)]
        HALF = HID // 2
        w1h = [fb(f"w1h{i}", [P, KC, HALF], F16) for i in range(2)]
        w1l = [fb(f"w1l{i}", [P, KC, HALF], F16) for i in range(2)]
        FH = HALF // P
        w2h = [fb(f"w2h{i}", [P, FH, D], F16) for i in range(2)]
        w2l = [fb(f"w2l{i}", [P, FH, D], F16) for i in range(2)]
        xg32 = big[0][:, :].rearrange("p (t n) -> p t n", t=4)
        y_sb = big[1][:, :].rearrange("p (t n) -> p t n", t=4)
        xgh = big[2][:, :].bitcast(F16)[:, 0:2048].rearrange("p (k n) -> p k n", k=KC)
        xgl = big[2][:, :].bitcast(F16)[:, 2048:4096].rearrange("p (k n) -> p k n", k=KC)
        hg = [big[3][:, i * D:(i + 1) * D] for i in range(2)]
        h16 = big[3][:, 2 * D:4 * D].bitcast(F16)
        hh = [h16[:, i * D:(i + 1) * D] for i in range(2)]
        hl = [h16[:, (2 + i) * D:(3 + i) * D] for i in range(2)]
        GET_ROWS = (E - 1) * CAP
        NG = 4
        yg = [xn_all[:, b * D:(b + 1) * D] for b in range(B)]
        ff.close()

        psum = [ctx.enter_context(nc.psum_tensor(f"ps{i}", [P, 1024], F32)) for i in range(4)]
        a0, a1 = psum[0][:, 0:512], psum[0][:, 512:1024]
        b0, b1 = psum[1][:, 0:512], psum[1][:, 512:1024]
        c0, c1 = psum[2][:, 0:512], psum[2][:, 512:1024]
        d0, d1 = psum[3][:, 0:512], psum[3][:, 512:1024]

        x_in = sems("x_in", 4)
        consts_a1_in, consts_b_in = sem("consts_a1_in"), sem("consts_b_in")
        stage_in = sems("stage_in", NSTAGE)
        cent, cent_done, stage_hi, stage_lo = map(sem, ("cent", "cent_done", "stage_hi", "stage_lo"))
        dca_in, dca_split, dca_ps, dca_out, dca_stored = map(sem, (
            "dca_in", "dca_split", "dca_ps", "dca_out", "dca_stored"))
        pool_const, dve_const = sem("pool_const"), sem("dve_const")
        ctx_in = sems("ctx_in", 2)
        kdca_in, vdca_in = sem("kdca_in"), sems("vdca_in", 2)

        stat, dev = sems("stat", 3), sems("dev", 3)
        hq, hv, hdev = (sems(n, 3) for n in ("hq", "hv", "hdev"))

        xn_r, xt_ps, xth_r, xtl_r = map(sem, ("xn_r", "xt_ps", "xth_r", "xtl_r"))
        kg1_ps, qk_ps, kg2_ps, v_ps, g_ps = map(sem, ("kg1_ps", "qk_ps", "kg2_ps", "v_ps", "g_ps"))
        kg1_r, z_r, lsig, sums, dk_r, eq_r, dke_r, qk_r = map(sem, (
            "kg1_r", "z_r", "lsig", "sums", "dk_r", "eq_r", "dke_r", "qk_r"))
        v_r, gf_r, ge_r, gl_r, gx_r, gate_r = map(sem, ("v_r", "gf_r", "ge_r", "gl_r", "gx_r", "gate_r"))
        sc_ps, scm_r = sem("sc_ps"), sem("scm_r")
        oT_ps, oT_r, o_ps, on_r, og_r, ot_ps, oth_r, otl_r, wo_ps, x1_r = map(sem, (
            "oT_ps", "oT_r", "o_ps", "on_r", "og_r", "ot_ps", "oth_r", "otl_r", "wo_ps", "x1_r"))
        cth_r, ctl_r, kv_ps, kv_ev, kb_r, vb_r = map(sem, ("cth_r", "ctl_r", "kv_ps", "kv_ev", "kb_r", "vb_r"))
        kn_r, kT_ps, kT_r = map(sem, ("kn_r", "kT_ps", "kT_r"))
        xn2_r, x2_ps, x2h_r, x2l_r, q_ps, q_r = map(sem, ("xn2_r", "x2_ps", "x2h_r", "x2l_r", "q_ps", "q_r"))
        qn_r, qT_ps, qT_r = map(sem, ("qn_r", "qT_ps", "qT_r"))
        xs_ps, shift = sem("xs_ps"), sem("shift")
        exp_r, norm, pr_r = (sems(n, 2) for n in ("exp_r", "norm", "pr_r"))
        pT_ps, pT_r, pv_ps = map(sem, ("pT_ps", "pT_r", "pv_ps"))
        xbo_r, ch_r, cl_r, xo_ps, x2_r = map(sem, ("xbo_r", "ch_r", "cl_r", "xo_ps", "x2_r"))
        xn3_r, lg_r, mean3_r = sem("xn3_r"), sem("lg_r"), sem("mean3_r")

        route, route_const, rep_r, scT_ps, route_act, cnt_r, dig_ps, pos_r, posT_ps = map(sem, (
            "route", "route_const", "rep_r", "scT_ps", "route_act", "cnt_r", "dig_ps", "pos_r",
            "posT_ps"))
        idx_r, xnall_r, zero_r, zero_st = map(sem, ("idx_r", "xnall_r", "zero_r", "zero_st"))
        put_done = sems("put_done", 2)
        w_in = sems("w_in", NST)
        w_hi, w_lo, xg_in = sem("w_hi"), sem("w_lo"), sem("xg_in")
        half_used = sems("half_used", 2)
        xgT_ps, xgh_r, xgl_r = sem("xgT_ps"), sem("xgh_r"), sem("xgl_r")
        h_ps, hg_r, hh_r, hl_r, h_used = map(sem, ("h_ps", "hg_r", "hh_r", "hl_r", "h_used"))
        y_ev, y_st = sem("y_ev"), sem("y_st")
        lo_in, hi_in, comb, out_st = sem("lo_in"), sems("hi_in", NG), sem("comb"), sem("out_st")
        slot_put, slot_in, part_in, last_st = map(sem, ("slot_put", "slot_in", "part_in", "last_st"))

        def heads(ap):
            return ap.rearrange("p (h c) -> p h c", c=DV)

        def per_head(ap):
            return ap.unsqueeze(2).to_broadcast([P, HEADS, DV])

        def over_heads(ap):
            return ap.unsqueeze(1).to_broadcast([P, HEADS, DV])

        LAGS = 4

        def after(eng, signal, b, nth=1, per=1, ago=0):
            if not isinstance(b, int) or b >= ago:
                eng.wait_ge(signal, per * (b - ago) + nth)

        def first(b, n):
            return isinstance(b, int) and b == n

        def on(stage, step, *args):
            if stage:
                step(stage, *args)

        def pipeline(eng, body, first={}):
            def fixed(t):
                return [(t - k, (t - k) % 2, (t - k) // 2) if 0 <= t - k < B else None for k in range(LAGS)]
            for t in range(LAGS):
                if t in first:
                    first[t]()
                body(fixed(t))
            with eng.Fori(LAGS // 2, B // 2) as j:
                for u in range(2):
                    body([(2 * j + (u - k), (u - k) % 2, j + (u - k) // 2) for k in range(LAGS)])
            for t in range(B, B + LAGS - 1):
                body(fixed(t))

        def seq(b):
            return bass.ds(b * D, D)

        block = ctx.enter_context(nc.Block())

        def w_piece_of(c):
            return (w_attn[:, c:c + D].rearrange("(k p) n -> p k n", p=P), wh[:, :, c:c + D], wl[:, :, c:c + D], KC)
        pieces = [w_piece_of(c) for c in (C_V, C_QK, C_G, C_O)]
        pieces.append((w_ctx[:, 2 * D:4 * D].rearrange("(k p) n -> p k n", p=P), None, None, CC))
        pieces.append((w_ctx[:, 0:2 * D].rearrange("(k p) n -> p k n", p=P), wch[:, :, :], wcl[:, :, :], CC))
        pieces += [w_piece_of(c) for c in (C_XQ, C_XO)]
        POOL_CENTRED = (4, 5, 6)

        def cent_means(n):
            m = POOL_CENTRED.index(n) * KC * HEADS
            return ksq[:, m:m + pieces[n][3] * HEADS]

        def cent_mean(n, i):
            return cent_means(n)[:, i * HEADS:(i + 1) * HEADS]
        KG_STAGE = xn3[:, 0:KC * DK].rearrange("p (k n) -> p k n", k=KC)

        def staged(n):
            return stage_buf[n % NSTAGE].rearrange("p (k n) -> p k n", k=pieces[n][3])

        def split_parts(n):
            _, hi, lo, k = pieces[n]
            if hi is None:
                return [(staged(n)[:, i, :], dca_w[0][i], dca_w[1][i]) for i in range(k)]
            return [(staged(n), hi, lo)]

        consts_a1 = [(KG_STAGE, w_attn[:, C_KG:C_KG + DK].rearrange("(k p) n -> p k n", p=P)), (wkg2_sb[:, :], w_kg2), (bkg2_sb[:, :], b_kg2), (bg_sb[:, :], b_g.partition_broadcast(P))]
        consts_b = [(bq_sb[:, :], b_q.partition_broadcast(P)), (bo_sb[:, :], b_o.partition_broadcast(P)),
                    (bkv_sb[0:KEYS, :], b_kv.partition_broadcast(KEYS)), (bkv_sb[KEYS:P, :], b_dca.partition_broadcast(NDCA)),
                    (head_cols[:, :], cols_n), (wgate_sb[:, :, :], w_gate.partition_broadcast(P)),
                    (bgate_sb[:, :], b_gate.partition_broadcast(P))]
        XPARTS = [(0, 1), (1, 2), (2, 4), (4, B)]

        def x_loaded(b):
            return [n for n, (lo, hi) in enumerate(XPARTS) if lo == b]

        def w_piece(e, n):
            hf, k = n // 4, n % 4
            if k < 2:
                src = w1[bass.ds(e, 1), k * 256:(k + 1) * 256, hf * HALF:(hf + 1) * HALF].rearrange("o (k p) n -> p (o k) n", p=P)
                return src, w1h[hf][:, 2 * k:2 * k + 2, :], w1l[hf][:, 2 * k:2 * k + 2, :], 2
            k -= 2
            lo = hf * HALF + k * 512
            src = w2[bass.ds(e, 1), lo:lo + 512, :].rearrange("o (f p) d -> p (o f) d", p=P)
            return src, w2h[hf][:, 4 * k:4 * k + 4, :], w2l[hf][:, 4 * k:4 * k + 4, :], 4
        W_PIECES = 8

        @block.sync
        def _(sp):
            sp.dma_start(x_all[:, 0:D], x[0]).then_inc(x_in[0], 16)

            def weights(n):
                if n >= NSTAGE:
                    sp.wait_ge(stage_lo, n - NSTAGE + 2)
                sp.dma_start(staged(n), pieces[n][0]).then_inc(stage_in[n % NSTAGE], 16)

            def load_x(n):
                lo, hi = XPARTS[n]
                sp.dma_start(x_all[:, lo * D:hi * D].rearrange("p (b d) -> p b d", d=D),
                             x[lo:hi].rearrange("b p d -> p b d")).then_inc(x_in[n], 16)

            def load_ctx(b, par):
                sp.dma_start(ctx32[par][:, :, :], ctx_t[bass.ds(b, 1)].rearrange("o (k p) n -> p (o k) n", p=P))\
                  .then_inc(ctx_in[par], 16)

            for dst, src in consts_a1:
                sp.dma_start(dst, src).then_inc(consts_a1_in, 16)
            for n in range(3):
                weights(n)
            load_x(1)
            weights(3)
            load_ctx(0, 0)
            weights(4)
            sp.dma_start(dca32, dca_t.rearrange("(k p) n -> p k n", p=P)).then_inc(dca_in, 16)
            load_x(2)
            for dst, src in consts_b:
                sp.dma_start(dst, src).then_inc(consts_b_in, 16)
            for n in range(NSTAGE, len(pieces)):
                weights(n)
            for t in range(4):
                sp.wait_ge(dca_out, t + 1)
                sp.dma_start(dca_dram[(t // 2) * P:(t // 2 + 1) * P, (t % 2) * D:(t % 2 + 1) * D],
                             dca_o[t]).then_inc(dca_stored, 16)
            sp.wait_ge(dca_stored, 64)

            def k_dca(s):
                b, par, half = s
                after(sp, kT_ps, b, ago=1)
                sp.dma_start(kraw[KEYS:P, :], dca_dram[bass.ds(b * NDCA, NDCA), 0:D]).then_inc(kdca_in, 16)

            def v_dca(s):
                b, par, half = s
                after(sp, pv_ps, b, nth=4, per=4, ago=2)
                sp.dma_start(vx[par][KEYS:P, :], dca_dram[bass.ds(b * NDCA, NDCA), D:2 * D]).then_inc(vdca_in[par], 16)

            def context(s):
                b, par, half = s
                if not isinstance(b, int) or b >= 1:
                    after(sp, ctl_r, b, ago=2)
                    load_ctx(b, par)

            def body(s):
                on(s[0], context)
                on(s[1], k_dca)
                on(s[2], v_dca)
            def last_x():
                sp.wait_ge(stage_lo, len(pieces) + 1)
                load_x(3)

            pipeline(sp, body, {2: last_x})

            sp.wait_ge(lg_r, E * B)
            sp.wait_ge(mean3_r, B)
            def load_piece(e, n):
                src, _, _, k = w_piece(e, n)
                sp.dma_start(wst[n % NST][:, :].rearrange("p (k n) -> p k n", k=k), src).then_inc(w_in[n % NST], 16)

            def load_pieces(e, ns):
                for n in ns:
                    if not (isinstance(e, int) and e == 0 and n < NST):
                        sp.wait_ge(w_lo, e * W_PIECES + (n + 1 - NST))
                    load_piece(e, n)

            def load_tokens(e):
                sp.dma_start(xg32, xg_dram[bass.ds(e * CAP, CAP), :].rearrange("(t p) d -> p t d", p=P)).then_inc(xg_in, 16)

            def store_results(e):
                sp.wait_ge(y_ev, 4 * (e + 1))
                sp.dma_start(y_dram[bass.ds(e * CAP, CAP), :].rearrange("(t p) d -> p t d", p=P), y_sb).then_inc(y_st, 16)
            FIRST_HALF, SECOND_HALF = range(W_PIECES // 2), range(W_PIECES // 2, W_PIECES)

            load_pieces(0, FIRST_HALF[:NST])
            sp.wait_ge(zero_r, 1)
            for t in range(N // P):
                sp.dma_start(xg_dram[t * P:(t + 1) * P, :], zero[:, :]).then_inc(zero_st, 16)
            sp.wait_ge(zero_r, 3)
            sp.dma_start(slot_dram[(E - 1) * CAP:E * CAP, :].rearrange("(p t) c -> p t c", p=P), no_token[:, :, :]).then_inc(zero_st, 16)
            load_pieces(0, FIRST_HALF[NST:])
            sp.wait_ge(put_done[0], 16 * B)
            load_tokens(0)

            def next_expert(e):
                sp.wait_ge(xgT_ps, 4 * (e + 1))
                load_tokens(e + 1)
                load_pieces(e, SECOND_HALF[NST:])
                load_pieces(e + 1, FIRST_HALF)
                load_pieces(e + 1, SECOND_HALF[:NST])
                store_results(e)
            load_pieces(0, SECOND_HALF[:1])
            sp.wait_ge(put_done[1], 16 * B)
            sp.wait_ge(xgT_ps, 4)
            load_tokens(1)
            load_pieces(0, SECOND_HALF[1:])
            load_pieces(1, FIRST_HALF)
            load_pieces(1, SECOND_HALF[:NST])
            store_results(0)
            with sp.Fori(1, E - 1) as e:
                next_expert(e)
            sp.wait_ge(slot_put, 16 * B)
            sp.dma_start(slot_id_w[:, :, :], slot_dram[(E - 1) * CAP:E * CAP, :].rearrange("(t p) c -> p t c", p=P)).then_inc(slot_in, 16)
            load_pieces(E - 1, SECOND_HALF[NST:])
            for g in range(NG):
                n = B // NG
                sp.wait_ge(comb, B + n * (g + 1))
                sp.dma_start(out_rows[g * n * L:(g + 1) * n * L, :].rearrange("(b p) d -> p b d", p=P),
                             x_all[:, g * n * D:(g + 1) * n * D].rearrange("p (b d) -> p b d", d=D)).then_inc(out_st, 16)
            sp.wait_ge(out_st, 16 * NG)
            sp.wait_ge(last_st, 16 * (CAP // P))

        @block.gpsimd
        def _(pool):
            pool.memset(ident[:, :], 0.0).then_inc(pool_const, 1)
            pool.memset(causal[:, :, :], 1.0).then_inc(pool_const, 1)
            pool.memset(neg_half[:, :], -0.5).then_inc(pool_const, 1)
            for n in range(3):
                pool.memset(eps_row[:, n:n + 1], EPS_ROW)
                pool.memset(eps_head[:, n, :], DV * EPS_HEAD[n])
            pool.memset(one_col[:, :], 1.0)
            pool.iota(row_id[:, :], [[0, 1]], base=0, channel_multiplier=1).then_inc(pool_const, 1)
            pool.wait_ge(pool_const, 4)
            pool.affine_select(out=ident[:, :], in_=ident[:, :], compare_op=ALU.not_equal, fill=1.0, base=0,
                               pattern=[[-1, P]], channel_multiplier=1).then_inc(pool_const, 1)
            cz = causal[:, :, :].rearrange("p i (e t) -> p i e t", e=2)
            pool.affine_select(out=cz, in_=cz, compare_op=ALU.is_ge, fill=0.0, base=0,
                               pattern=[[BLK, NBLK], [0, 2], [1, BLK]], channel_multiplier=-1).then_inc(pool_const, 1)

            def deviation(s, n):
                b, par, half = s
                after(pool, stat[n], b, nth=3, per=3)
                pool.tensor_tensor(vare[n][:, :], aggr[n][:, 1:2], eps_row[:, n:n + 1], ALU.add).then_inc(dev[n], 1)
                after(pool, dev[n], b, nth=1, per=3)
                pool.tensor_tensor(rstd[n][:, :], vare[n][:, :], neg_half[:, 0:1], ALU.pow).then_inc(dev[n], 1)
                after(pool, dev[n], b, nth=2, per=3)
                pool.tensor_tensor(shift_row[n][:, :], neg_mean[n][:, :], rstd[n][:, :], ALU.mult).then_inc(dev[n], 1)
                if n == 0 and first(b, 1):
                    centre(5)
                    centre(6)

            def head_deviation(s, n):
                b, par, half = s
                after(pool, hv[n], b)
                pool.tensor_tensor(hve[n][:, :], hvar[n][:, :], eps_head[:, n, :], ALU.add).then_inc(hdev[n], 1)
                after(pool, hdev[n], b, nth=1, per=2)
                pool.tensor_tensor(hrs[n][:, :], hve[n][:, :], neg_half[:, :], ALU.pow).then_inc(hdev[n], 1)

            def centre(n):
                pool.wait_ge(cent, 2 * (KC + POOL_CENTRED.index(n) + 1))
                for i in range(pieces[n][3]):
                    w = heads(staged(n)[:, i, 0:D])
                    last = pool.tensor_tensor(w, w, per_head(cent_mean(n, i)), ALU.subtract)
                last.then_inc(cent_done, 1)

            def k_decay(s):
                b, par, half = s
                after(pool, sums, b, nth=2, per=3)
                G3 = G[:, :].rearrange("p (c t) -> p c t", c=2)
                for i in range(NBLK):
                    m = BLK * i + BLK // 2 - 1
                    last = pool.tensor_tensor(dk[:, :, KTO[i]:KTO[i] + KTW[i]],
                                              G3[:, :, m:m + 1].to_broadcast([P, 2, KTW[i]]),
                                              G3[:, :, 0:KTW[i]], ALU.subtract)
                last.then_inc(dk_r, 1)
                if first(b, 0):
                    centre(4)

            def gate_silu(s):
                b, par, half = s
                after(pool, gx_r, b)
                pool.tensor_tensor(gate[par][:, :], gf[:, :], ge[:, :], ALU.mult).then_inc(gate_r, 1)

            def gated(s):
                b, par, half = s
                after(pool, on_r, b)
                after(pool, gate_r, b)
                pool.tensor_tensor(od[:, :], od[:, :], gate[par][:, :], ALU.mult).then_inc(og_r, 1)

            def k_bias(s):
                b, par, half = s
                after(pool, kv_ev, b, nth=1, per=2)
                after(pool, kdca_in, b, nth=16, per=16)
                pool.tensor_tensor(kraw[:, :], kraw[:, :], bkv_sb[:, 0:D], ALU.add).then_inc(kb_r, 1)

            def v_bias(s):
                b, par, half = s
                after(pool, kv_ev, b, nth=2, per=2)
                after(pool, vdca_in[par], half, nth=16, per=16)
                pool.tensor_tensor(vx[par][:, :], vx[par][:, :], bkv_sb[:, D:2 * D], ALU.add).then_inc(vb_r, 1)

            def out_bias(s):
                b, par, half = s
                after(pool, xn2_r, b)
                pool.tensor_tensor(x_all[:, seq(b)], x_all[:, seq(b)], bo_sb[:, :], ALU.add).then_inc(xbo_r, 1)

            def probs(s, rnd):
                b, par, half = s
                after(pool, norm[rnd], b, nth=2, per=2)
                p3 = pr[par][:, rnd * 1024:(rnd + 1) * 1024].rearrange("p (h k) -> p h k", k=L)
                rr = rc[:, :, rnd * 8:(rnd + 1) * 8]
                pool.tensor_tensor(p3[:, :, 0:KEYS], p3[:, :, 0:KEYS],
                                   rr[:, 0].unsqueeze(2).to_broadcast([P, 8, KEYS]), ALU.mult)
                pool.tensor_tensor(p3[:, :, KEYS:L], p3[:, :, KEYS:L],
                                   rr[:, 1].unsqueeze(2).to_broadcast([P, 8, NDCA]), ALU.mult).then_inc(pr_r[rnd], 1)

            def keep_norm(s):
                b, par, half = s
                deviation(s, 2)
                pool.tensor_copy(mr_all[:, bass.ds(2 * b + 1, 1)], rstd[2][:, :])
                after(pool, dev[2], b, nth=3, per=3)
                pool.tensor_copy(mr_all[:, bass.ds(2 * b, 1)], shift_row[2][:, :]).then_inc(mean3_r, 1)

            def body(s):
                on(s[2], k_bias)
                on(s[3], probs, 1)
                on(s[0], deviation, 0)
                on(s[2], head_deviation, 1)
                on(s[2], head_deviation, 2)
                on(s[2], out_bias)
                on(s[1], head_deviation, 0)
                on(s[1], gate_silu)
                on(s[1], gated)
                on(s[0], k_decay)
                on(s[3], keep_norm)
                on(s[2], probs, 0)
                on(s[2], v_bias)
                on(s[1], deviation, 1)
            pipeline(pool, body, {2: lambda: pool.wait_ge(dve_const, 8)})

            pool.wait_ge(lg_r, E * B)
            pool.wait_ge(mean3_r, B)
            pool.memset(zero[:, :], 0.0).then_inc(zero_r, 1)
            pool.memset(no_token[:, :, 0:1], float(N)).then_inc(zero_r, 1)
            pool.memset(no_token[:, :, 1:2], 0.0).then_inc(zero_r, 1)
            pool.memset(tri4[:, :, :], 1.0).then_inc(route_const, 1)
            pool.memset(same_e[:, :, :], 1.0).then_inc(route_const, 1)
            pool.memset(tri_in[:, :], 1.0).then_inc(route_const, 1)
            for e in range(E):
                pool.memset(slot0[:, e:e + 1], e * CAP - 1.0 - FAR)
            pool.memset(ones_w[:, :], 1.0)
            pool.iota(ids[:, :], [[P, B]], base=0, channel_multiplier=1)
            pool.iota(pid[:, :], [[0, 1]], base=0, channel_multiplier=1).then_inc(route_const, 1)
            pool.wait_ge(route_const, 4)
            pool.affine_select(out=tri4[:, :, :], in_=tri4[:, :, :], compare_op=ALU.is_gt, fill=0.0, base=0,
                               pattern=[[1, E], [-1, E]], channel_multiplier=0).then_inc(route_const, 1)
            pool.affine_select(out=same_e[:, :, :], in_=same_e[:, :, :], compare_op=ALU.is_ge, fill=0.0, base=0,
                               pattern=[[-(P // E), E], [0, P // E]], channel_multiplier=1).then_inc(route_const, 1)
            pool.affine_select(out=tri_in[:, :], in_=tri_in[:, :], compare_op=ALU.is_ge, fill=0.0, base=0,
                               pattern=[[1, P]], channel_multiplier=-1).then_inc(route_const, 1)
            pool.wait_ge(route_const, 7)
            pool.affine_select(out=same_e[:, :, :], in_=same_e[:, :, :], compare_op=ALU.is_gt, fill=0.0, base=P // E,
                               pattern=[[P // E, E], [0, P // E]], channel_multiplier=-1).then_inc(route_const, 1)
            pool.wait_ge(xnall_r, 1)
            pool.wait_ge(zero_st, 16 * (N // P + 1))
            pool.wait_ge(idx_r, 1)
            for k in range(2):
                for b in range(B):
                    pool.indirect_dma_start(out=xg_dram, out_offset=bass.IndirectOffsetOnAxis(ap=idx_put[:, k, b:b + 1], axis=0),
                                            in_=xn_all[:, b * D:(b + 1) * D], in_offset=None,
                                            bounds_check=N - 1, oob_is_err=False).then_inc(put_done[k], 16)

            pool.wait_ge(idx_r, 2)
            for b in range(B):
                pool.indirect_dma_start(out=slot_dram, out_offset=bass.IndirectOffsetOnAxis(ap=idx_put[:, 1, b:b + 1], axis=0),
                                        in_=id_w[:, b, :], in_offset=None,
                                        bounds_check=N - 1, oob_is_err=False).then_inc(slot_put, 16)

            def fetch(k, b, done):
                pool.indirect_dma_start(out=yg[b], out_offset=None, in_=y_dram,
                                        in_offset=bass.IndirectOffsetOnAxis(ap=idx_get[:, k, b:b + 1], axis=0),
                                        bounds_check=GET_ROWS - 1, oob_is_err=False).then_inc(done, 16)
            for k in range(2):
                pool.wait_ge(put_done[k], 16 * B)
            pool.wait_ge(y_st, 16 * (E - 1))
            for b in range(B):
                fetch(0, b, lo_in)
            for g in range(NG):
                pool.wait_ge(comb, (g + 1) * (B // NG))
                for b in range(g * (B // NG), (g + 1) * (B // NG)):
                    fetch(1, b, hi_in[g])

            pool.wait_ge(idx_r, 3)
            pool.wait_ge(xgT_ps, 4 * E)
            pool.wait_ge(out_st, 16 * NG)
            for t in range(CAP // P):
                pool.indirect_dma_start(out=xg32[:, t, :], out_offset=None, in_=out_rows,
                                        in_offset=bass.IndirectOffsetOnAxis(ap=slot_id[:, t:t + 1], axis=0),
                                        bounds_check=N - 1, oob_is_err=False).then_inc(part_in, 16)
            for t in range(CAP // P):
                pool.wait_ge(y_ev, 4 * (E - 1) + t + 1)
                pool.indirect_dma_start(out=out_rows, out_offset=bass.IndirectOffsetOnAxis(ap=slot_id[:, t:t + 1], axis=0),
                                        in_=y_sb[:, t, :], in_offset=None,
                                        bounds_check=N - 1, oob_is_err=False).then_inc(last_st, 16)

        @block.scalar
        def _(act):
            def split_hi(n):
                act.wait_ge(stage_in[n % NSTAGE], 16 * (n // NSTAGE + 1))
                if n == 0:
                    act.wait_ge(cent, 2 * KC)
                if n in POOL_CENTRED:
                    act.wait_ge(cent_done, POOL_CENTRED.index(n) + 1)
                for src, hi, lo in split_parts(n):
                    last = act.activation(hi, src, ACT.Copy, scale=WS)
                last.then_inc(stage_hi, 1)

            def weights_attention():
                act.wait_ge(consts_a1_in, 16 * len(consts_a1))
                act.activation(wh[:, :, C_KG:C_KG + DK], KG_STAGE, ACT.Copy, scale=WS).then_inc(stage_hi, 1)

            def second_hi():
                act.wait_ge(dca_in, 16)
                act.activation(dca_h, dca32, ACT.Copy, scale=XS).then_inc(dca_split, 1)
                split_hi(4)

            def second_out():
                for t in range(4):
                    act.wait_ge(dca_ps, t + 1)
                    act.activation(dca_o[t], psum[2 + t // 2][:, (t % 2) * 512:(t % 2 + 1) * 512], ACT.Copy, scale=UN).then_inc(dca_out, 1)

            def square(dst, src, ready, value_of, done):
                after(act, ready, value_of)
                act.activation(dst, src, ACT.Square).then_inc(done, 1)

            def take(dst, ps, scale, done):
                act.activation(dst, ps, ACT.Copy, scale=scale).then_inc(done, 1)

            def cols(ps):
                return ps.rearrange("p (k n) -> p k n", k=KC)

            def x_hi(s):
                after(act, xt_ps, s[0])
                take(xth[:, :, :], cols(a0), XS, xth_r)
                if first(s[0], 0):
                    split_hi(0)

            def kg1_out(s):
                after(act, kg1_ps, s[0])
                take(kg1[:, :], a1[0:DK, 0:L], UN, kg1_r)
                if first(s[0], 0):
                    split_hi(1)
                if first(s[0], 1):
                    split_hi(6)

            def log_sigmoid(s):
                b, par, half = s
                after(act, z_r, b)
                act.activation(zl[:, :], z[:, :], ACT.Abs).then_inc(lsig, 1)
                after(act, lsig, b, nth=1, per=3)
                act.activation(zl[:, :], zl[:, :], ACT.Exp, scale=-1.0).then_inc(lsig, 1)
                after(act, lsig, b, nth=2, per=3)
                act.activation(zl[:, :], zl[:, :], ACT.Ln, bias=1.0).then_inc(lsig, 1)
                if first(b, 0):
                    split_hi(2)
                if first(b, 1):
                    second_out()
                    split_hi(7)

            def q_decay(s):
                after(act, sums, s[0], nth=3, per=3)
                act.activation(eq[:, :], dq[:, :], ACT.Exp, scale=1.0 / NORM).then_inc(eq_r, 1)

            def k_decay(s):
                after(act, dk_r, s[0])
                act.activation(dk[:, :, :], dk[:, :, :], ACT.Exp, scale=1.0 / NORM).then_inc(dke_r, 1)
                if first(s[0], 0):
                    split_hi(3)

            def v_out(s):
                b, par, half = s
                after(act, v_ps, b)
                take(v[par][:, :], a1, UN, v_r)

            def gate_log(s):
                b, par, half = s
                after(act, gf_r, b)
                act.activation(ge[:, :], gf[:, :], ACT.Abs).then_inc(ge_r, 1)
                after(act, ge_r, b, nth=1, per=3)
                act.activation(ge[:, :], ge[:, :], ACT.Exp, scale=-1.0).then_inc(ge_r, 1)
                after(act, ge_r, b, nth=2, per=3)
                act.activation(ge[:, :], ge[:, :], ACT.Ln, bias=1.0).then_inc(ge_r, 1)
                if first(b, 0):
                    second_hi()

            def gate_sigmoid(s):
                after(act, gl_r, s[0])
                act.activation(ge[:, :], ge[:, :], ACT.Exp).then_inc(gx_r, 1)

            def row_norm(s, n, dst, done):
                b, par, half = s
                after(act, dev[n], b, nth=3, per=3)
                act.activation(act_pad[:, n:n + 1], rstd[n][:, :], ACT.Copy)
                act.activation(dst[:, :], x_all[:, seq(b)], ACT.Identity, scale=rstd[n][:, :], bias=shift_row[n][:, :]).then_inc(done, 1)

            def o_out(s):
                after(act, oT_ps, s[0])
                take(oT[:, :, :], cols(b0), 1.0, oT_r)
                if first(s[0], 0):
                    split_hi(5)

            def o_square(s):
                square(od[:, :], b1, o_ps, s[0], hq[0])

            def o_hi(s):
                after(act, ot_ps, s[0])
                take(oth[:, :, :], cols(b0), XS, oth_r)

            def ctx_hi(s):
                b, par, half = s
                after(act, ctx_in[par], half, nth=16, per=16)
                after(act, kv_ps, b, nth=2, per=2, ago=1)
                act.activation(cth[:, :, :], ctx32[par][:, :, :], ACT.Copy, scale=XS).then_inc(cth_r, 1)

            def kv_out(s):
                b, par, half = s
                after(act, kv_ps, b, nth=1, per=2)
                take(kraw[0:KEYS, :], c0[0:KEYS], UN, kv_ev)
                after(act, kv_ps, b, nth=2, per=2)
                take(vx[par][0:KEYS, :], c1[0:KEYS], UN, kv_ev)

            def k_square(s):
                square(ksq[:, :], kraw[:, :], kb_r, s[0], hq[1])

            def k_out(s):
                after(act, kT_ps, s[0])
                act.activation(kT[:, :, 0:KEYS], cols(c0)[:, :, 0:KEYS], ACT.Identity, scale=head_cols[:, 2:3], bias=head_cols[:, 3:4])
                act.activation(kT[:, :, KEYS:L], cols(c0)[:, :, KEYS:L], ACT.Identity, scale=head_cols[:, 4:5], bias=head_cols[:, 5:6]).then_inc(kT_r, 1)

            def x2_hi(s):
                after(act, x2_ps, s[0])
                take(x2h[:, :, :], cols(c0), XS, x2h_r)

            def q_square(s):
                square(qsq[:, :], qraw[:, :], q_r, s[0], hq[2])

            def q_out(s):
                after(act, qT_ps, s[0])
                act.activation(qT[:, :, :], cols(c0), ACT.Identity, scale=head_cols[:, 0:1], bias=head_cols[:, 1:2]).then_inc(qT_r, 1)

            def exponents(s, rnd):
                b, par, half = s
                after(act, shift, b, nth=2 * rnd + 2, per=4)
                half_p = pr[par][:, rnd * 1024:(rnd + 1) * 1024]
                act.activation(half_p, half_p, ACT.Exp, scale=XSCALE).then_inc(exp_r[rnd], 1)

            def p_out(s, r):
                after(act, pT_ps, s[0], nth=r + 1, per=4)
                take(pT[r % 2][:, :, :], cols(d0), 1.0, pT_r)

            def c_hi(s):
                after(act, pv_ps, s[0], nth=4, per=4)
                take(ch[:, :, :], cols(d1), XS, ch_r)

            def body(s):
                on(s[2], k_square)
                on(s[1], gate_log)
                on(s[2], q_square)
                on(s[3], p_out, 0)
                on(s[0], row_norm, 0, xn, xn_r)
                on(s[3], p_out, 1)
                on(s[0], x_hi)
                on(s[3], p_out, 2)
                on(s[2], k_out)
                on(s[1], o_out)
                on(s[3], p_out, 3)
                on(s[0], kg1_out)
                on(s[2], q_out)
                on(s[3], c_hi)
                on(s[1], o_square)
                on(s[1], gate_sigmoid)
                on(s[0], log_sigmoid)
                on(s[2], exponents, 0)
                on(s[0], v_out)
                on(s[0], q_decay)
                on(s[1], o_hi)
                on(s[0], k_decay)
                on(s[2], exponents, 1)
                on(s[3], row_norm, 2, xn3, xn3_r)
                on(s[1], kv_out)
                on(s[1], row_norm, 1, xn2, xn2_r)
                on(s[0], ctx_hi)
                on(s[1], x2_hi)
            nc.scalar.preload_act_table_set("natural_log_exp_and_others")
            pipeline(act, body, {0: weights_attention})

            act.wait_ge(route, ROUTE_DIFF)
            act.activation(ed[:, :], ldiff[:, :], ACT.Exp).then_inc(route_act, 1)
            for i in range(4):
                act.wait_ge(scT_ps, i + 1)
                act.activation(big[0][:, i * 512:(i + 1) * 512], psum[i // 2][:, (i % 2) * 512:(i % 2 + 1) * 512],
                               ACT.Copy).then_inc(route_act, 1)
            act.wait_ge(mean3_r, B)
            for b in range(B):
                last = act.activation(xn_all[:, b * D:(b + 1) * D], x_all[:, b * D:(b + 1) * D], ACT.Identity,
                                      scale=mr_all[:, 2 * b + 1:2 * b + 2], bias=mr_all[:, 2 * b:2 * b + 1])
            last.then_inc(xnall_r, 1)

            def split_piece(e, n):
                _, dst, _, k = w_piece(e, n)
                act.wait_ge(w_in[n % NST], 16 * (e * (W_PIECES // NST) + n // NST + 1))
                act.activation(dst, wst[n % NST][:, :].rearrange("p (k n) -> p k n", k=k), ACT.Copy, scale=WS).then_inc(w_hi, 1)

            def tokens_hi(e):
                for t in range(4):
                    act.wait_ge(xgT_ps, 4 * e + (t + 1))
                    act.activation(xgh[:, :, t * P:(t + 1) * P], cols(psum[t % 2][:, 0:512]),
                                   ACT.Copy, scale=XS).then_inc(xgh_r, 1)

            def gelu(e, f):
                n = e * (2 * FH) + f
                act.wait_ge(h_ps, n + 1)
                if not (isinstance(e, int) and e == 0 and f < 2):
                    act.wait_ge(hl_r, n - 1)
                act.activation(hg[f % 2], psum[f % 2][:, 512:1024], ACT.Gelu, scale=UN).then_inc(hg_r, 1)

            def expert(e, more):
                for f in range(2 * FH):
                    gelu(e, f)
                    if f < FH and f % 2 == 0:
                        if not (isinstance(e, int) and e == 0):
                            act.wait_ge(half_used[1], e)
                        split_piece(e, W_PIECES // 2 + f // 2)
                    if more and f >= FH and f % 2 == 0:
                        act.wait_ge(half_used[0], e + 1)
                        split_piece(e + 1, (f - FH) // 2)
                if more:
                    tokens_hi(e + 1)

            for n in range(W_PIECES // 2):
                split_piece(0, n)
            tokens_hi(0)
            expert(0, True)
            with act.Fori(1, E - 1) as e:
                expert(e, True)
            expert(E - 1, False)

        @block.tensor
        def _(pe):
            def mm3(o, lh, ll, rh, rl, first, last):
                nc.tensor.matmul(o, lh, rh, start=first, stop=False)
                nc.tensor.matmul(o, lh, rl, start=False, stop=False)
                return nc.tensor.matmul(o, ll, rh, start=False, stop=last)

            def turn(ps, src, done):
                for c in range(KC):
                    last = nc.tensor.transpose(ps[:, c * P:(c + 1) * P], src[:, c * P:(c + 1) * P], ident[:, :])
                last.then_inc(done, 1)

            def rows(ps, xh, xl, col, done):
                for k in range(KC):
                    last = mm3(ps, xh[:, k, :], xl[:, k, :], wh[:, k, col:col + D], wl[:, k, col:col + D], k == 0, k == KC - 1)
                last.then_inc(done, 1)

            def second_kv():
                pe.wait_ge(stage_lo, 4 + 2)
                pe.wait_ge(dca_split, 2)
                for t in range(4):
                    ps = psum[2 + t // 2][:, (t % 2) * 512:(t % 2 + 1) * 512]
                    tok = slice((t // 2) * P, (t // 2 + 1) * P)
                    col = slice((t % 2) * D, (t % 2 + 1) * D)
                    for k in range(CC):
                        last = mm3(ps, dca_h[:, k, tok], dca_l[:, k, tok], dca_w[0][k][:, col], dca_w[1][k][:, col], k == 0, k == CC - 1)
                    last.then_inc(dca_ps, 1)

            def weights(b, n):
                if isinstance(b, int) and b == 0:
                    pe.wait_ge(stage_lo, n + 2)

            def a1_turn(s):
                b, par, half = s
                if isinstance(b, int) and b == 0:
                    pe.wait_ge(pool_const, 5)
                after(pe, xn_r, b)
                turn(a0, xn[:, :], xt_ps)

            def a1_kg1(s):
                b, par, half = s
                weights(b, -1)
                after(pe, xtl_r, b)
                for k in range(KC):
                    last = mm3(a1[0:DK, 0:L], wh[:, k, C_KG:C_KG + DK], wl[:, k, C_KG:C_KG + DK],
                               xth[:, k, :], xtl[:, k, :], k == 0, k == KC - 1)
                last.then_inc(kg1_ps, 1)

            def a1_qk(s):
                b, par, half = s
                weights(b, 1)
                after(pe, xtl_r, b)
                for g in range(4):
                    for k in range(KC):
                        c = C_QK + g * P
                        last = mm3(a0[:, g * L:(g + 1) * L], wh[:, k, c:c + P], wl[:, k, c:c + P],
                                   xth[:, k, :], xtl[:, k, :], k == 0, k == KC - 1)
                last.then_inc(qk_ps, 1)

            def a1_kg2(s):
                b, par, half = s
                if isinstance(b, int) and b == 0:
                    pe.wait_ge(consts_a1_in, 16 * len(consts_a1))
                after(pe, kg1_r, b)
                for c in range(2):
                    last = nc.tensor.matmul(a1[:, c * L:(c + 1) * L], wkg2_sb[:, c * P:(c + 1) * P], kg1[:, :], start=True, stop=True)
                last.then_inc(kg2_ps, 1)
                if first(b, 1):
                    second_kv()

            def a1_v(s):
                b, par, half = s
                weights(b, 0)
                after(pe, z_r, b)
                rows(a1, xth, xtl, C_V, v_ps)

            def a1_g(s):
                b, par, half = s
                weights(b, 2)
                after(pe, v_r, b)
                rows(a1, xth, xtl, C_G, g_ps)

            def a2_scores(s, rnd):
                b, par, half = s
                after(pe, qk_r, b)
                if rnd:
                    after(pe, scm_r, b, nth=1, per=2)
                for c in range(2):
                    for i in reversed(range(NBLK)):
                        for r in (2 * rnd, 2 * rnd + 1):
                            rw = slice(32 * r, 32 * r + 32)
                            col = (r % 2) * 512 + c * 256 + i * 2 * BLK
                            last = nc.tensor.matmul(psum[1][0:KTW[i], col:col + 2 * BLK], kt[par][rw, c, KTO[i]:KTO[i] + KTW[i]],
                                                    qeo[par][rw, c * NBLK + i, :, :].rearrange("p e t -> p (e t)"), start=True, stop=True)
                last.then_inc(sc_ps, 1)

            def a2_o(s):
                b, par, half = s
                after(pe, scm_r, b, nth=2, per=2)
                after(pe, v_r, b)
                sc = scm[:, :].rearrange("p (r c e t) -> p r c e t", r=4, c=2, e=2)
                for h in range(HEADS):
                    j, e = h // 2, h % 2
                    n, c = h % 4, h // 4
                    last = nc.tensor.matmul(b0[n * DV:(n + 1) * DV, c * L:(c + 1) * L], v[par][:, h * DV:(h + 1) * DV],
                                            sc[:, j % 4, j // 4, e, :], start=True, stop=True)
                last.then_inc(oT_ps, 1)

            def a2_o_turn(s):
                after(pe, oT_r, s[0])
                turn(b1, oT[:, :, :].rearrange("p k n -> p (k n)"), o_ps)

            def a2_turn(s):
                after(pe, og_r, s[0])
                turn(b0, od[:, :], ot_ps)

            def a2_wo(s):
                b, par, half = s
                weights(b, 3)
                after(pe, otl_r, b)
                rows(b1, oth, otl, C_O, wo_ps)

            def b1_kv(s):
                b, par, half = s
                weights(b, 5)
                if isinstance(b, int) and b == 0:
                    pe.wait_ge(dca_out, 4)
                after(pe, ctl_r, b)
                after(pe, shift, b, nth=4, per=4, ago=1)
                for n, ps in enumerate((c0, c1)):
                    col = slice(n * D, (n + 1) * D)
                    for k in range(CC):
                        last = mm3(ps[0:KEYS, :], cth[:, k, :], ctl[:, k, :], wch[:, k, col], wcl[:, k, col], k == 0, k == CC - 1)
                    last.then_inc(kv_ps, 1)

            def b1_x(s):
                b, par, half = s
                after(pe, xn2_r, b)
                after(pe, kv_ev, b, nth=1, per=2)
                turn(c0, xn2[:, :], x2_ps)

            def b1_q(s):
                b, par, half = s
                weights(b, 6)
                after(pe, x2l_r, b)
                after(pe, kv_ev, b, nth=2, per=2)
                rows(c1, x2h, x2l, C_XQ, q_ps)

            def b1_kT(s):
                after(pe, kn_r, s[0])
                turn(c0, kraw[:, :], kT_ps)

            def b1_qT(s):
                b, par, half = s
                after(pe, qn_r, b)
                after(pe, kT_r, b)
                turn(c0, qraw[:, :], qT_ps)

            def b1_scores(s, rnd):
                b, par, half = s
                if rnd:
                    after(pe, shift, b, nth=2, per=4)
                else:
                    after(pe, qT_r, b)
                for c in range(KC):
                    for r in (2 * rnd, 2 * rnd + 1):
                        rw = slice(32 * r, 32 * r + 32)
                        col = (r % 2) * 512 + c * P
                        last = nc.tensor.matmul(psum[2][:, col:col + L], qT[rw, c, :], kT[rw, c, :], start=True, stop=True)
                last.then_inc(xs_ps, 1)

            def pv_heads(g):
                return [(2 * (g // 2) + i, 2 * (g % 2) + c) for c in range(2) for i in range(2)]

            def b2_turn(s, r):
                b, par, half = s
                after(pe, pr_r[r // 2], b)
                if r:
                    after(pe, pT_r, b, nth=r, per=4)
                else:
                    after(pe, x2_r, b, ago=1)
                pg = pr[par][:, :].rearrange("p (m n) -> p m n", n=L)
                for i, (rr, c) in enumerate(pv_heads(r)):
                    last = nc.tensor.transpose(d0[:, i * L:(i + 1) * L], pg[:, rr * KC + c, :], ident[:, :])
                last.then_inc(pT_ps, 1)

            def b2_pv(s, r):
                b, par, half = s
                after(pe, pT_r, b, nth=r + 1, per=4)
                after(pe, vb_r, b)
                if r == 0:
                    after(pe, lg_r, b, nth=E, per=E, ago=1)
                for i, (rr, c) in enumerate(pv_heads(r)):
                    h = 4 * c + rr
                    last = nc.tensor.matmul(d1[32 * rr:32 * rr + 32, c * L:(c + 1) * L], vx[par][:, h * DV:(h + 1) * DV],
                                            pT[r % 2][:, i, :], start=True, stop=True)
                last.then_inc(pv_ps, 1)

            def b2_wo(s):
                b, par, half = s
                weights(b, 7)
                after(pe, cl_r, b)
                rows(d0, ch, cl, C_XO, xo_ps)

            def body(s):
                on(s[1], a2_scores, 0)
                on(s[2], b1_q)
                on(s[3], b2_turn, 0)
                on(s[1], a2_scores, 1)
                on(s[3], b2_turn, 1)
                on(s[3], b2_pv, 0)
                on(s[0], a1_turn)
                on(s[2], b1_kT)
                on(s[3], b2_turn, 2)
                on(s[3], b2_pv, 1)
                on(s[1], a2_o)
                on(s[3], b2_turn, 3)
                on(s[0], a1_kg1)
                on(s[3], b2_pv, 2)
                on(s[2], b1_qT)
                on(s[3], b2_pv, 3)
                on(s[1], a2_o_turn)
                on(s[0], a1_kg2)
                on(s[2], b1_scores, 0)
                on(s[3], b2_wo)
                on(s[0], a1_v)
                on(s[2], b1_scores, 1)
                on(s[1], a2_turn)
                on(s[0], a1_qk)
                on(s[1], a2_wo)
                on(s[1], b1_kv)
                on(s[0], a1_g)
                on(s[1], b1_x)
            pipeline(pe, body)

            pe.wait_ge(rep_r, 1)
            for b in range(B):
                ps = psum[b // 8][:, (b % 8) * P:(b % 8 + 1) * P]
                last = nc.tensor.transpose(ps, big[0][:, b * P:(b + 1) * P], ident[:, :])
                if b % 4 == 3:
                    last.then_inc(scT_ps, 1)
            pe.wait_ge(route_const, 8)
            for n in range(len(SHIFTS)):
                pe.wait_ge(cnt_r, n + 1)
                nc.tensor.matmul(psum[2][:, 0:1], same_e[:, :, :].rearrange("p e r -> p (e r)"), enough[:, :],
                                 start=True, stop=True).then_inc(dig_ps, 1)
            pe.wait_ge(pos_r, 1)
            nc.tensor.transpose(psum[3][:, 0:P], thr_w[:, :], ident[:, :]).then_inc(posT_ps, 1)
            pe.wait_ge(pos_r, 3)
            masks = picked[:, :, :, :].rearrange("p m e b -> p (m e b)")
            nc.tensor.matmul(psum[3][:, P:2 * P], tri_in[:, :], masks, start=True, stop=True)
            nc.tensor.matmul(psum[3][:, 2 * P:3 * P], ones_w[:, :], masks, start=True, stop=True).then_inc(posT_ps, 1)

            def token_turn(e, t):
                if not (isinstance(e, int) and e == 0 and t < 2):
                    pe.wait_ge(xgl_r, 4 * e + (t - 1))
                turn(psum[t % 2][:, 0:512], xg32[:, t, :], xgT_ps)

            def up(e, f):
                n = e * (2 * FH) + f
                if not (isinstance(e, int) and e == 0 and f < 2):
                    pe.wait_ge(hg_r, n - 1)
                hf, fc = f // FH, f % FH
                pe.wait_ge(w_lo, W_PIECES * e + (4 * hf + 2))
                for k in range(KC):
                    c = slice(fc * P, (fc + 1) * P)
                    last = mm3(psum[f % 2][:, 512:1024], w1h[hf][:, k, c], w1l[hf][:, k, c], xgh[:, k, :], xgl[:, k, :],
                               k == 0, k == KC - 1)
                last.then_inc(h_ps, 1)

            def down(e, f, final=False):
                n = e * (2 * FH) + f
                hf, fc = f // FH, f % FH
                pe.wait_ge(w_lo, W_PIECES * e + (4 * hf + 4))
                pe.wait_ge(hl_r, n + 1)
                if f == 0 and not (isinstance(e, int) and e == 0):
                    pe.wait_ge(y_ev, 4 * e)
                for t in range(4):
                    tk = slice(t * P, (t + 1) * P)
                    last = mm3(psum[2 + t // 2][:, (t % 2) * 512:(t % 2 + 1) * 512], hh[f % 2][:, tk], hl[f % 2][:, tk],
                               w2h[hf][:, fc, :], w2l[hf][:, fc, :], f == 0, f == 2 * FH - 1)
                    if final and t < 3:
                        last.then_inc(h_used, 1)
                if fc == FH - 1:
                    last.then_inc(half_used[hf], 1)
                else:
                    last.then_inc(h_used, 1)

            def expert(e, more):
                pe.wait_ge(xgl_r, 4 * (e + 1))
                up(e, 0)
                for f in range(2 * FH):
                    if f + 1 < 2 * FH:
                        up(e, f + 1)
                    if more and f >= 2 * FH - 2:
                        if f == 2 * FH - 2:
                            pe.wait_ge(xg_in, 16 * (e + 2))
                        token_turn(e + 1, 2 * (f - 2 * FH + 2))
                        token_turn(e + 1, 2 * (f - 2 * FH + 2) + 1)
                    down(e, f, not more and f == 2 * FH - 1)

            pe.wait_ge(xg_in, 16)
            for t in range(4):
                token_turn(0, t)
            expert(0, True)
            with pe.Fori(1, E - 1) as e:
                expert(e, True)
            expert(E - 1, False)

        @block.vector
        def _(dve):
            dve.memset(carry[:, :], 1.0).then_inc(dve_const, 1)
            dve.wait_ge(dve_const, 1)
            dve.memset(carry[:, L:L + 1], 0.0).then_inc(dve_const, 1)
            dve.wait_ge(pool_const, 6)
            dve.tensor_scalar(half_id[:, :], row_id[:, :], DK, None, ALU.bitwise_and).then_inc(dve_const, 1)
            dve.wait_ge(dve_const, 3)
            dve.tensor_scalar(pair_half[:, 1:2], half_id[:, :], UN / DK, None, ALU.mult).then_inc(dve_const, 1)
            dve.tensor_scalar(pair_half[:, 0:1], half_id[:, :], -UN / DK, UN, ALU.mult, ALU.add).then_inc(dve_const, 1)
            dve.memset(scm[:, :], 0.0).then_inc(dve_const, 1)

            def low(dst, src, scale, hi):
                return dve.scalar_tensor_tensor(dst, src, scale, hi, ALU.mult, ALU.subtract)

            def centre_heads(ap, sums_ap, n):
                dve.tensor_reduce(sums_ap, ap, AX.X, ALU.add).then_inc(cent, 1)
                dve.wait_ge(cent, 2 * n - 1)
                return dve.scalar_tensor_tensor(ap, sums_ap.unsqueeze(len(sums_ap.shape)).to_broadcast(list(sums_ap.shape) + [DV]),
                                                -1.0 / DV, ap, ALU.mult, ALU.add).then_inc(cent, 1)

            def centre_first():
                dve.wait_ge(stage_in[0], 16)
                for i in range(KC):
                    centre_heads(heads(staged(0)[:, i, :]), cent_sums[:, i, :], i + 1)

            def means(n):
                dve.wait_ge(stage_in[n % NSTAGE], 16 * (n // NSTAGE + 1))
                for i in range(pieces[n][3]):
                    last = dve.tensor_reduce(cent_mean(n, i), heads(staged(n)[:, i, 0:D]), AX.X, ALU.add)
                last.then_inc(cent, 1)
                m = KC + POOL_CENTRED.index(n)
                dve.wait_ge(cent, 2 * m + 1)
                dve.tensor_scalar(cent_means(n), cent_means(n), 1.0 / DV, None, ALU.mult).then_inc(cent, 1)

            def split_low(n):
                dve.wait_ge(stage_hi, n + 2)
                for src, hi, lo in split_parts(n):
                    last = low(lo, src, WS, hi)
                last.then_inc(stage_lo, 1)

            def weights_attention():
                dve.wait_ge(stage_hi, 1)
                low(wl[:, :, C_KG:C_KG + DK], KG_STAGE, WS, wh[:, :, C_KG:C_KG + DK]).then_inc(stage_lo, 1)
                dve.wait_ge(dve_const, 6)
                dve.wait_ge(consts_a1_in, 16 * len(consts_a1))

            def second_low():
                dve.wait_ge(dca_split, 1)
                low(dca_l, dca32, XS, dca_h).then_inc(dca_split, 1)
                split_low(4)

            def weights_cross():
                split_low(7)
                dve.wait_ge(consts_b_in, 16 * len(consts_b))
                n = KC + len(POOL_CENTRED)
                centre_heads(heads(bq_sb[:, :]), cent_sums[:, 0, :], n + 1)
                centre_heads(heads(bkv_sb[:, 0:D]), cent_sums[:, 1, :], n + 2)
                dve.wait_ge(cent, 2 * n + 4)
                dve.memset(wait_pad[:, 0:1], 0.0).then_inc(dve_const, 2)

            def cols(ps):
                return ps.rearrange("p (k n) -> p k n", k=KC)

            apart = [0]

            def wait_apart(signal, value):
                dve.wait_ge(signal, value)
                apart[0] = (apart[0] + 1) % PADS
                dve.memset(wait_pad[:, apart[0]:apart[0] + 1], 0.0)

            def row_stats(n, src, b):
                dve.bn_stats(stats[n][:, :], src).then_inc(stat[n], 1)
                wait_apart(stat[n], 3 * b + 1)
                dve.bn_aggr(aggr[n][:, :], stats[n][:, :]).then_inc(stat[n], 1)
                after(dve, stat[n], b, nth=2, per=3)
                dve.tensor_scalar(neg_mean[n][:, :], aggr[n][:, 0:1], -1.0, None, ALU.mult).then_inc(stat[n], 1)

            def head_var(s, n, sq):
                after(dve, hq[n], s[0])
                dve.tensor_reduce(hvar[n][:, :], heads(sq[:, :]), AX.X, ALU.add).then_inc(hv[n], 1)

            def head_norm(s, n, dst, src, done):
                after(dve, hdev[n], s[0], nth=2, per=2)
                dve.scalar_tensor_tensor(heads(dst[:, :]), heads(src), DV ** 0.5, per_head(hrs[n][:, :]), ALU.mult, ALU.mult).then_inc(done, 1)

            def a1_stats(s):
                b, par, half = s
                if isinstance(b, int):
                    for n in x_loaded(b):
                        dve.wait_ge(x_in[n], 16)
                row_stats(0, x_all[:, seq(b)], b)
                if first(b, 0):
                    centre_first()

            def a1_low(s):
                after(dve, xth_r, s[0])
                low(xtl[:, :, :], cols(a0), XS, xth[:, :, :]).then_inc(xtl_r, 1)
                if first(s[0], 0):
                    split_low(0)

            def a1_z(s):
                after(dve, kg2_ps, s[0])
                z3 = z[:, :].rearrange("p (c t) -> p c t", c=2)
                dve.tensor_tensor(z3, a1[:, 0:QK].rearrange("p (c t) -> p c t", c=2),
                                  bkg2_sb[:, :].unsqueeze(2).to_broadcast([P, 2, L]), ALU.add).then_inc(z_r, 1)
                if first(s[0], 0):
                    split_low(1)

            def a1_sums(s):
                b, par, half = s
                after(dve, lsig, b, nth=3, per=3)
                dve.scalar_tensor_tensor(lsg[:, :], z[:, :], 0.0, zl[:, :], ALU.min, ALU.subtract).then_inc(sums, 1)
                after(dve, sums, b, nth=1, per=3)
                dve.tensor_tensor_scan(G[:, :], carry[:, :], lsg[:, :], 0.0, ALU.mult, ALU.add).then_inc(sums, 1)
                after(dve, sums, b, nth=2, per=3)
                G3 = G[:, :].rearrange("p (n t) -> p n t", t=BLK)
                m = BLK // 2 - 1
                dve.tensor_tensor(dq[:, :].rearrange("p (n t) -> p n t", t=BLK), G3,
                                  G3[:, :, m:m + 1].to_broadcast([P, 2 * NBLK, BLK]), ALU.subtract).then_inc(sums, 1)
                if first(b, 0):
                    split_low(2)
                    means(4)

            def a1_decayed(s):
                b, par, half = s
                after(dve, qk_ps, b)
                after(dve, eq_r, b)
                blocks = lambda ap: ap.rearrange("p (n t) -> p n t", t=BLK)
                for e in range(2):
                    dve.scalar_tensor_tensor(qeo[par][:, :, e, :], blocks(a0[:, 0:QK]), pair_half[:, e:e + 1], blocks(eq[:, :]),
                                             ALU.mult, ALU.mult)
                after(dve, dke_r, b)
                k3 = a0[:, QK:2 * QK].rearrange("p (c t) -> p c t", c=2)
                for i in range(NBLK):
                    w = slice(KTO[i], KTO[i] + KTW[i])
                    last = dve.scalar_tensor_tensor(kt[par][:, :, w], k3[:, :, 0:KTW[i]], GLA_SCALE * UN, dk[:, :, w],
                                                    ALU.mult, ALU.mult)
                last.then_inc(qk_r, 1)
                if first(b, 0):
                    split_low(3)

            def a1_gate(s):
                after(dve, g_ps, s[0])
                dve.scalar_tensor_tensor(gf[:, :], a1, UN, bg_sb[:, :], ALU.mult, ALU.add).then_inc(gf_r, 1)
                if first(s[0], 0):
                    means(5)
                    means(6)

            def a1_gate_log(s):
                after(dve, ge_r, s[0], nth=3, per=3)
                dve.scalar_tensor_tensor(ge[:, :], gf[:, :], 0.0, ge[:, :], ALU.min, ALU.subtract).then_inc(gl_r, 1)

            def a2_mask(s, rnd):
                wait_apart(sc_ps, 2 * s[0] + (rnd + 1))
                for i in range(NBLK):
                    w = KTW[i]
                    dst = scm[0:w, rnd * 1024:(rnd + 1) * 1024].rearrange("p (g t) -> p g t", t=L)[:, :, i * BLK:(i + 1) * BLK]
                    dst = dst.rearrange("p (g e) t -> p g e t", e=2)
                    src = psum[1][0:w, :].rearrange("p (g i e t) -> p g i e t", i=NBLK, e=2, t=BLK)[:, :, i]
                    mask = causal[0:w, i:i + 1, :].bitcast(I32).rearrange("p i (e t) -> p i e t", e=2).to_broadcast([w, 4, 2, BLK])
                    last = dve.copy_predicated(dst, mask, src)
                last.then_inc(scm_r, 1)
                if rnd and first(s[0], 0):
                    second_low()

            def a2_norm(s):
                head_norm(s, 0, od, b1, on_r)
                if first(s[0], 0):
                    split_low(6)

            def a2_low(s):
                after(dve, oth_r, s[0])
                low(otl[:, :, :], cols(b0), XS, oth[:, :, :]).then_inc(otl_r, 1)
                if first(s[0], 0):
                    weights_cross()

            def a2_residual(s):
                b, par, half = s
                after(dve, wo_ps, b)
                dve.scalar_tensor_tensor(x_all[:, seq(b)], b1, UN, x_all[:, seq(b)], ALU.mult, ALU.add).then_inc(x1_r, 1)

            def b1_stats(s):
                b, par, half = s
                wait_apart(x1_r, b + 1)
                row_stats(1, x_all[:, seq(b)], b)

            def b1_ctx(s):
                b, par, half = s
                after(dve, cth_r, b)
                low(ctl[:, :, :], ctx32[par][:, :, :], XS, cth[:, :, :]).then_inc(ctl_r, 1)
                if first(b, 0):
                    split_low(5)

            def b1_k_norm(s):
                head_norm(s, 1, kraw, kraw[:, :], kn_r)

            def b1_low(s):
                after(dve, x2h_r, s[0])
                low(x2l[:, :, :], cols(c0), XS, x2h[:, :, :]).then_inc(x2l_r, 1)

            def b1_q(s):
                b, par, half = s
                if isinstance(b, int) and b == 0:
                    dve.wait_ge(dca_stored, 64)
                after(dve, q_ps, b)
                dve.scalar_tensor_tensor(qraw[:, :], c1, UN, bq_sb[:, :], ALU.mult, ALU.add).then_inc(q_r, 1)

            def b1_q_norm(s):
                head_norm(s, 2, qraw, qraw[:, :], qn_r)

            def b1_softmax(s, rnd):
                b, par, half = s
                after(dve, xs_ps, b, nth=rnd + 1, per=2)
                s3 = psum[2][:, :].rearrange("p (h k) -> p h k", k=L)
                p3 = pr[par][:, rnd * 1024:(rnd + 1) * 1024].rearrange("p (h k) -> p h k", k=L)
                hh8 = slice(rnd * 8, rnd * 8 + 8)
                parts = ((0, slice(0, KEYS), KEYS), (1, slice(KEYS, L), NDCA))
                for n, ks, w in parts:
                    last = dve.tensor_reduce(mx[:, n, hh8], s3[:, :, ks], AX.X, ALU.max)
                last.then_inc(shift, 1)
                after(dve, shift, b, nth=2 * rnd + 1, per=4)
                for n, ks, w in parts:
                    last = dve.tensor_tensor(p3[:, :, ks], s3[:, :, ks], mx[:, n, hh8].unsqueeze(2).to_broadcast([P, 8, w]), ALU.subtract)
                last.then_inc(shift, 1)

            def b1_sums(s, rnd):
                b, par, half = s
                p3 = pr[par][:, rnd * 1024:(rnd + 1) * 1024].rearrange("p (h k) -> p h k", k=L)
                hh8 = slice(rnd * 8, rnd * 8 + 8)
                after(dve, exp_r[rnd], b)
                for n, ks in ((0, slice(0, KEYS)), (1, slice(KEYS, L))):
                    last = dve.tensor_reduce(sm[:, n, hh8], p3[:, :, ks], AX.X, ALU.add)
                last.then_inc(norm[rnd], 1)
                after(dve, norm[rnd], b, nth=1, per=2)
                dve.reciprocal(rc[:, :, hh8], sm[:, :, hh8]).then_inc(norm[rnd], 1)

            def b2_low(s):
                after(dve, ch_r, s[0])
                low(cl[:, :, :], cols(d1), XS, ch[:, :, :]).then_inc(cl_r, 1)

            def b2_residual(s):
                b, par, half = s
                after(dve, xo_ps, b)
                after(dve, xbo_r, b)
                dve.scalar_tensor_tensor(x_all[:, seq(b)], d0, UN, x_all[:, seq(b)], ALU.mult, ALU.add).then_inc(x2_r, 1)

            def b2_stats(s):
                b, par, half = s
                wait_apart(x2_r, b + 1)
                row_stats(2, x_all[:, seq(b)], b)

            def b2_logits(s):
                b, par, half = s
                after(dve, xn3_r, b)
                after(dve, cl_r, b)
                for e in range(E):
                    if e:
                        after(dve, lg_r, b, nth=e, per=E)
                    dve.scalar_tensor_tensor(d1, xn3[:, :], 1.0, wgate_sb[:, e, :], ALU.mult, ALU.mult,
                                             accum_out=logit_all[:, bass.ds(b * E + e, 1)]).then_inc(lg_r, 1)

            def body(s):
                on(s[2], b1_low)
                on(s[0], a1_stats)
                on(s[1], a1_gate)
                on(s[2], head_var, 1, ksq)
                on(s[1], a2_mask, 0)
                on(s[2], b1_q)
                on(s[2], head_var, 2, qsq)
                on(s[2], b1_k_norm)
                on(s[1], a2_mask, 1)
                on(s[0], a1_low)
                on(s[1], a1_gate_log)
                on(s[2], b1_q_norm)
                on(s[1], b1_ctx)
                on(s[3], b2_low)
                on(s[1], head_var, 0, od)
                on(s[0], a1_z)
                on(s[2], b1_softmax, 0)
                on(s[3], b2_residual)
                on(s[1], a2_norm)
                on(s[0], a1_sums)
                on(s[3], b2_stats)
                on(s[2], b1_sums, 0)
                on(s[1], a2_low)
                on(s[2], b1_softmax, 1)
                on(s[0], a1_decayed)
                on(s[1], a2_residual)
                on(s[1], b1_stats)
                on(s[2], b1_sums, 1)
                on(s[3], b2_logits)
            pipeline(dve, body, {0: weights_attention})

            step = [0]

            def link(ins):
                step[0] += 1
                ins.then_inc(route, 1)
                dve.wait_ge(route, step[0])

            dve.wait_ge(lg_r, E * B)
            dve.wait_ge(mean3_r, B)
            dve.wait_ge(route_const, 8)
            lg = logit_all[:, :].rearrange("p (b e) -> p b e", e=E)
            link(dve.tensor_tensor(lg, lg, bgate_sb[:, :].unsqueeze(1).to_broadcast([P, B, E]), ALU.add))
            mine = lg.unsqueeze(3).to_broadcast([P, B, E, E])
            other = lg.unsqueeze(2).to_broadcast([P, B, E, E])
            tri_b = tri4[:, :, :].rearrange("p a c -> p (a c)").unsqueeze(1).to_broadcast([P, B, E * E])
            flat = lambda t: t[:, :, :, :].rearrange("p b a c -> p b (a c)")
            dve.tensor_tensor(cmp_gt[:, :, :, :], other, mine, ALU.is_gt)
            link(dve.tensor_tensor(cmp_eq[:, :, :, :], other, mine, ALU.is_equal))
            link(dve.tensor_tensor(flat(cmp_eq), flat(cmp_eq), tri_b, ALU.mult))
            link(dve.tensor_tensor(flat(cmp_gt), flat(cmp_gt), flat(cmp_eq), ALU.add))
            link(dve.tensor_reduce(rank[:, :, :], cmp_gt[:, :, :, :], AX.X, ALU.add))
            dve.tensor_scalar(oh[0][:, :, :], rank[:, :, :], 0.0, None, ALU.is_equal)
            dve.tensor_reduce(l1[:, :], lg, AX.X, ALU.max)
            link(dve.tensor_scalar(oh[1][:, :, :], rank[:, :, :], 1.0, None, ALU.is_equal))
            link(dve.tensor_tensor(ohl[:, :, :], oh[1][:, :, :], lg, ALU.mult))
            link(dve.tensor_reduce(l2[:, :], ohl[:, :, :], AX.X, ALU.add))
            link(dve.tensor_tensor(ldiff[:, :], l2[:, :], l1[:, :], ALU.subtract))
            assert step[0] == ROUTE_DIFF
            dve.wait_ge(route_act, 1)
            link(dve.tensor_scalar(den[:, :], ed[:, :], 1.0, None, ALU.add))
            link(dve.reciprocal(p12[:, 0, :], den[:, :]))
            link(dve.tensor_tensor(p12[:, 1, :], p12[:, 0, :], ed[:, :], ALU.mult))
            pk = lambda k: p12[:, k, :].unsqueeze(2).to_broadcast([P, B, E])
            dve.tensor_tensor(score[:, :, :], oh[0][:, :, :], pk(0), ALU.mult)
            link(dve.tensor_tensor(sc2[:, :, :], oh[1][:, :, :], pk(1), ALU.mult))
            link(dve.tensor_tensor(score[:, :, :], score[:, :, :], sc2[:, :, :], ALU.add))
            rep = score[:, :, :].rearrange("p b e -> p (b e)").unsqueeze(2).to_broadcast([P, B * E, P // E])
            dve.tensor_copy(big[0][:, :].rearrange("p (n r) -> p n r", r=P // E), rep).then_inc(rep_r, 1)
            link(dve.tensor_scalar(digit[:, :], pid[:, :], P // E - 1, None, ALU.bitwise_and))
            for n, s in enumerate(SHIFTS):
                dve.tensor_scalar(cands[:, n:n + 1], digit[:, :], s, None, ALU.logical_shift_left)
            dve.memset(restart[:, :, :, :], 1.0)
            link(dve.memset(thr[:, :], 0))
            link(dve.memset(restart[:, :, :, 0:1], 0.0))
            link(dve.tensor_copy(cand[:, :], cands[:, 0:1]))
            link(dve.tensor_scalar(taken[:, :, :], rank[:, :, :], 2.0, None, ALU.is_lt))
            link(dve.tensor_copy(upto[:, :, 0], taken[:, :, 0]))
            for e in range(1, E):
                link(dve.tensor_tensor(upto[:, :, e], upto[:, :, e - 1], taken[:, :, e], ALU.add))
            for k in range(2):
                link(dve.scalar_tensor_tensor(by_id[k][:, :, :], upto[:, :, :], float(k + 1), taken[:, :, :], ALU.is_equal, ALU.mult))
            dve.wait_ge(route_act, 5)
            for n, s in enumerate(SHIFTS):
                link(dve.tensor_scalar(big[1][:, :], big[0][:, :], cand[:, :].bitcast(F32), 0.0, ALU.is_ge, ALU.add, accum_out=count[:, :]))
                dve.tensor_scalar(enough[:, :], count[:, :], float(CAP), float(2 ** s), ALU.is_ge, ALU.mult).then_inc(cnt_r, 1)
                if n + 1 < len(SHIFTS):
                    link(dve.tensor_tensor(base[:, :], thr[:, :], cands[:, n + 1:n + 2], ALU.bitwise_or))
                dve.wait_ge(dig_ps, n + 1)
                link(dve.tensor_scalar(digit[:, :], psum[2][:, 0:1], -float(2 ** s), None, ALU.add))
                if n + 1 < len(SHIFTS):
                    dve.tensor_tensor(cand[:, :], base[:, :], digit[:, :], ALU.bitwise_or)
                link(dve.tensor_tensor(thr[:, :], thr[:, :], digit[:, :], ALU.bitwise_or))
            dve.tensor_copy(thr_w[:, :], thr[:, :].bitcast(F32).to_broadcast([P, P])).then_inc(pos_r, 1)
            dve.wait_ge(posT_ps, 1)
            thr_t = psum[3][:, 0:P].rearrange("p (e r) -> p e r", e=E)[:, :, 0].unsqueeze(2).to_broadcast([P, E, B])
            by_e = lambda t: t[:, :, :].rearrange("p b e -> p e b")
            per_e = lambda t: t.unsqueeze(2).to_broadcast([P, E, B])
            dve.tensor_tensor(picked[:, 0], by_e(score), thr_t, ALU.is_gt).then_inc(pos_r, 1)
            dve.tensor_tensor(picked[:, 1], by_e(score), thr_t, ALU.is_equal).then_inc(pos_r, 1)
            dve.wait_ge(posT_ps, 2)
            flat4 = lambda t: t[:, :, :, :].rearrange("p m e b -> p (m e b)")
            within, total = psum[3][:, P:2 * P], psum[3][:, 2 * P:3 * P]
            link(dve.tensor_tensor_scan(flat4(running), flat4(restart), total, 0.0, ALU.mult, ALU.add))
            all_gt = running[:, 0, :, B - 1]
            link(dve.tensor_tensor(flat4(place), flat4(running), total, ALU.subtract))
            link(dve.tensor_tensor(flat4(place), flat4(place), within, ALU.add))
            dve.tensor_scalar(ties[:, :], all_gt, -1.0, float(CAP), ALU.mult, ALU.add)
            dve.tensor_tensor(slot1[:, :], slot0[:, :], all_gt, ALU.add)
            link(dve.tensor_tensor(pos_gt[:, :, :], place[:, 0], per_e(slot0[:, :]), ALU.add))
            link(dve.tensor_tensor(take[:, :, :], place[:, 1], per_e(ties[:, :]), ALU.is_le))
            dve.tensor_tensor(take[:, :, :], take[:, :, :], picked[:, 1], ALU.mult)
            link(dve.tensor_tensor(pos_eq[:, :, :], place[:, 1], per_e(slot1[:, :]), ALU.add))
            dve.tensor_tensor(pos_gt[:, :, :], pos_gt[:, :, :], picked[:, 0], ALU.mult)
            link(dve.tensor_tensor(pos_eq[:, :, :], pos_eq[:, :, :], take[:, :, :], ALU.mult))
            link(dve.scalar_tensor_tensor(posT[:, :, :], pos_gt[:, :, :], FAR, pos_eq[:, :, :], ALU.add, ALU.add))
            for k in range(2):
                link(dve.tensor_tensor(sel_k[:, :, :], by_id[k][:, :, :], posT[:, :, :].rearrange("p e b -> p b e"), ALU.mult))
                link(dve.tensor_reduce(idx[:, k, :], sel_k[:, :, :], AX.X, ALU.add))
            link(dve.tensor_copy(idx_put[:, :, :], idx[:, :, :]))
            dve.tensor_scalar(idx_get[:, 0, :], idx[:, 0, :], float(GET_ROWS - 1), None, ALU.min)
            dve.tensor_scalar(idx_get[:, 1, :], idx[:, 1, :], float(GET_ROWS - 1), None, ALU.min).then_inc(idx_r, 1)

            def token_weights():
                for k in range(2):
                    link(dve.tensor_tensor(sel_k[:, :, :], by_id[k][:, :, :], score[:, :, :], ALU.mult))
                    link(dve.tensor_reduce(w_raw[:, k, :], sel_k[:, :, :], AX.X, ALU.add))
                dve.scalar_tensor_tensor(wk[:, :, :], idx[:, :, :], float(GET_ROWS), w_raw[:, :, :], ALU.is_lt, ALU.mult)
                link(dve.tensor_copy(id_w[:, :, 0], ids[:, :]))
                dve.tensor_copy(id_w[:, :, 1], w_raw[:, 1, :]).then_inc(idx_r, 1)

            def low_piece(e, n):
                _, hi, lo, k = w_piece(e, n)
                dve.wait_ge(w_hi, e * W_PIECES + (n + 1))
                low(lo, wst[n % NST][:, :].rearrange("p (k n) -> p k n", k=k), WS, hi).then_inc(w_lo, 1)

            def tokens_low(e):
                for t in range(4):
                    dve.wait_ge(xgh_r, 4 * e + (t + 1))
                    tk = slice(t * P, (t + 1) * P)
                    low(xgl[:, :, tk], cols(psum[t % 2][:, 0:512]), XS, xgh[:, :, tk]).then_inc(xgl_r, 1)

            def split_h(e, f):
                n = e * (2 * FH) + f
                dve.wait_ge(hg_r, n + 1)
                dve.tensor_scalar(hh[f % 2], hg[f % 2], XS, None, ALU.mult).then_inc(hh_r, 1)
                dve.wait_ge(hh_r, n + 1)
                low(hl[f % 2], hg[f % 2], XS, hh[f % 2]).then_inc(hl_r, 1)

            def last_slots():
                dve.wait_ge(slot_in, 16)
                dve.tensor_scalar(slot_w[:, :], slot_id_w[:, :, 1], UN, None, ALU.mult)
                dve.tensor_copy(slot_id[:, :], slot_id_w[:, :, 0]).then_inc(idx_r, 1)

            def last_results():
                dve.wait_ge(y_st, 16 * (E - 1))
                dve.wait_ge(part_in, 16 * (CAP // P))
                dve.wait_ge(idx_r, 3)
                for t in range(CAP // P):
                    if t < 3:
                        dve.wait_ge(h_used, E * (2 * FH - 2) + t + 1)
                    else:
                        dve.wait_ge(half_used[1], E)
                    dve.scalar_tensor_tensor(y_sb[:, t, :], psum[2 + t // 2][:, (t % 2) * 512:(t % 2 + 1) * 512], slot_w[:, t:t + 1],
                                             xg32[:, t, :], ALU.mult, ALU.add).then_inc(y_ev, 1)

            def results(e):
                dve.wait_ge(half_used[1], e + 1)
                if not isinstance(e, int) or e >= 1:
                    dve.wait_ge(y_st, 16 * e)
                for t in range(4):
                    dve.tensor_scalar(y_sb[:, t, :], psum[2 + t // 2][:, (t % 2) * 512:(t % 2 + 1) * 512], UN, None,
                                      ALU.mult).then_inc(y_ev, 1)

            def expert(e, more):
                for f in range(2 * FH):
                    if f >= 2 and f != FH + 1:
                        dve.wait_ge(h_used, e * (2 * FH - 2) + (f - 1 if f <= FH else f - 2))
                    split_h(e, f)
                    if f < FH and f % 2 == 0:
                        low_piece(e, W_PIECES // 2 + f // 2)
                    if more and f >= FH and f % 2 == 0:
                        low_piece(e + 1, (f - FH) // 2)
                    if not more and f == FH - 4:
                        last_slots()
                    if not more and LO_STEP <= f < LO_STEP + NG:
                        for b in range((f - LO_STEP) * (B // NG), (f - LO_STEP + 1) * (B // NG)):
                            combine(0, b, lo_in, 16 * B)
                    if not more and LO_STEP + NG <= f < LO_STEP + 2 * NG:
                        g = f - LO_STEP - NG
                        for b in range(g * (B // NG), (g + 1) * (B // NG)):
                            combine(1, b, hi_in[g], 16 * (B // NG))
                if more:
                    tokens_low(e + 1)
                    results(e)
                else:
                    last_results()
            LO_STEP = 2 * FH - 2 * NG - 3

            def combine(k, b, fetched, count):
                dve.wait_ge(fetched, count)
                if k:
                    dve.wait_ge(comb, b + 1)
                dve.scalar_tensor_tensor(x_all[:, b * D:(b + 1) * D], yg[b], wk[:, k, b:b + 1],
                                         x_all[:, b * D:(b + 1) * D], ALU.mult, ALU.add).then_inc(comb, 1)

            for n in range(W_PIECES // 2):
                low_piece(0, n)
            token_weights()
            tokens_low(0)
            expert(0, True)
            with dve.Fori(1, E - 1) as e:
                expert(e, True)
            expert(E - 1, False)


ROUTE_DIFF = 9


def kernel(**inputs):
    import numpy as np
    import concourse.bacc as bacc
    from concourse import mybir as my
    from concourse.bass_utils import run_bass_kernel_spmd

    g = {k: np.asarray(a) for k, a in inputs.items()}
    cat = np.concatenate
    main = g["ctx_1024"].shape[1] - 16
    kv = cat([g["L0_xattn_Wk"], g["L0_xattn_Wv"]], axis=1).reshape(256, 16, 2, 32)
    kvb = cat([g["L0_xattn_bk"], g["L0_xattn_bv"]]).reshape(16, 2, 32)
    arrays = {
        "x": g["x"],
        "ctx_t": g["ctx_1024"][:, :main].transpose(0, 2, 1),
        "dca_t": g["ctx_1024"][:, main:].reshape(-1, 256).T,
        "w_attn": cat([g["L0_attn_Wq"].T, g["L0_attn_Wk"].T, g["L0_attn_Wkg1"].T, g["L0_attn_Wv"].T, g["L0_attn_Wg"].T,
                       g["L0_attn_Wo"].T, g["L0_xattn_Wq"], g["L0_xattn_Wo"]], axis=1),
        "w_ctx": cat([kv[:, :, 0].reshape(256, 512), kv[:, :, 1].reshape(256, 512), g["L0_xattn_Wkv_dca"]], axis=1),
        "w_kg2": g["L0_attn_Wkg2"].T,
        "b_kg2": g["L0_attn_bkg2"].reshape(2, 128).T,
        "b_g": g["L0_attn_bg"], "b_q": g["L0_xattn_bq"],
        "b_kv": cat([kvb[:, 0].reshape(512), kvb[:, 1].reshape(512)]),
        "b_dca": g["L0_xattn_bkv_dca"],
        "cols_n": np.stack([np.tile(g["L0_xattn_" + n], 4) for n in ("qn_w", "qn_b", "kn_w", "kn_b", "kn_dca_w", "kn_dca_b")], axis=1),
        "b_o": g["L0_xattn_bo"], "w_gate": g["L0_ffn_Wg"].T, "b_gate": g["L0_ffn_bg"],
        "w1": g["L0_ffn_W1"], "w2": g["L0_ffn_W2"],
    }
    nc = bacc.Bacc("TRN2", target_bir_lowering=False, num_devices=1)
    feed, args = {}, []
    for name, a in arrays.items():
        a = np.ascontiguousarray(a)
        feed[f"in_{name}"] = a
        args.append(nc.dram_tensor(f"in_{name}", a.shape, my.dt.from_np(a.dtype), kind="ExternalInput").ap())
    out = nc.dram_tensor("out", g["x"].shape, my.dt.float32, kind="ExternalOutput").ap()
    decoder_layer(nc, None, *args, out)
    r = run_bass_kernel_spmd(nc, [feed], core_ids=[0])
    return r.results[0]["out"]
```
